# Optimizing a Trainium2 kernel written in Bass

```python
import numpy as np
import jax
import jax.numpy as jnp

def _softmax(x, axis=-1):
    return jax.nn.softmax(x, axis=axis)

def _gelu(x):
    return jax.nn.gelu(x, approximate=True)

def _silu(x):
    return jax.nn.silu(x)

def _sigmoid(x):
    return jax.nn.sigmoid(x)

def _layernorm(x, axis=-1, eps=1e-05):
    m = jnp.mean(x, axis=axis, keepdims=True)
    v = jnp.var(x, axis=axis, keepdims=True)
    return (x - m) / jnp.sqrt(v + eps)

def _scatter_add(tgt, idx, src, axis=0):
    return tgt.at[idx].add(src)

def _segment_sum(src, seg, n):
    return jax.ops.segment_sum(src, seg, n)
kernel_name = 'mk_decoder_preln_d1_seqx_r4_f136d1'

def setup_inputs(seed: int=0):
    np.random.seed(seed)
    _w = jnp.asarray

    def _rec_inputs():
        import jax
        import jax.numpy as jnp
        _rk = jax.random.key(seed)
        x = 7.22e-05 + 1 * jax.random.normal(jax.random.fold_in(_rk, 1), (4, 512, 256), jnp.float32)
        _lenS = 512 - jax.random.randint(jax.random.fold_in(_rk, 7), (4,), 0, max(1, 512 // 4) + 1, jnp.int32)
        _lenS2 = 512 - jax.random.randint(jax.random.fold_in(_rk, 8), (4,), 0, max(1, 512 // 4) + 1, jnp.int32)
        _ctx_1024P = jax.random.normal(jax.random.fold_in(_rk, 11), (4, 16, 256), jnp.float32)
        _ctx_1024c = jax.random.dirichlet(jax.random.fold_in(_rk, 511), 0.3 * jnp.ones((16,), jnp.float32), (4, 512))
        _ctx_1024t = jnp.einsum('bsk,bkd->bsd', _ctx_1024c, _ctx_1024P)
        _ctx_1024t = _ctx_1024t * jax.lax.rsqrt(jnp.mean(jnp.square(_ctx_1024t)) + 1e-12) * 0.953939
        ctx_1024 = 4.13588e-05 + 0.999923 * (_ctx_1024t + 0.3 * jax.random.normal(jax.random.fold_in(_rk, 611), (4, 512, 256), jnp.float32))
        return (x, ctx_1024)
    x, ctx_1024 = _rec_inputs()

    def _L0_attn_setup():
        import jax, jax.numpy as jnp
        import numpy as np
        ALPHA_SCALE = 8.0
        EPS = 1e-06

        def _depthwise_causal_conv(x, conv_w, conv_b):
            K = conv_w.shape[-1]
            y = jax.lax.conv_general_dilated(x, conv_w, window_strides=(1,), padding=[(K - 1, 0)], dimension_numbers=('NCH', 'OIH', 'NCH'), feature_group_count=x.shape[1])
            return y + conv_b[None, :, None]

        def _linear_scan(alpha, x):

            def combine(c1, c2):
                a1, b1 = c1
                a2, b2 = c2
                return (a1 * a2, a2 * b1 + b2)
            _, h = jax.lax.associative_scan(combine, (alpha, x), axis=1)
            return h
        key = jax.random.key(seed)
        ks = jax.random.split(key, 8)
        N, T, D = (4, 1024, 256)
        H, K = (384, 4)
        return {'x': jax.random.normal(ks[0], (N, T, D), dtype=jnp.float32), 'W_in': jax.random.normal(ks[1], (2 * H, D), dtype=jnp.float32) * D ** (-0.5), 'conv_w': jax.random.normal(ks[2], (H, 1, K), dtype=jnp.float32) * 0.1, 'conv_b': jax.random.normal(ks[3], (H,), dtype=jnp.float32) * 0.1, 'W_g': jax.random.normal(ks[4], (2 * H, H), dtype=jnp.float32) * H ** (-0.5), 'b_g': jax.random.normal(ks[5], (2 * H,), dtype=jnp.float32) * 0.1, 'forget_base': jax.random.normal(ks[6], (H,), dtype=jnp.float32), 'W_out': jax.random.normal(ks[7], (D, H), dtype=jnp.float32) * H ** (-0.5)}
    _L0_attn_all = _L0_attn_setup()
    _L0_attn_in = {k: v for k, v in _L0_attn_all.items() if k in ('W_in', 'conv_w', 'conv_b', 'W_g', 'b_g', 'forget_base', 'W_out')}
    del _L0_attn_all

    def _L0_xattn_setup():
        import jax, jax.numpy as jnp
        import numpy as np
        B, T, D, H = (4, 512, 256, 1024)
        S = 64
        EPS = 1e-05

        def _layer_norm(x, gamma, beta):
            mu = jnp.mean(x, axis=-1, keepdims=True)
            var = jnp.mean(jnp.square(x - mu), axis=-1, keepdims=True)
            return (x - mu) * jax.lax.rsqrt(var + EPS) * gamma + beta

        def _aft_local(emb, wq, bq, wk, bk, wv, bv, wo, bo, pos_bias):
            q = emb @ wq + bq
            k = emb @ wk + bk
            v = emb @ wv + bv
            idx = jnp.arange(T)
            mask = (jnp.abs(idx[:, None] - idx[None, :]) < S).astype(pos_bias.dtype)
            w = pos_bias * mask
            max_k = jnp.max(k, axis=1, keepdims=True)
            max_w = jnp.max(w, axis=1, keepdims=True)
            ek = jnp.exp(k - max_k)
            ew = jnp.exp(w - max_w)
            num = jnp.einsum('tj,bjd->btd', ew, ek * v)
            den = jnp.einsum('tj,bjd->btd', ew, ek)
            y = jax.nn.sigmoid(q) * num / den
            return y @ wo + bo
        key = jax.random.key(seed)
        ks = jax.random.split(key, 16)
        sd = 0.02
        return {'x': jax.random.normal(ks[0], (B, T, D), jnp.float32), 'pos_encod': jax.random.normal(ks[1], (B, T, D), jnp.float32), 'wq': jax.random.normal(ks[2], (D, D), jnp.float32) * sd, 'bq': jnp.zeros((D,), jnp.float32), 'wk': jax.random.normal(ks[3], (D, D), jnp.float32) * sd, 'bk': jnp.zeros((D,), jnp.float32), 'wv': jax.random.normal(ks[4], (D, D), jnp.float32) * sd, 'bv': jnp.zeros((D,), jnp.float32), 'wo': jax.random.normal(ks[5], (D, D), jnp.float32) * sd, 'bo': jnp.zeros((D,), jnp.float32), 'pos_bias': jax.random.normal(ks[6], (T, T), jnp.float32) * sd, 'gamma': jnp.ones((D,), jnp.float32), 'beta': jnp.zeros((D,), jnp.float32), 'w1': jax.random.normal(ks[7], (D, H), jnp.float32) * sd, 'b1': jnp.zeros((H,), jnp.float32), 'w2': jax.random.normal(ks[8], (H, D), jnp.float32) * sd, 'b2': jnp.zeros((D,), jnp.float32)}
    _L0_xattn_all = _L0_xattn_setup()
    _L0_xattn_in = {k: v for k, v in _L0_xattn_all.items() if k in ('wq', 'bq', 'wk', 'bk', 'wv', 'bv', 'wo', 'bo', 'pos_bias', 'gamma', 'beta', 'w1', 'b1', 'w2', 'b2')}
    del _L0_xattn_all

    def _L0_ffn_setup():
        import jax, jax.numpy as jnp
        import numpy as np
        DIM = 256
        DEPTH = 2
        HEADS = 8
        DIM_HEAD = 64
        WINDOW = 128
        INNER = HEADS * DIM_HEAD
        HID = int(DIM * 4 * 2 / 3)
        B, N = (2, 2048)
        QK_SCALE = 8.0

        def shift_token(t):
            t1, t2 = jnp.split(t, 2, axis=-1)
            t2 = jnp.pad(t2, ((0, 0), (1, 0), (0, 0)))[:, :-1]
            return jnp.concatenate([t1, t2], axis=-1)

        def l2norm(t):
            return t / jnp.clip(jnp.linalg.norm(t, axis=-1, keepdims=True), 1e-12)

        def rotate_half(x):
            x1, x2 = jnp.split(x, 2, axis=-1)
            return jnp.concatenate([-x2, x1], axis=-1)

        def rotary_xpos(q, k):
            n = q.shape[-2]
            half_idx = jnp.arange(0, DIM_HEAD, 2, dtype=jnp.float32)
            inv_freq = 1.0 / 10000.0 ** (half_idx / DIM_HEAD)
            t = jnp.arange(n, dtype=jnp.float32)
            freqs = t[:, None] * inv_freq[None, :]
            freqs = jnp.concatenate([freqs, freqs], axis=-1)
            base = (half_idx + 0.4 * DIM_HEAD) / (1.4 * DIM_HEAD)
            power = (t - n // 2) / float(WINDOW // 2)
            scale = base[None, :] ** power[:, None]
            scale = jnp.concatenate([scale, scale], axis=-1)
            cos, sin = (jnp.cos(freqs), jnp.sin(freqs))
            q = q * cos * scale + rotate_half(q) * sin * scale
            k = k * cos / scale + rotate_half(k) * sin / scale
            return (q, k)

        def local_attention(q, k, v):
            b, h, n, d = q.shape
            w = n // WINDOW
            bq = q.reshape(b, h, w, WINDOW, d) * QK_SCALE
            bk = k.reshape(b, h, w, WINDOW, d)
            bv = v.reshape(b, h, w, WINDOW, d)

            def look_around(t):
                p = jnp.pad(t, ((0, 0), (0, 0), (1, 0), (0, 0), (0, 0)))
                return jnp.concatenate([p[:, :, :w], p[:, :, 1:]], axis=3)
            bk, bv = (look_around(bk), look_around(bv))
            bt = jnp.arange(n).reshape(w, WINDOW)
            btp = jnp.pad(bt, ((1, 0), (0, 0)), constant_values=-1)
            btk = jnp.concatenate([btp[:w], btp[1:]], axis=1)
            sim = jnp.einsum('bhwid,bhwjd->bhwij', bq, bk)
            i = bt[:, :, None]
            j = btk[:, None, :]
            mask = (i < j) | (i > j + WINDOW) | (j == -1)
            sim = jnp.where(mask, -jnp.finfo(sim.dtype).max, sim)
            attn = jax.nn.softmax(sim, axis=-1)
            out = jnp.einsum('bhwij,bhwjd->bhwid', attn, bv)
            return out.reshape(b, h, n, d)

        def _layer(x, wqkv, qs, ksc, wo, lg, lb, w1, b1, w2, b2):
            b, n, _ = x.shape
            h = shift_token(x)
            qkv = h @ wqkv
            q, k, v = jnp.split(qkv, 3, axis=-1)
            to_heads = lambda t: t.reshape(b, n, HEADS, DIM_HEAD).transpose(0, 2, 1, 3)
            q, k, v = (to_heads(q), to_heads(k), to_heads(v))
            q = l2norm(q) * qs
            k = l2norm(k) * ksc
            q, k = rotary_xpos(q, k)
            o = local_attention(q, k, v)
            o = o.transpose(0, 2, 1, 3).reshape(b, n, INNER)
            x = x + o @ wo
            h = shift_token(x)
            mu = h.mean(-1, keepdims=True)
            var = h.var(-1, keepdims=True)
            h = (h - mu) / jnp.sqrt(var + 1e-05) * lg + lb
            h = h @ w1 + b1
            a, g = jnp.split(h, 2, axis=-1)
            h = a * jax.nn.gelu(g, approximate=False)
            x = x + h @ w2 + b2
            return x
        key = jax.random.key(seed)
        ks = jax.random.split(key, 6)
        return {'x': jax.random.normal(ks[0], (B, N, DIM), jnp.float32), 'wqkv': jax.random.normal(ks[1], (DEPTH, DIM, 3 * INNER), jnp.float32) * 0.02, 'q_scale': jnp.ones((DEPTH, DIM_HEAD), jnp.float32), 'k_scale': jnp.ones((DEPTH, DIM_HEAD), jnp.float32), 'wo': jax.random.normal(ks[2], (DEPTH, INNER, DIM), jnp.float32) * 0.02, 'ln_g': jnp.ones((DEPTH, DIM), jnp.float32), 'ln_b': jnp.zeros((DEPTH, DIM), jnp.float32), 'w1': jax.random.normal(ks[3], (DEPTH, DIM, 2 * HID), jnp.float32) * 0.02, 'b1': jnp.zeros((DEPTH, 2 * HID), jnp.float32), 'w2': jax.random.normal(ks[4], (DEPTH, HID, DIM), jnp.float32) * 0.02, 'b2': jnp.zeros((DEPTH, DIM), jnp.float32)}
    _L0_ffn_all = _L0_ffn_setup()
    _L0_ffn_in = {k: v for k, v in _L0_ffn_all.items() if k in ('wqkv', 'q_scale', 'k_scale', 'wo', 'ln_g', 'ln_b', 'w1', 'b1', 'w2', 'b2')}
    del _L0_ffn_all
    return {'x': x, 'ctx_1024': ctx_1024, 'L0_attn_W_in': _L0_attn_in['W_in'], 'L0_attn_conv_w': _L0_attn_in['conv_w'], 'L0_attn_conv_b': _L0_attn_in['conv_b'], 'L0_attn_W_g': _L0_attn_in['W_g'], 'L0_attn_b_g': _L0_attn_in['b_g'], 'L0_attn_forget_base': _L0_attn_in['forget_base'], 'L0_attn_W_out': _L0_attn_in['W_out'], 'L0_xattn_wq': _L0_xattn_in['wq'], 'L0_xattn_bq': _L0_xattn_in['bq'], 'L0_xattn_wk': _L0_xattn_in['wk'], 'L0_xattn_bk': _L0_xattn_in['bk'], 'L0_xattn_wv': _L0_xattn_in['wv'], 'L0_xattn_bv': _L0_xattn_in['bv'], 'L0_xattn_wo': _L0_xattn_in['wo'], 'L0_xattn_bo': _L0_xattn_in['bo'], 'L0_xattn_pos_bias': _L0_xattn_in['pos_bias'], 'L0_xattn_gamma': _L0_xattn_in['gamma'], 'L0_xattn_beta': _L0_xattn_in['beta'], 'L0_xattn_w1': _L0_xattn_in['w1'], 'L0_xattn_b1': _L0_xattn_in['b1'], 'L0_xattn_w2': _L0_xattn_in['w2'], 'L0_xattn_b2': _L0_xattn_in['b2'], 'L0_ffn_wqkv': _L0_ffn_in['wqkv'], 'L0_ffn_q_scale': _L0_ffn_in['q_scale'], 'L0_ffn_k_scale': _L0_ffn_in['k_scale'], 'L0_ffn_wo': _L0_ffn_in['wo'], 'L0_ffn_ln_g': _L0_ffn_in['ln_g'], 'L0_ffn_ln_b': _L0_ffn_in['ln_b'], 'L0_ffn_w1': _L0_ffn_in['w1'], 'L0_ffn_b1': _L0_ffn_in['b1'], 'L0_ffn_w2': _L0_ffn_in['w2'], 'L0_ffn_b2': _L0_ffn_in['b2']}

def reference(x, ctx_1024, L0_attn_W_in, L0_attn_conv_w, L0_attn_conv_b, L0_attn_W_g, L0_attn_b_g, L0_attn_forget_base, L0_attn_W_out, L0_xattn_wq, L0_xattn_bq, L0_xattn_wk, L0_xattn_bk, L0_xattn_wv, L0_xattn_bv, L0_xattn_wo, L0_xattn_bo, L0_xattn_pos_bias, L0_xattn_gamma, L0_xattn_beta, L0_xattn_w1, L0_xattn_b1, L0_xattn_w2, L0_xattn_b2, L0_ffn_wqkv, L0_ffn_q_scale, L0_ffn_k_scale, L0_ffn_wo, L0_ffn_ln_g, L0_ffn_ln_b, L0_ffn_w1, L0_ffn_b1, L0_ffn_w2, L0_ffn_b2):
    import jax
    import jax.numpy as jnp

    def _L0_attn_ref(x, W_in, conv_w, conv_b, W_g, b_g, forget_base, W_out):
        import jax, jax.numpy as jnp
        import numpy as np
        ALPHA_SCALE = 8.0
        EPS = 1e-06

        def _depthwise_causal_conv(x, conv_w, conv_b):
            K = conv_w.shape[-1]
            y = jax.lax.conv_general_dilated(x, conv_w, window_strides=(1,), padding=[(K - 1, 0)], dimension_numbers=('NCH', 'OIH', 'NCH'), feature_group_count=x.shape[1])
            return y + conv_b[None, :, None]

        def _linear_scan(alpha, x):

            def combine(c1, c2):
                a1, b1 = c1
                a2, b2 = c2
                return (a1 * a2, a2 * b1 + b2)
            _, h = jax.lax.associative_scan(combine, (alpha, x), axis=1)
            return h
        H = W_g.shape[1]
        gx = jnp.einsum('ntd,hd->nth', x, W_in)
        gate, xb = (gx[..., :H], gx[..., H:])
        xb = _depthwise_causal_conv(jnp.swapaxes(xb, 1, 2), conv_w, conv_b)
        xb = jnp.swapaxes(xb, 1, 2)
        fg = jnp.einsum('nth,gh->ntg', xb, W_g) + b_g
        forget, inp = (fg[..., :H], fg[..., H:])
        alpha = jnp.exp(-ALPHA_SCALE * jax.nn.softplus(forget_base) * jax.nn.sigmoid(forget))
        beta = jnp.sqrt(1.0 - alpha ** 2 + EPS)
        xs = beta * jax.nn.sigmoid(inp) * xb
        h = _linear_scan(alpha, xs)
        return jnp.einsum('nth,dh->ntd', jax.nn.gelu(gate, approximate=False) * h, W_out)

    def _L0_xattn_ref(x, pos_encod, wq, bq, wk, bk, wv, bv, wo, bo, pos_bias, gamma, beta, w1, b1, w2, b2):
        import jax, jax.numpy as jnp
        import numpy as np
        B, T, D, H = (4, 512, 256, 1024)
        S = 64
        EPS = 1e-05

        def _layer_norm(x, gamma, beta):
            mu = jnp.mean(x, axis=-1, keepdims=True)
            var = jnp.mean(jnp.square(x - mu), axis=-1, keepdims=True)
            return (x - mu) * jax.lax.rsqrt(var + EPS) * gamma + beta

        def _aft_local(emb, wq, bq, wk, bk, wv, bv, wo, bo, pos_bias):
            q = emb @ wq + bq
            k = emb @ wk + bk
            v = emb @ wv + bv
            idx = jnp.arange(T)
            mask = (jnp.abs(idx[:, None] - idx[None, :]) < S).astype(pos_bias.dtype)
            w = pos_bias * mask
            max_k = jnp.max(k, axis=1, keepdims=True)
            max_w = jnp.max(w, axis=1, keepdims=True)
            ek = jnp.exp(k - max_k)
            ew = jnp.exp(w - max_w)
            num = jnp.einsum('tj,bjd->btd', ew, ek * v)
            den = jnp.einsum('tj,bjd->btd', ew, ek)
            y = jax.nn.sigmoid(q) * num / den
            return y @ wo + bo
        emb = x + pos_encod
        attn = _aft_local(emb, wq, bq, wk, bk, wv, bv, wo, bo, pos_bias)
        a = _layer_norm(attn + emb, gamma, beta)
        ff = jax.nn.relu(a @ w1 + b1) @ w2 + b2
        return _layer_norm(ff + a, gamma, beta)

    def _L0_ffn_ref(x, wqkv, q_scale, k_scale, wo, ln_g, ln_b, w1, b1, w2, b2):
        import jax, jax.numpy as jnp
        import numpy as np
        DIM = 256
        DEPTH = 2
        HEADS = 8
        DIM_HEAD = 64
        WINDOW = 128
        INNER = HEADS * DIM_HEAD
        HID = int(DIM * 4 * 2 / 3)
        B, N = (2, 2048)
        QK_SCALE = 8.0

        def shift_token(t):
            t1, t2 = jnp.split(t, 2, axis=-1)
            t2 = jnp.pad(t2, ((0, 0), (1, 0), (0, 0)))[:, :-1]
            return jnp.concatenate([t1, t2], axis=-1)

        def l2norm(t):
            return t / jnp.clip(jnp.linalg.norm(t, axis=-1, keepdims=True), 1e-12)

        def rotate_half(x):
            x1, x2 = jnp.split(x, 2, axis=-1)
            return jnp.concatenate([-x2, x1], axis=-1)

        def rotary_xpos(q, k):
            n = q.shape[-2]
            half_idx = jnp.arange(0, DIM_HEAD, 2, dtype=jnp.float32)
            inv_freq = 1.0 / 10000.0 ** (half_idx / DIM_HEAD)
            t = jnp.arange(n, dtype=jnp.float32)
            freqs = t[:, None] * inv_freq[None, :]
            freqs = jnp.concatenate([freqs, freqs], axis=-1)
            base = (half_idx + 0.4 * DIM_HEAD) / (1.4 * DIM_HEAD)
            power = (t - n // 2) / float(WINDOW // 2)
            scale = base[None, :] ** power[:, None]
            scale = jnp.concatenate([scale, scale], axis=-1)
            cos, sin = (jnp.cos(freqs), jnp.sin(freqs))
            q = q * cos * scale + rotate_half(q) * sin * scale
            k = k * cos / scale + rotate_half(k) * sin / scale
            return (q, k)

        def local_attention(q, k, v):
            b, h, n, d = q.shape
            w = n // WINDOW
            bq = q.reshape(b, h, w, WINDOW, d) * QK_SCALE
            bk = k.reshape(b, h, w, WINDOW, d)
            bv = v.reshape(b, h, w, WINDOW, d)

            def look_around(t):
                p = jnp.pad(t, ((0, 0), (0, 0), (1, 0), (0, 0), (0, 0)))
                return jnp.concatenate([p[:, :, :w], p[:, :, 1:]], axis=3)
            bk, bv = (look_around(bk), look_around(bv))
            bt = jnp.arange(n).reshape(w, WINDOW)
            btp = jnp.pad(bt, ((1, 0), (0, 0)), constant_values=-1)
            btk = jnp.concatenate([btp[:w], btp[1:]], axis=1)
            sim = jnp.einsum('bhwid,bhwjd->bhwij', bq, bk)
            i = bt[:, :, None]
            j = btk[:, None, :]
            mask = (i < j) | (i > j + WINDOW) | (j == -1)
            sim = jnp.where(mask, -jnp.finfo(sim.dtype).max, sim)
            attn = jax.nn.softmax(sim, axis=-1)
            out = jnp.einsum('bhwij,bhwjd->bhwid', attn, bv)
            return out.reshape(b, h, n, d)

        def _layer(x, wqkv, qs, ksc, wo, lg, lb, w1, b1, w2, b2):
            b, n, _ = x.shape
            h = shift_token(x)
            qkv = h @ wqkv
            q, k, v = jnp.split(qkv, 3, axis=-1)
            to_heads = lambda t: t.reshape(b, n, HEADS, DIM_HEAD).transpose(0, 2, 1, 3)
            q, k, v = (to_heads(q), to_heads(k), to_heads(v))
            q = l2norm(q) * qs
            k = l2norm(k) * ksc
            q, k = rotary_xpos(q, k)
            o = local_attention(q, k, v)
            o = o.transpose(0, 2, 1, 3).reshape(b, n, INNER)
            x = x + o @ wo
            h = shift_token(x)
            mu = h.mean(-1, keepdims=True)
            var = h.var(-1, keepdims=True)
            h = (h - mu) / jnp.sqrt(var + 1e-05) * lg + lb
            h = h @ w1 + b1
            a, g = jnp.split(h, 2, axis=-1)
            h = a * jax.nn.gelu(g, approximate=False)
            x = x + h @ w2 + b2
            return x
        for l in range(DEPTH):
            x = _layer(x, wqkv[l], q_scale[l], k_scale[l], wo[l], ln_g[l], ln_b[l], w1[l], b1[l], w2[l], b2[l])
        return x
    x = x + _L0_attn_ref(_layernorm(x, axis=-1), L0_attn_W_in, L0_attn_conv_w, L0_attn_conv_b, L0_attn_W_g, L0_attn_b_g, L0_attn_forget_base, L0_attn_W_out)
    x = x + _L0_xattn_ref(_layernorm(x, axis=-1), ctx_1024, L0_xattn_wq, L0_xattn_bq, L0_xattn_wk, L0_xattn_bk, L0_xattn_wv, L0_xattn_bv, L0_xattn_wo, L0_xattn_bo, L0_xattn_pos_bias, L0_xattn_gamma, L0_xattn_beta, L0_xattn_w1, L0_xattn_b1, L0_xattn_w2, L0_xattn_b2)
    x = x + _L0_ffn_ref(_layernorm(x, axis=-1), L0_ffn_wqkv, L0_ffn_q_scale, L0_ffn_k_scale, L0_ffn_wo, L0_ffn_ln_g, L0_ffn_ln_b, L0_ffn_w1, L0_ffn_b1, L0_ffn_w2, L0_ffn_b2)
    return x

_drawn_inputs = setup_inputs


def setup_inputs(seed=0):
    import zlib

    import numpy as np

    out = dict(_drawn_inputs(seed))
    spreads = {'L0_xattn_bq': (0.0, 0.8),
     'L0_xattn_bk': (0.0, 2.0),
     'L0_xattn_bv': (0.0, 0.8),
     'L0_xattn_bo': (0.0, 0.1),
     'L0_xattn_gamma': (1.0, 0.2),
     'L0_xattn_beta': (0.0, 0.1),
     'L0_xattn_b1': (0.0, 0.39),
     'L0_xattn_b2': (0.0, 0.1),
     'L0_ffn_q_scale': (1.0, 0.6),
     'L0_ffn_k_scale': (1.0, 0.6),
     'L0_ffn_ln_g': (1.0, 0.6),
     'L0_ffn_ln_b': (0.0, 0.8),
     'L0_ffn_b1': (0.0, 0.8),
     'L0_ffn_b2': (0.0, 0.285)}
    factors = {'L0_attn_W_g': 5.961,
     'L0_attn_b_g': 8.0,
     'L0_attn_forget_base': 3.059,
     'L0_xattn_wq': 8.0,
     'L0_xattn_wk': 8.0,
     'L0_xattn_wv': 5.366,
     'L0_xattn_wo': 4.456,
     'L0_xattn_pos_bias': 29.878,
     'L0_ffn_wqkv': 2.794,
     'L0_ffn_wo': 2.769,
     'L0_ffn_w1': 3.365,
     'L0_ffn_w2': 3.356}
    for name, (base, spread) in spreads.items():
        noise = np.random.default_rng([zlib.crc32(name.encode()), seed]).standard_normal(out[name].shape)
        drawn = base * np.exp(spread * noise) if base else spread * noise
        out[name] = jnp.asarray(drawn.astype(out[name].dtype))
    for name, factor in factors.items():
        out[name] = (out[name] * factor).astype(out[name].dtype)
    return out
```

```python
from contextlib import ExitStack

import concourse.bass as bass
from concourse import mybir

F32 = mybir.dt.float32
ALU = mybir.AluOpType
ACT = mybir.ActivationFunctionType
AX_X = mybir.AxisListType.X

P = 128
NB, T, D = 4, 512, 256
TT = T // P
NT = NB * TT
KD = D // P
RH = 384
KR = RH // P
TAPS = 4
FH = 1024
KF = FH // P
LAYERS, HEADS, DH = 2, 8, 64
INNER = HEADS * DH
KI = INNER // P
HID = 682
KH = 6
HLAST = HID - (KH - 1) * P
BAND = 64
QK_SCALE = 8.0
LN_EPS = 1e-5
BETA_EPS = 1e-6
NEG = -1e30

C_CONVW, C_CONVB, C_BG, C_FB = 0, 12, 15, 21
C_BQ, C_BK, C_BV, C_B1 = 24, 26, 28, 30
NCOL = 38
L_G, L_B, L_B1A, L_B1G = 0, 2, 4, 10
NLCOL = 16
R_BO, R_GAMMA, R_BETA, R_B2 = range(4)
TQC, TQS, TKC, TKS = range(4)


def build(nc, stages, x, ctx_in, cols_in, rows_in, w_in, w_gate, w_out, wq, wk, wv, wo_x, pos_bias,
          w1_x, w2_x, lcols_in, qk_scale, rope, wqkv, wo_l, w1_l, w2_l, out):
    with ExitStack() as ctx:
        def sb(name, shape, dt=F32, stack=ctx):
            return stack.enter_context(nc.sbuf_tensor(name, shape, dt))

        def signals(names):
            return [ctx.enter_context(nc.semaphore(n)) for n in names.split()]

        bank = [ctx.enter_context(nc.psum_tensor(f"bank{i}", [P, 512], F32)) for i in range(8)]

        stream = sb("stream", [P, NT, D])
        cols = sb("cols", [P, NCOL])
        ident = sb("ident", [P, P])
        minus_half = sb("minus_half", [P, 2 * HEADS])
        mask = sb("mask", [P, 2 * P])
        rows = sb("rows", [P, 4, D])
        stats = sb("stats", [P, TT, 12])
        mean_var = sb("mean_var", [P, TT, 2])
        var_eps = sb("var_eps", [P, TT])
        rstd = sb("rstd", [P, TT])
        normed = sb("normed", [P, TT, D])
        normed_t = sb("normed_t", [P, KD, T])
        lcols_all = sb("lcols_all", [P, LAYERS, NLCOL])
        lcols = sb("lcols", [P, NLCOL])
        inner = sb("inner", [P, NT, D])
        wqkv_sb = sb("wqkv_sb", [P, KD, 3 * INNER])
        wo_sb = sb("wo_sb", [P, KI, D])
        qk_scale_sb = sb("qk_scale_sb", [P, LAYERS, 2, DH])
        rope_sb = sb("rope_sb", [P, 4, TT, DH])
        st12 = ExitStack()
        w_q = sb("w_q", [P, KD, D], stack=st12)
        w_k = sb("w_k", [P, KD, D], stack=st12)
        w_v = sb("w_v", [P, KD, D], stack=st12)
        w_o = sb("w_o", [P, KD, D], stack=st12)
        w_1 = sb("w_1", [P, KD, FH], stack=st12)
        w_2 = sb("w_2", [P, KF, D], stack=st12)
        emb = sb("emb", [P, NT, D], stack=st12)
        ew = sb("ew", [P, TT, T], stack=st12)
        ew_t = sb("ew_t", [P, TT, T], stack=st12)
        ew_stat = sb("ew_stat", [P, TT, 2], stack=st12)
        ek = sb("ek", [P, KD, T], stack=st12)
        ekv = sb("ekv", [P, KD, T], stack=st12)
        eq = sb("eq", [P, KD, T], stack=st12)
        minus_bq = sb("minus_bq", [P, KD], stack=st12)
        kstat = sb("kstat", [P, KD, 3], stack=st12)
        st1 = ExitStack()
        w_in_sb = sb("w_in_sb", [P, KD, 2 * RH], stack=st1)
        w_gate_sb = sb("w_gate_sb", [P, KR, 2 * RH], stack=st1)
        w_out_sb = sb("w_out_sb", [P, KR, D], stack=st1)
        raw = sb("raw", [P, KR, TAPS - 1 + T], stack=st1)
        conv = sb("conv", [P, KR, T], stack=st1)
        gate_act = sb("gate_act", [P, 2, KR, T], stack=st1)
        th_in = sb("th_in", [P, KR, T], stack=st1)
        alpha = sb("alpha", [P, KR, T], stack=st1)
        beta = sb("beta", [P, KR, T], stack=st1)
        scanned = beta
        fb_tmp = sb("fb_tmp", [P, 3, KR], stack=st1)
        m4sp = sb("m4sp", [P, KR], stack=st1)
        half_bf = sb("half_bf", [P, 2 * KR], stack=st1)
        quarter = sb("quarter", [P, 1], stack=st1)
        st1.close()
        st2 = ExitStack()
        ek_tok = sb("ek_tok", [P, TT, D], stack=st2)
        ekv_tok = sb("ekv_tok", [P, TT, D], stack=st2)
        y = sb("y", [P, KD, T], stack=st2)
        mix = sb("mix", [P, TT, D], stack=st2)
        a_tok = sb("a_tok", [P, TT, D], stack=st2)
        a_t = sb("a_t", [P, KD, T], stack=st2)
        a_b2 = sb("a_b2", [P, TT, D], stack=st2)
        ff = sb("ff", [P, KF, T], stack=st2)
        mixed_out = sb("mixed_out", [P, TT, D], stack=st2)
        lstats = sb("lstats", [P, 2, TT, 6], stack=st2)
        lmv = sb("lmv", [P, 2, TT, 2], stack=st2)
        lveps = sb("lveps", [P, 2, TT], stack=st2)
        lrstd = sb("lrstd", [P, 2, TT], stack=st2)

        st2.close()
        st12.close()
        w1_sb = sb("w1_sb", [P, KD, 2 * HID])
        w2_sb = sb("w2_sb", [P, KH, D])
        x_tile = sb("x_tile", [P, 2, D])
        x_t = sb("x_t", [P, KD, T + 1])
        rope_l = sb("rope_l", [P, 4, TT, DH])
        squares = sb("squares", [P, 2, INNER])
        norms = sb("norms", [P, 3, 2 * HEADS])
        q_rnorm = sb("q_rnorm", [P, 4, HEADS])
        rot = sb("rot", [P, 4, INNER])
        q_tok = sb("q_tok", [P, 2, INNER])
        k_tok = sb("k_tok", [P, 2, INNER])
        q_heads = sb("q_heads", [P, HEADS, P])
        k_t = sb("k_t", [P, KI, T])
        v_tok = sb("v_tok", [P, TT, INNER])
        scores = sb("scores", [P, 2, 2, 2 * P])
        probs = sb("probs", [P, 2, 2, 2 * P])
        probs_t = sb("probs_t", [P, 2, 4, P])
        row_max = sb("row_max", [P, 2, HEADS])
        row_bias = sb("row_bias", [P, 2, HEADS])
        row_sum = sb("row_sum", [P, 2, HEADS])
        row_rsum = sb("row_rsum", [P, HEADS])
        o_tok = sb("o_tok", [P, INNER])
        o_t = sb("o_t", [P, KI, P])
        shifted = sb("shifted", [P, TT, P])
        gelu = sb("gelu", [P, 2, T])
        hidden = sb("hidden", [P, KH, T])

        (x0_in, xr_in, col_in, w1s_in, wg_in, wor_in, aft_in, ctx_sem, pos_in, mlp_in, rows_sem) = signals(
            "x0_in xr_in col_in w1s_in wg_in wor_in aft_in ctx_sem pos_in mlp_in rows_sem")
        (pool_ready, fb_step, fb_vec, ready_consts) = signals("pool_ready fb_step fb_vec ready_consts")
        (n_stats, n_aggr, n_eps, n_rstd, n_norm) = signals("n_stats n_aggr n_eps n_rstd n_norm")
        (a_tp, a_tp_out, a_full, a_thf, a_th, a_gelu, a_exp, a_sq, a_beta, a_raw, a_tap0, a_tap, a_conv,
         a_xs0, a_xs, a_scan, a_gh, a_o, a_res) = signals(
            "a_tp a_tp_out a_full a_thf a_th a_gelu a_exp a_sq a_beta a_raw a_tap0 a_tap a_conv "
            "a_xs0 a_xs a_scan a_gh a_o a_res")
        (e_band, e_max, e_neg, e_exp, e_tp, e_tp_out) = signals("e_band e_max e_neg e_exp e_tp e_tp_out")
        (b_emb, b_embo, b_tp, b_tp_out, b_full, b_kmax, b_kbias, b_ek, b_ekv, b_eq, b_tk, b_tk_out, b_aft, b_den,
         b_rec, b_y, b_o, b_mix, b_ta, b_ta_out, b_relu, b_f1, b_ab2, b_f2, b_sum, b_res) = signals(
            "b_emb b_embo b_tp b_tp_out b_full b_kmax b_kbias b_ek b_ekv b_eq b_tk b_tk_out b_aft b_den b_rec "
            "b_y b_o b_mix b_ta b_ta_out b_relu b_f1 b_ab2 b_f2 b_sum b_res")
        (l_stats, l_aggr, l_eps, l_rstd, l_mid, l_out) = signals("l_stats l_aggr l_eps l_rstd l_mid l_out")
        (n_inner, b_x2, out_sum) = signals("n_inner b_x2 out_sum")
        (c_zero, c_tab, c_lcols, c_xs, c_xt, c_xt_out, c_p, c_sq, c_v, c_ss, c_clip, c_rn, c_rq, c_rope, c_add,
         c_kn, c_t, c_kt, c_qe, c_qo, c_qk, c_tt, c_nb, c_ex, c_pt, c_pt_out, c_pv, c_ri, c_on, c_ot, c_ot_out,
         c_wo, c_res) = signals(
            "c_zero c_tab c_lcols c_xs c_xt c_xt_out c_p c_sq c_v c_ss c_clip c_rn c_rq c_rope c_add c_kn c_t "
            "c_kt c_qe c_qo c_qk c_tt c_nb c_ex c_pt c_pt_out c_pv c_ri c_on c_ot c_ot_out c_wo c_res")
        (d_shift, d_stats, d_aggr, d_eps, d_rstd, d_norm, d_tp, d_tp_out, d_w1, d_gelu, d_act, d_w2, d_res0) = signals(
            "d_shift d_stats d_aggr d_eps d_rstd d_norm d_tp d_tp_out d_w1 d_gelu d_act d_w2 d_res0")
        (rope_in, watt_in, wmlp_in) = signals("rope_in watt_in wmlp_in")
        (out_sem,) = signals("out_sem")

        tiles = lambda b: bass.ts(b, TT) if not isinstance(b, int) else slice(b * TT, (b + 1) * TT)
        block = ctx.enter_context(nc.Block())
        xv = x.rearrange("b (t p) d -> p (b t) d", p=P)
        ov = out.rearrange("b (t p) d -> p (b t) d", p=P)
        cv = ctx_in.rearrange("b (t p) d -> p (b t) d", p=P)

        def wait_alone(engine, sem, value):
            engine.wait_ge(sem, value)
            if not isinstance(value, int):
                engine.nop(nofuse=True)

        @block.sync
        def _(sp):
            sp.dma_start(stream[:, 0:TT, :], xv[:, 0:TT, :]).then_inc(x0_in, 16)
            sp.dma_start(cols[:, :], cols_in).then_inc(col_in, 16)
            sp.dma_start(w_in_sb[:, :, :], w_in).then_inc(w1s_in, 16)
            sp.dma_start(w_gate_sb[:, :, :], w_gate).then_inc(wg_in, 16)
            sp.dma_start(stream[:, TT:NT, :], xv[:, TT:NT, :]).then_inc(xr_in, 16)
            sp.dma_start(w_out_sb[:, :, :], w_out).then_inc(wor_in, 16)
            sp.dma_start(ew[:, :, :], pos_bias).then_inc(pos_in, 16)
            sp.dma_start(emb[:, :, :], cv).then_inc(ctx_sem, 16)
            for n, (w, src) in enumerate(((w_k, wk), (w_v, wv), (w_q, wq), (w_o, wo_x))):
                sp.dma_start(w[:, :, :], src).then_inc(aft_in, 16)
            sp.dma_start(rows[:, :, :], rows_in).then_inc(rows_sem, 16)
            sp.dma_start(w_1[:, :, :], w1_x).then_inc(mlp_in, 16)
            sp.dma_start(w_2[:, :, :], w2_x).then_inc(mlp_in, 16)
            sp.dma_start(rope_sb[:, :, :, :], rope).then_inc(rope_in, 16)
            sp.dma_start(qk_scale_sb[:, :, :, :], qk_scale).then_inc(rope_in, 16)
            sp.dma_start(lcols_all[:, :, :], lcols_in).then_inc(rope_in, 16)

            def load_att(l):
                sp.dma_start(wqkv_sb[:, :, :], wqkv[l]).then_inc(watt_in, 16)
                sp.dma_start(wo_sb[:, :, :], wo_l[l]).then_inc(watt_in, 16)

            def load_mlp(l):
                sp.dma_start(w1_sb[:, :, :], w1_l[l]).then_inc(wmlp_in, 16)
                sp.dma_start(w2_sb[:, :, :], w2_l[l]).then_inc(wmlp_in, 16)

            def shift(l, b):
                m = l * NB + b
                sp.wait_ge(c_res, l * NT + b * TT + TT)
                sp.wait_ge(d_norm, 8 * m)
                sp.dma_start(shifted[1:P, :, :], inner[0:P - 1, b * TT:(b + 1) * TT, P:D]).then_inc(d_shift, 16)
                sp.dma_start(shifted[0:1, 1:TT, :], inner[P - 1:P, b * TT:(b + 1) * TT - 1, P:D]).then_inc(d_shift, 16)

            load_att(0)
            sp.wait_ge(b_res, NB)
            load_mlp(0)
            sp.wait_ge(c_zero, 4)
            for l in range(LAYERS):
                for b in range(NB):
                    shift(l, b)
                    if l == 0 and b == 0:
                        sp.wait_ge(c_p, 3 * NT)
                        sp.wait_ge(c_wo, NT)
                        load_att(1)
                if l == 0:
                    sp.wait_ge(d_w2, TT * NB)
                    load_mlp(1)
            for b in range(NB):
                sp.wait_ge(out_sum, b + 1)
                sp.dma_start(ov[:, b * TT:(b + 1) * TT, :], stream[:, b * TT:(b + 1) * TT, :]).then_inc(out_sem, 16)
            sp.wait_ge(out_sem, 16 * NB)

        @block.gpsimd
        def _(pool):
            pool.memset(ident[:, :], 0.0).then_inc(pool_ready, 1)
            pool.memset(minus_half[:, :], -0.5).then_inc(pool_ready, 1)
            pool.memset(raw[:, :, 0:TAPS - 1], 0.0).then_inc(pool_ready, 1)
            pool.memset(mask[:, :], 0.0).then_inc(pool_ready, 1)
            pool.memset(quarter[:, :], 0.25 * (1.0 + BETA_EPS)).then_inc(pool_ready, 1)
            pool.wait_ge(pool_ready, 5)
            pool.affine_select(out=ident[:, :], in_=ident[:, :], compare_op=ALU.not_equal, fill=1.0, base=0,
                               pattern=[[-1, P]], channel_multiplier=1).then_inc(ready_consts, 1)
            pool.affine_select(out=mask[:, :], in_=mask[:, :], compare_op=ALU.is_ge, fill=NEG, base=P,
                               pattern=[[-1, 2 * P]], channel_multiplier=1).then_inc(pool_ready, 1)
            pool.wait_ge(pool_ready, 6)
            pool.affine_select(out=mask[:, :], in_=mask[:, :], compare_op=ALU.is_ge, fill=NEG, base=0,
                               pattern=[[1, 2 * P]], channel_multiplier=-1).then_inc(ready_consts, 1)

            def rstd_of(n):
                wait_alone(pool, n_aggr, 4 * n + 4)
                pool.tensor_scalar(var_eps[:, :], mean_var[:, :, 1], 1.0, LN_EPS, ALU.mult, ALU.add)\
                    .then_inc(n_eps, 1)
                pool.wait_ge(n_eps, n + 1)
                pool.tensor_tensor(rstd[:, :], var_eps[:, :], minus_half[:, 0:TT], ALU.pow).then_inc(n_rstd, 1)

            rstd_of(0)
            pool.wait_ge(pos_in, 16)
            for n, (step, ch) in enumerate(((P, 1), (-P, -1))):
                pool.wait_ge(e_band, n)
                pool.affine_select(out=ew[:, :, :], in_=ew[:, :, :], compare_op=ALU.is_ge, fill=0.0,
                                   base=BAND - 1, pattern=[[step, TT], [-ch, T]], channel_multiplier=ch)\
                    .then_inc(e_band, 1)
            with pool.Fori(0, NB - 1) as b:
                rstd_of(b + 1)

            def keep_emb(b):
                pool.wait_ge(b_emb, b + 1)
                pool.tensor_tensor(emb[:, tiles(b), :], normed[:, :, :],
                                   rows[:, R_BO:R_BO + 1, :].to_broadcast([P, TT, D]), ALU.add)\
                    .then_inc(b_embo, 1)

            def rstd_affine(i, s):
                wait_alone(pool, l_aggr, 4 * i + 4)
                pool.tensor_scalar(lveps[:, s, :], lmv[:, s, :, 1], 1.0, LN_EPS, ALU.mult, ALU.add)\
                    .then_inc(l_eps, 1)
                pool.wait_ge(l_eps, i + 1)
                pool.tensor_tensor(lrstd[:, s, :], lveps[:, s, :], minus_half[:, 0:TT], ALU.pow).then_inc(l_rstd, 1)

            def add_b2(b):
                pool.wait_ge(l_out, 8 * b + 4)
                pool.wait_ge(l_mid, 8 * b)
                pool.tensor_tensor(a_b2[:, :, :], a_tok[:, :, :],
                                   rows[:, R_B2:R_B2 + 1, :].to_broadcast([P, TT, D]), ALU.add).then_inc(b_ab2, 1)

            def add_out(b):
                pool.wait_ge(l_out, 8 * b + 8)
                pool.tensor_tensor(stream[:, tiles(b), :], stream[:, tiles(b), :], mixed_out[:, :, :], ALU.add)\
                    .then_inc(b_x2, 1)

            pool.wait_ge(rows_sem, 16)
            rstd_of(NB)
            keep_emb(0)
            rstd_of(NB + 1)
            keep_emb(1)
            rstd_affine(0, 0)
            add_b2(0)

            def finish(b, nxt, norm2):
                if norm2:
                    rstd_of(2 * b + NB + 2)
                    keep_emb(b + 2)
                rstd_affine(2 * b + 1, 1)
                if nxt:
                    rstd_affine(2 * b + 2, 0)
                add_out(b)
                if nxt:
                    add_b2(b + 1)
                rstd_of(2 * b + NB + 3 if norm2 else b + 2 * NB)

            with pool.Fori(0, NB - 2) as b:
                finish(b, True, True)
            finish(NB - 2, True, False)
            finish(NB - 1, False, False)

            pool.wait_ge(b_res, NB)
            pool.memset(x_t[:, 1, 0:1], 0.0).then_inc(c_zero, 1)
            pool.memset(q_heads[:, :, :], 0.0).then_inc(c_zero, 1)
            pool.wait_ge(c_zero, 2)
            pool.memset(hidden[32:64, KH - 1, :], 1.0).then_inc(c_zero, 1)
            pool.wait_ge(c_zero, 3)
            pool.memset(shifted[0:1, 0, :], 0.0).then_inc(c_zero, 1)
            pool.wait_ge(c_zero, 4)

            def copy_tile(n, tile, par, batch_done):
                pool.wait_ge(b_res, batch_done)
                wait_alone(pool, c_xt, n - 1) if not (isinstance(n, int) and n == 0) else None
                pool.tensor_copy(x_tile[:, par, :], inner[:, tile, :]).then_inc(c_xs, 1)

            def rotate(n, par):
                for i, dst in enumerate((q_tok, k_tok)):
                    pool.wait_ge(c_rope, 6 * n + 3 * i + 3)
                    pool.wait_ge(c_t, 2 * n - 2) if not (isinstance(n, int) and n == 0) else None
                    pool.tensor_tensor(dst[:, par, :], rot[:, 2 * i, :], rot[:, 2 * i + 1, :], ALU.add)\
                        .then_inc(c_add, 1)

            def rnorm(n, w):
                pool.wait_ge(c_ss, n + 1)
                wait_alone(pool, c_kn, n)
                pool.tensor_scalar(norms[:, 1, :], norms[:, 0, :], 1e-24, 1.0, ALU.max, ALU.mult).then_inc(c_clip, 1)
                pool.wait_ge(c_clip, n + 1)
                pool.tensor_tensor(norms[:, 2, :], norms[:, 1, :], minus_half[:, :], ALU.pow).then_inc(c_rn, 1)
                wait_alone(pool, c_rn, n + 1)
                pool.tensor_scalar(q_rnorm[:, w, :], norms[:, 2, 0:HEADS], QK_SCALE, 0.0, ALU.mult, ALU.add)\
                    .then_inc(c_rq, 1)

            def attention(n0, b, l, nxt):
                for w in range(TT):
                    if w == 0 or nxt:
                        v = (w + 3) % TT
                        copy_tile(n0 + w + 3, (b + (w + 3) // TT) * TT + v, (w + 3) % 2, l * NB + b + (w + 3) // TT + 1)
                    if w < 2 or nxt:
                        rotate(n0 + w + 2, w % 2)
                        rnorm(n0 + w + 2, (w + 2) % TT)

            def mlp_rstd(m):
                wait_alone(pool, d_aggr, 4 * m + 4)
                pool.tensor_scalar(var_eps[:, :], mean_var[:, :, 1], 1.0, LN_EPS, ALU.mult, ALU.add)\
                    .then_inc(d_eps, 1)
                pool.wait_ge(d_eps, m + 1)
                pool.tensor_tensor(rstd[:, :], var_eps[:, :], minus_half[:, 0:TT], ALU.pow).then_inc(d_rstd, 1)

            with pool.Fori(0, LAYERS) as l:
                n0 = l * NT
                pool.wait_ge(c_xt, n0)
                for w in range(3):
                    wait_alone(pool, b_res, l * NB + 1)
                    if w == 2:
                        wait_alone(pool, c_xt, n0 + 1)
                    pool.tensor_copy(x_tile[:, w % 2, :], inner[:, w, :]).then_inc(c_xs, 1)
                for w in range(2):
                    pool.wait_ge(c_t, 2 * n0)
                    for i, dst in enumerate((q_tok, k_tok)):
                        pool.wait_ge(c_rope, 6 * (n0 + w) + 3 * i + 3)
                        pool.tensor_tensor(dst[:, w % 2, :], rot[:, 2 * i, :], rot[:, 2 * i + 1, :], ALU.add)\
                            .then_inc(c_add, 1)
                    rnorm(n0 + w, w)
                with pool.Fori(0, NB - 1) as b:
                    attention(n0 + b * TT, b, l, True)
                attention(n0 + (NB - 1) * TT, NB - 1, l, False)
                mlp_rstd(l * NB)
                with pool.Fori(0, NB - 1) as b:
                    mlp_rstd(l * NB + b + 1)
            for b in range(NB):
                pool.wait_ge(b_res, NB * LAYERS + b + 1)
                pool.tensor_tensor(stream[:, tiles(b), :], stream[:, tiles(b), :], inner[:, tiles(b), :], ALU.add)\
                    .then_inc(out_sum, 1)

        @block.vector
        def _(dve):
            def norm(n, b, to_inner=False):
                for t in range(TT):
                    dve.bn_stats(stats[:, t, 0:6], stream[:, b * TT + t, :]).then_inc(n_stats, 1)
                for t in range(TT):
                    wait_alone(dve, n_stats, 4 * n + t + 1)
                    dve.bn_aggr(mean_var[:, t, :], stats[:, t, 0:6]).then_inc(n_aggr, 1)
                dve.wait_ge(n_rstd, n + 1)
                for t in range(TT):
                    dst = inner[:, b * TT + t, :] if to_inner else normed[:, t, :]
                    done = n_norm if not to_inner else n_inner if t < TT - 1 else b_res
                    dve.tensor_scalar(dst, stream[:, b * TT + t, :], mean_var[:, t, 0:1],
                                      rstd[:, t:t + 1], ALU.subtract, ALU.mult).then_inc(done, 1)

            def conv_taps(b):
                for j in range(KR):
                    dve.wait_ge(a_tap0, 3 * b + j + 1)
                    for k in range(1, TAPS):
                        ins = dve.scalar_tensor_tensor(
                            conv[:, j, :], raw[:, j, TAPS - 1 - k:TAPS - 1 - k + T],
                            cols[:, C_CONVW + TAPS * j + TAPS - 1 - k:C_CONVW + TAPS * j + TAPS - k],
                            conv[:, j, :], ALU.mult, ALU.add)
                        if k < TAPS - 1:
                            ins.then_inc(a_tap, 1)
                            dve.wait_ge(a_tap, 6 * b + 2 * j + k)
                        else:
                            ins.then_inc(a_conv, 1)

            def recurrence(b):
                for j in range(KR):
                    dve.wait_ge(a_th, 3 * b + j + 1)
                    dve.scalar_tensor_tensor(th_in[:, j, :], th_in[:, j, :], 1.0, conv[:, j, :], ALU.add,
                                             ALU.mult).then_inc(a_xs0, 1)
                dve.wait_ge(a_beta, b + 1)
                for j in range(KR):
                    dve.wait_ge(a_xs0, 3 * b + j + 1)
                    dve.tensor_tensor(th_in[:, j, :], th_in[:, j, :], beta[:, j, :], ALU.mult).then_inc(a_xs, 1)
                for j in range(KR):
                    dve.wait_ge(a_xs, 3 * b + j + 1)
                    dve.tensor_tensor_scan(scanned[:, j, :], alpha[:, j, :], th_in[:, j, :], 0.0, ALU.mult,
                                           ALU.add).then_inc(a_scan, 1)
                dve.wait_ge(a_gelu, 3 * b + 3)
                for j in range(KR):
                    dve.wait_ge(a_scan, 3 * b + j + 1)
                    dve.tensor_tensor(scanned[:, j, :], scanned[:, j, :], gate_act[:, b % 2, j, :], ALU.mult)\
                        .then_inc(a_gh, 1)

            def residual(b):
                for h in range(2):
                    dve.wait_ge(a_o, 2 * b + h + 1)
                    t = slice(0, 2)
                    s = stream[:, bass.ds(b * TT + 2 * h, 2), :]
                    dve.tensor_tensor(s, s, bank[6 + h][:, :].rearrange("p (t d) -> p t d", t=2), ALU.add)\
                        .then_inc(a_res, 1)

            def embed(b, n):
                dve.wait_ge(a_res, 2 * b + 2)
                if isinstance(b, int) and b == 0:
                    dve.wait_ge(a_tp, 2 * NB)
                else:
                    dve.wait_ge(b_tp, 2 * b)
                    dve.wait_ge(b_embo, b)
                norm(n, b)
                dve.wait_ge(n_norm, 4 * (NB + b) + 4)
                dve.tensor_tensor(normed[:, :, :], normed[:, :, :], emb[:, tiles(b), :], ALU.add).then_inc(b_emb, 1)

            def keys_values(b):
                for m in range(KD):
                    dve.wait_ge(b_full, 6 * b + m + 1)
                    dve.tensor_reduce(kstat[:, m, 0:1], bank[2 + m][:, :], AX_X, ALU.max).then_inc(b_kmax, 1)
                for m in range(KD):
                    bk = cols[:, C_BK + m:C_BK + m + 1]
                    dve.wait_ge(b_kmax, 4 * b + m + 1)
                    dve.tensor_scalar(kstat[:, m, 1:2], kstat[:, m, 0:1], bk, -1.0, ALU.add, ALU.mult)\
                        .then_inc(b_kmax, 1)
                for m in range(KD):
                    dve.wait_ge(b_kmax, 4 * b + 2 + m + 1)
                    dve.tensor_scalar(kstat[:, m, 2:3], kstat[:, m, 1:2], cols[:, C_BK + m:C_BK + m + 1], None,
                                      ALU.add).then_inc(b_kbias, 1)
                for m in range(KD):
                    dve.wait_ge(b_full, 6 * b + 2 + m + 1)
                    dve.wait_ge(b_ek, 2 * b + m + 1)
                    dve.scalar_tensor_tensor(ekv[:, m, :], bank[4 + m][:, :], cols[:, C_BV + m:C_BV + m + 1],
                                             ek[:, m, :], ALU.add, ALU.mult).then_inc(b_ekv, 1)

            def gated_ratio(b):
                for m in range(KD):
                    den, num = bank[2 + (2 * m + 2) % 4], bank[2 + (2 * m + 3) % 4]
                    dve.wait_ge(b_aft, 4 * b + 2 * m + 1)
                    dve.scalar_tensor_tensor(y[:, m, :], eq[:, m, :], 1.0, den[:, :], ALU.add, ALU.mult)\
                        .then_inc(b_den, 1)
                    dve.wait_ge(b_den, 2 * b + m + 1)
                    dve.reciprocal(y[:, m, :], y[:, m, :]).then_inc(b_rec, 1)
                    dve.wait_ge(b_rec, 2 * b + m + 1)
                    dve.wait_ge(b_aft, 4 * b + 2 * m + 2)
                    dve.tensor_tensor(y[:, m, :], y[:, m, :], num[:, :], ALU.mult).then_inc(b_y, 1)

            def lstat(i, s, src, done, of):
                for t in range(TT):
                    dve.wait_ge(done, of + t // 2 + 1)
                    dve.bn_stats(lstats[:, s, t, :], src[:, t, :]).then_inc(l_stats, 1)
                for t in range(TT):
                    wait_alone(dve, l_stats, 4 * i + t + 1)
                    dve.bn_aggr(lmv[:, s, t, :], lstats[:, s, t, :]).then_inc(l_aggr, 1)

            def norm_affine(i, s, src, dst):
                for t in range(TT):
                    dve.wait_ge(l_aggr, 4 * i + t + 1)
                    dve.scalar_tensor_tensor(src[:, t, :], src[:, t, :], lmv[:, s, t, 0:1], rows[:, R_GAMMA, :],
                                             ALU.subtract, ALU.mult).then_inc(l_mid, 1)
                dve.wait_ge(l_rstd, i + 1)
                for t in range(TT):
                    dve.wait_ge(l_mid, 4 * i + t + 1)
                    dve.scalar_tensor_tensor(dst[:, t, :], src[:, t, :], lrstd[:, s, t:t + 1], rows[:, R_BETA, :],
                                             ALU.mult, ALU.add).then_inc(l_out, 1)

            def mixed(b):
                dve.wait_ge(b_embo, b + 1)
                for h in range(2):
                    dve.wait_ge(b_o, 2 * b + h + 1)
                    dve.tensor_tensor(mix[:, 2 * h:2 * h + 2, :], emb[:, bass.ds(b * TT + 2 * h, 2), :],
                                      bank[6 + h][:, :].rearrange("p (t d) -> p t d", t=2), ALU.add)\
                        .then_inc(b_mix, 1)
                lstat(2 * b, 0, mix, b_mix, 2 * b)

            def to_a(b):
                dve.wait_ge(b_ab2, b)
                dve.wait_ge(b_ta, 2 * b)
                norm_affine(2 * b, 0, mix, a_tok)

            def mlp_sum(b):
                dve.wait_ge(b_ab2, b + 1)
                for h in range(2):
                    dve.wait_ge(b_f2, 2 * b + h + 1)
                    dve.tensor_tensor(a_b2[:, 2 * h:2 * h + 2, :], a_b2[:, 2 * h:2 * h + 2, :],
                                      bank[6 + h][:, :].rearrange("p (t d) -> p t d", t=2), ALU.add)\
                        .then_inc(b_sum, 1)
                lstat(2 * b + 1, 1, a_b2, b_sum, 2 * b)

            dve.wait_ge(x0_in, 16)
            dve.wait_ge(ready_consts, 2)
            norm(0, 0)
            dve.wait_ge(col_in, 16)
            dve.tensor_scalar(fb_tmp[:, 2, :], cols[:, C_FB:C_FB + KR], 0.0, None, ALU.max).then_inc(fb_vec, 1)
            dve.tensor_scalar(half_bf[:, :], cols[:, C_BG:C_BG + 2 * KR], 0.5, None, ALU.mult).then_inc(fb_vec, 1)
            dve.wait_ge(fb_step, 3)
            dve.wait_ge(fb_vec, 1)
            dve.tensor_tensor(fb_tmp[:, 2, :], fb_tmp[:, 2, :], fb_tmp[:, 0, :], ALU.add).then_inc(fb_vec, 1)
            dve.wait_ge(fb_vec, 3)
            dve.tensor_scalar(m4sp[:, :], fb_tmp[:, 2, :], -4.0, None, ALU.mult).then_inc(fb_vec, 1)
            conv_taps(0)
            dve.wait_ge(xr_in, 16)
            with dve.Fori(0, NB - 1) as b:
                dve.wait_ge(a_tp, 2 * b + 2)
                norm(b + 1, b + 1)
                recurrence(b)
                conv_taps(b + 1)
                residual(b)
            dve.wait_ge(e_band, 2)
            dve.tensor_reduce(ew_stat[:, :, 0], ew[:, :, :], AX_X, ALU.max).then_inc(e_max, 1)
            dve.wait_ge(e_max, 1)
            dve.tensor_scalar(ew_stat[:, :, 1], ew_stat[:, :, 0], -1.0, None, ALU.mult).then_inc(e_neg, 1)
            dve.wait_ge(ctx_sem, 16)
            embed(0, NB)
            recurrence(NB - 1)
            keys_values(0)
            residual(NB - 1)
            embed(1, NB + 1)
            dve.wait_ge(rows_sem, 16)
            gated_ratio(0)
            mixed(0)
            to_a(0)

            def mixing(b, nxt, norm2):
                if nxt:
                    keys_values(b + 1)
                if norm2:
                    embed(b + 2, 2 * b + NB + 2)
                if nxt:
                    gated_ratio(b + 1)
                mlp_sum(b)
                if nxt:
                    mixed(b + 1)
                dve.wait_ge(b_x2, b)
                norm_affine(2 * b + 1, 1, a_b2, mixed_out)
                if nxt:
                    to_a(b + 1)
                dve.wait_ge(b_x2, b + 1)
                norm(2 * b + NB + 3 if norm2 else b + 2 * NB, b, to_inner=True)

            with dve.Fori(0, NB - 2) as b:
                mixing(b, True, True)
            mixing(NB - 2, True, False)
            mixing(NB - 1, False, False)



            def tables(l):
                for i in range(4):
                    s = qk_scale_sb[:, l, i // 2, :].unsqueeze(1)
                    src = rope_sb[:, i, :, :]
                    dst = rope_l[:, i, :, :]
                    if i % 2:
                        for lo, other in ((0, DH // 2), (DH // 2, 0)):
                            dve.tensor_tensor(dst[:, :, lo:lo + DH // 2], src[:, :, lo:lo + DH // 2],
                                              s[:, :, other:other + DH // 2].to_broadcast([P, TT, DH // 2]),
                                              ALU.mult).then_inc(c_tab, 1)
                    else:
                        dve.tensor_tensor(dst, src, s.to_broadcast([P, TT, DH]), ALU.mult).then_inc(c_tab, 1)

            def rope_products(n, w, i, first=False):
                src = bank[i][:, :].rearrange("p (h d) -> p h d", d=DH)
                dve.wait_ge(c_sq, 2 * n + i + 1)
                if not first:
                    dve.wait_ge(c_add, 2 * n - 1 + i)
                cos = rope_l[:, 2 * i, w:w + 1, :].to_broadcast([P, HEADS, DH])
                dve.tensor_tensor(rot[:, 2 * i, :].rearrange("p (h d) -> p h d", d=DH), src, cos, ALU.mult)\
                    .then_inc(c_rope, 1)
                rotated = rot[:, 2 * i + 1, :].rearrange("p (h d) -> p h d", d=DH)
                for lo, other in ((0, DH // 2), (DH // 2, 0)):
                    sin = rope_l[:, 2 * i + 1, w:w + 1, lo:lo + DH // 2].to_broadcast([P, HEADS, DH // 2])
                    dve.tensor_tensor(rotated[:, :, lo:lo + DH // 2], src[:, :, other:other + DH // 2], sin,
                                      ALU.mult).then_inc(c_rope, 1)

            def sum_squares(n):
                dve.wait_ge(c_sq, 2 * n + 2)
                dve.wait_ge(c_clip, n)
                dve.tensor_reduce(norms[:, 0, :], squares[:, :, :].rearrange("p i (h d) -> p (i h) d", d=DH), AX_X,
                                  ALU.add).then_inc(c_ss, 1)

            def norm_keys(n, par):
                dve.wait_ge(c_add, 2 * n + 2)
                dve.wait_ge(c_rn, n + 1)
                k = k_tok[:, par, :].rearrange("p (h d) -> p h d", d=DH)
                dve.tensor_tensor(k, k, norms[:, 2, HEADS:2 * HEADS].unsqueeze(2).to_broadcast([P, HEADS, DH]),
                                  ALU.mult).then_inc(c_kn, 1)

            def q_odd(n):
                dve.wait_ge(c_t, 2 * n + 2)
                dve.tensor_copy(q_heads[64:128, :, :].rearrange("p (c e) t -> p e c t", e=2)[:, 1, :, :],
                                bank[2][64:128, :].rearrange("p (c t) -> p c t", t=P)).then_inc(c_qo, 1)

            def masked(n, w, i, first=False):
                u = 4 * n + i
                nk = 2 * P if w else P
                if w or i >= 2:
                    dve.wait_ge(c_ex, 2 * u - 2)
                wait_alone(dve, c_qk, u + 1)
                for e in range(2):
                    dve.tensor_tensor_reduce(scores[:, i % 2, e, 0:nk], bank[6 + i % 2][:, e * 2 * P:e * 2 * P + nk],
                                             mask[:, 2 * P - nk:2 * P], 1.0, NEG, ALU.add, ALU.max,
                                             row_max[:, w % 2, 2 * i + e:2 * i + e + 1]).then_inc(c_tt, 1)
                dve.wait_ge(c_tt, 2 * u + 2)
                dve.wait_ge(c_rq, n + 1)
                dve.scalar_tensor_tensor(row_bias[:, w % 2, 2 * i:2 * i + 2], row_max[:, w % 2, 2 * i:2 * i + 2],
                                         -1.0, q_rnorm[:, w, 2 * i:2 * i + 2], ALU.mult, ALU.mult).then_inc(c_nb, 1)

            def normalise(n, w):
                dve.wait_ge(c_ex, 8 * n + 8)
                dve.reciprocal(row_rsum[:, :], row_sum[:, w % 2, :]).then_inc(c_ri, 1)
                dve.wait_ge(c_ri, n + 1)
                dve.wait_ge(c_pv, 4 * n + 4)
                dve.tensor_tensor(o_tok[:, :].rearrange("p (h d) -> p h d", d=DH),
                                  bank[3][:, :].rearrange("p (h d) -> p h d", d=DH),
                                  row_rsum[:, :].unsqueeze(2).to_broadcast([P, HEADS, DH]), ALU.mult)\
                    .then_inc(c_on, 1)

            def o_transposed(n):
                dve.wait_ge(c_ot, n + 1)
                dve.tensor_copy(o_t[:, :, :].rearrange("p c t -> p (c t)"), bank[2][:, :]).then_inc(c_ot_out, 1)

            def att_residual(n, tile):
                dve.wait_ge(c_wo, n + 1)
                dve.tensor_tensor(inner[:, tile, :], inner[:, tile, :], bank[2][:, 0:D], ALU.add).then_inc(c_res, 1)

            def attention(n0, b, l, nxt):
                for w in range(TT):
                    n = n0 + w
                    two, one = (w < 2 or nxt), (w < 3 or nxt)
                    masked(n, w, 0)
                    masked(n, w, 1)
                    if w:
                        o_transposed(n - 1)
                    if one:
                        norm_keys(n + 1, (w + 1) % 2)
                    if two:
                        rope_products(n + 2, (w + 2) % TT, 0)
                    masked(n, w, 2)
                    if two:
                        rope_products(n + 2, (w + 2) % TT, 1)
                    if w:
                        att_residual(n - 1, b * TT + w - 1)
                    masked(n, w, 3)
                    if two:
                        sum_squares(n + 2)
                    if one:
                        q_odd(n + 1)
                    normalise(n, w)
                    if w == TT - 1:
                        o_transposed(n)
                        att_residual(n, b * TT + w)

            def mlp_stats(m, b, t):
                dve.wait_ge(d_shift, 32 * m + 32)
                for i, src in enumerate((inner[:, b * TT + t, 0:P], shifted[:, t, :])):
                    dve.bn_stats(stats[:, t, 6 * i:6 * i + 6], src).then_inc(d_stats, 1)

            def mlp_aggr(m):
                for t in range(TT):
                    wait_alone(dve, d_stats, 8 * m + 2 * t + 2)
                    dve.bn_aggr(mean_var[:, t, :], stats[:, t, :]).then_inc(d_aggr, 1)

            def mlp_norm(m, b):
                dve.wait_ge(d_rstd, m + 1)
                dve.wait_ge(d_tp, 2 * m)
                for t in range(TT):
                    for i, src in enumerate((inner[:, b * TT + t, 0:P], shifted[:, t, :])):
                        dve.tensor_scalar(normed[:, t, i * P:(i + 1) * P], src, mean_var[:, t, 0:1],
                                          rstd[:, t:t + 1], ALU.subtract, ALU.mult).then_inc(d_norm, 1)

            def mlp(m, b, nxt):
                for j in range(KH):
                    r = P if j < KH - 1 else HLAST
                    dve.wait_ge(d_w1, 2 * (KH * m + j) + 2)
                    dve.wait_ge(d_gelu, KH * m + j + 1)
                    dve.scalar_tensor_tensor(hidden[0:r, j, :], bank[3 + 2 * (j % 2)][0:r, :],
                                             lcols[0:r, L_B1A + j:L_B1A + j + 1], gelu[0:r, j % 2, :], ALU.add,
                                             ALU.mult).then_inc(d_act, 1)
                    if nxt:
                        if j < TT:
                            mlp_stats(m + 1, b + 1, j)
                        if j == TT:
                            mlp_aggr(m + 1)
                if nxt:
                    mlp_norm(m + 1, b + 1)
                for h in range(2):
                    dve.wait_ge(d_w2, TT * m + 2 * h + 2)
                    s = inner[:, bass.ds(b * TT + 2 * h, 2), :]
                    dve.tensor_tensor(s, s, bank[6 + h][:, :].rearrange("p (t d) -> p t d", t=2), ALU.add)\
                        .then_inc((d_res0, b_res)[h], 1)

            dve.wait_ge(c_zero, 4)
            dve.wait_ge(rope_in, 48)
            with dve.Fori(0, LAYERS) as l:
                n0 = l * NT
                tables(l)
                dve.wait_ge(d_gelu, KH * NB * l)
                dve.tensor_copy(lcols[:, :], lcols_all[:, l, :]).then_inc(c_lcols, 1)
                dve.wait_ge(c_tab, 6 * l + 6)
                for w in range(2):
                    dve.wait_ge(c_add, 2 * n0 + 2 * w)
                    for i in range(2):
                        rope_products(n0 + w, w, i, first=(w == 0))
                    sum_squares(n0 + w)
                    if w == 0:
                        norm_keys(n0, 0)
                q_odd(n0)
                with dve.Fori(0, NB - 1) as b:
                    attention(n0 + b * TT, b, l, True)
                attention(n0 + (NB - 1) * TT, NB - 1, l, False)
                for t in range(TT):
                    mlp_stats(l * NB, 0, t)
                mlp_aggr(l * NB)
                mlp_norm(l * NB, 0)
                wait_alone(dve, c_lcols, l + 1)
                with dve.Fori(0, NB - 1) as b:
                    mlp(l * NB + b, b, True)
                mlp(l * NB + NB - 1, NB - 1, False)

        @block.scalar
        def _(act):
            def transposed_out(b):
                for c in range(KD):
                    act.wait_ge(a_tp, 2 * b + c + 1)
                    act.activation(normed_t[:, c, :], bank[c][:, :], ACT.Copy).then_inc(a_tp_out, 1)

            def inputs(b):
                for j in range(KR):
                    u = 12 * b + j
                    src = bank[2 + j % 4]
                    act.wait_ge(a_full, u + 1)
                    act.activation(raw[:, j, TAPS - 1:TAPS - 1 + T], src[:, :], ACT.Copy).then_inc(a_raw, 1)
                    act.activation(conv[:, j, :], src[:, :], ACT.Identity,
                                   bias=cols[:, C_CONVB + j:C_CONVB + j + 1],
                                   scale=cols[:, C_CONVW + TAPS * j + TAPS - 1:C_CONVW + TAPS * j + TAPS])\
                        .then_inc(a_tap0, 1)
                for j in range(KR):
                    act.wait_ge(a_full, 12 * b + KR + j + 1)
                    act.activation(gate_act[:, b % 2, j, :], bank[2 + (KR + j) % 4][:, :], ACT.Gelu).then_inc(a_gelu, 1)

            act.wait_ge(col_in, 16)
            act.activation(minus_bq[:, :], cols[:, C_BQ:C_BQ + KD], ACT.Copy, scale=-1.0)
            act.activation(fb_tmp[:, 0, :], cols[:, C_FB:C_FB + KR], ACT.Abs).then_inc(fb_step, 1)
            act.wait_ge(fb_step, 1)
            act.activation(fb_tmp[:, 1, :], fb_tmp[:, 0, :], ACT.Exp, scale=-1.0).then_inc(fb_step, 1)
            act.wait_ge(fb_step, 2)
            act.activation(fb_tmp[:, 0, :], fb_tmp[:, 1, :], ACT.Ln, bias=1.0).then_inc(fb_step, 1)
            transposed_out(0)
            inputs(0)

            def gates(b, last):
                act.wait_ge(fb_vec, 4)
                for j in range(KR):
                    act.wait_ge(a_full, 12 * b + 6 + 2 * j + 1)
                    act.activation(beta[:, j, :], bank[2 + (2 * j + 2) % 4][:, :], ACT.Tanh,
                                   bias=half_bf[:, j:j + 1], scale=0.5).then_inc(a_thf, 1)
                    act.wait_ge(a_full, 12 * b + 6 + 2 * j + 2)
                    act.activation(th_in[:, j, :], bank[2 + (2 * j + 3) % 4][:, :], ACT.Tanh,
                                   bias=half_bf[:, KR + j:KR + j + 1], scale=0.5).then_inc(a_th, 1)
                    act.wait_ge(a_thf, 3 * b + j + 1)
                    act.activation(alpha[:, j, :], beta[:, j, :], ACT.Exp, bias=m4sp[:, j:j + 1],
                                   scale=m4sp[:, j:j + 1]).then_inc(a_exp, 1)
                    if j == 0 and not last:
                        transposed_out(b + 1)
                for j in range(KR):
                    act.wait_ge(a_exp, 3 * b + j + 1)
                    act.activation(beta[:, j, :], alpha[:, j, :], ACT.Square).then_inc(a_sq, 1)
                act.wait_ge(a_sq, 3 * b + 3)
                act.activation(beta[:, :, :], beta[:, :, :], ACT.Sqrt, bias=quarter[:, 0:1], scale=-0.25)\
                    .then_inc(a_beta, 1)

            with act.Fori(0, NB - 1) as b:
                gates(b, False)
                act.wait_ge(a_xs0, 3 * b + 3)
                act.wait_ge(a_conv, 3 * b + 3)
                inputs(b + 1)
            gates(NB - 1, True)

            act.wait_ge(e_neg, 1)
            for t in range(TT):
                act.activation(ew[:, t, :], ew[:, t, :], ACT.Exp, bias=ew_stat[:, t, 1:2]).then_inc(e_exp, 1)
            for j in range(TT):
                act.wait_ge(e_tp, j + 1)
                act.activation(ew_t[:, j, :], bank[2 + j][:, :], ACT.Copy).then_inc(e_tp_out, 1)

            def transposed_emb(b):
                for c in range(KD):
                    act.wait_ge(b_tp, 2 * b + c + 1)
                    act.activation(normed_t[:, c, :], bank[c][:, :], ACT.Copy).then_inc(b_tp_out, 1)

            def exps(b):
                for m in range(KD):
                    act.wait_ge(b_kbias, 2 * b + m + 1)
                    act.activation(ek[:, m, :], bank[2 + m][:, :], ACT.Exp, bias=kstat[:, m, 2:3]).then_inc(b_ek, 1)
                for m in range(KD):
                    act.wait_ge(b_full, 6 * b + 4 + m + 1)
                    act.activation(eq[:, m, :], bank[2 + m][:, :], ACT.Exp, bias=minus_bq[:, m:m + 1], scale=-1.0)\
                        .then_inc(b_eq, 1)

            def by_token(b):
                for i, dst in enumerate((ek_tok, ek_tok, ekv_tok, ekv_tok)):
                    h = i % 2
                    act.wait_ge(b_tk, 4 * b + i + 1)
                    act.activation(dst[:, 2 * h:2 * h + 2, :],
                                   bank[2 + (2 + i) % 4][:, :].rearrange("p (t d) -> p t d", t=2), ACT.Copy)\
                        .then_inc(b_tk_out, 1)

            def mlp(b):
                for c in range(KD):
                    act.wait_ge(b_ta, 2 * b + c + 1)
                    act.activation(a_t[:, c, :], bank[c][:, :], ACT.Copy).then_inc(b_ta_out, 1)
                for c in range(KF):
                    act.wait_ge(b_f1, KF * b + c + 1)
                    act.activation(ff[:, c, :], bank[2 + (2 + c) % 4][:, :], ACT.Relu,
                                   bias=cols[:, C_B1 + c:C_B1 + c + 1]).then_inc(b_relu, 1)

            transposed_emb(0)
            exps(0)
            by_token(0)

            def mixing(b, nxt):
                if nxt:
                    transposed_emb(b + 1)
                    exps(b + 1)
                mlp(b)
                if nxt:
                    by_token(b + 1)

            with act.Fori(0, NB - 1) as b:
                mixing(b, True)
            mixing(NB - 1, False)

            def x_transposed(n, w):
                act.wait_ge(c_xt, n + 1)
                act.activation(x_t[:, 0, w * P:(w + 1) * P], bank[2][:, 0:P], ACT.Copy)
                act.activation(x_t[:, 1, w * P + 1:(w + 1) * P + 1], bank[2][:, P:2 * P], ACT.Copy)\
                    .then_inc(c_xt_out, 1)

            def square(n, i):
                act.wait_ge(c_p, 3 * n + i + 1)
                act.wait_ge(c_ss, n)
                act.activation(squares[:, i, :], bank[i][:, :], ACT.Square).then_inc(c_sq, 1)

            def values(n, w):
                act.wait_ge(c_p, 3 * n + 3)
                act.activation(v_tok[:, w, :], bank[0][:, :], ACT.Copy).then_inc(c_v, 1)

            def keys(n, w):
                act.wait_ge(c_t, 2 * n + 1)
                act.activation(k_t[:, :, w * P:(w + 1) * P], bank[2][:, :].rearrange("p (c t) -> p c t", t=P),
                               ACT.Copy).then_inc(c_kt, 1)

            def q_even(n):
                act.wait_ge(c_t, 2 * n + 2)
                act.activation(q_heads[0:64, :, :].rearrange("p (c e) t -> p e c t", e=2)[:, 0, :, :],
                               bank[2][0:64, :].rearrange("p (c t) -> p c t", t=P), ACT.Copy).then_inc(c_qe, 1)

            def exps(n, w, i):
                u = 4 * n + i
                nk = 2 * P if w else P
                act.wait_ge(c_nb, u + 1)
                if w or i >= 2:
                    act.wait_ge(c_pt, u - 1)
                for e in range(2):
                    h = 2 * i + e
                    act.activation(probs[:, i % 2, e, 0:nk], scores[:, i % 2, e, 0:nk], ACT.Exp,
                                   bias=row_bias[:, w % 2, h:h + 1], scale=q_rnorm[:, w, h:h + 1],
                                   accum_out=row_sum[:, w % 2, h:h + 1]).then_inc(c_ex, 1)

            def probs_transposed(n, w, i):
                u = 4 * n + i
                act.wait_ge(c_pt, u + 1)
                if w or i >= 2:
                    act.wait_ge(c_pv, u - 1)
                if w:
                    act.activation(probs_t[:, i % 2, :, :], bank[4 + i % 2][:, :].rearrange("p (c t) -> p c t", t=P),
                                   ACT.Copy).then_inc(c_pt_out, 1)
                else:
                    act.activation(probs_t[:, i % 2, 0:4:2, :],
                                   bank[4 + i % 2][:, :].rearrange("p (c t) -> p c t", t=P)[:, 0:4:2, :],
                                   ACT.Copy).then_inc(c_pt_out, 1)

            def attention(n0, nxt):
                for w in range(TT):
                    n = n0 + w
                    two, one, three = (w < 2 or nxt), (w < 3 or nxt), (w < 1 or nxt)
                    exps(n, w, 0)
                    if two:
                        square(n + 2, 0)
                    exps(n, w, 1)
                    probs_transposed(n, w, 0)
                    if two:
                        square(n + 2, 1)
                    exps(n, w, 2)
                    probs_transposed(n, w, 1)
                    exps(n, w, 3)
                    probs_transposed(n, w, 2)
                    if two and w < TT - 1:
                        values(n + 2, (w + 2) % TT)
                    if three:
                        x_transposed(n + 3, (w + 3) % TT)
                    if one:
                        keys(n + 1, (w + 1) % TT)
                    probs_transposed(n, w, 3)
                    if one:
                        q_even(n + 1)
                    if two and w == TT - 1:
                        values(n + 2, (w + 2) % TT)

            def mlp_input(m):
                for c in range(KD):
                    act.wait_ge(d_tp, 2 * m + c + 1)
                    act.activation(normed_t[:, c, :], bank[c][:, :], ACT.Identity, bias=lcols[:, L_B + c:L_B + c + 1],
                                   scale=lcols[:, L_G + c:L_G + c + 1]).then_inc(d_tp_out, 1)

            def mlp(m, nxt):
                for j in range(KH):
                    r = P if j < KH - 1 else HLAST
                    act.wait_ge(d_w1, 2 * (KH * m + j) + 1)
                    if j >= 2:
                        act.wait_ge(d_act, KH * m + j - 1)
                    act.activation(gelu[0:r, j % 2, :], bank[2 + 2 * (j % 2)][0:r, :], ACT.Gelu,
                                   bias=lcols[0:r, L_B1G + j:L_B1G + j + 1]).then_inc(d_gelu, 1)
                if nxt:
                    mlp_input(m + 1)

            act.wait_ge(c_zero, 4)
            with act.Fori(0, LAYERS) as l:
                n0 = l * NT
                for w in range(2):
                    x_transposed(n0 + w, w)
                for w in range(2):
                    square(n0 + w, 0)
                    square(n0 + w, 1)
                    values(n0 + w, w)
                x_transposed(n0 + 2, 2)
                keys(n0, 0)
                q_even(n0)
                with act.Fori(0, NB - 1) as b:
                    attention(n0 + b * TT, True)
                attention(n0 + (NB - 1) * TT, False)
                act.wait_ge(c_lcols, l + 1)
                mlp_input(l * NB)
                with act.Fori(0, NB - 1) as b:
                    mlp(l * NB + b, True)
                mlp(l * NB + NB - 1, False)

        @block.tensor
        def _(pe):
            def transpose_in(b):
                pe.wait_ge(n_norm, 4 * b + 4)
                for c in range(KD):
                    for t in range(TT):
                        ins = pe.transpose(bank[c][:, t * P:(t + 1) * P], normed[:, t, c * P:(c + 1) * P],
                                           ident[:, :])
                    ins.then_inc(a_tp, 1)

            def inputs(b):
                pe.wait_ge(a_tp_out, 2 * b + 2)
                for j in range(2 * KR):
                    m = (j + KR) % (2 * KR)
                    if not (isinstance(b, int) and b == 0):
                        if j < 4:
                            if j % 2 == 0:
                                pe.wait_ge(a_thf, 3 * (b - 1) + (2 + j) // 2 + 1)
                            else:
                                pe.wait_ge(a_th, 3 * (b - 1) + (2 + j) // 2 + 1)
                    if j >= 4:
                        pe.wait_ge(a_tap0, 3 * b + j - 4 + 1)
                    for k in range(KD):
                        ins = pe.matmul(bank[2 + j % 4][:, :], w_in_sb[:, k, m * P:(m + 1) * P],
                                        normed_t[:, k, :], start=(k == 0), stop=(k == KD - 1))
                    ins.then_inc(a_full, 1)

            def gates(b, last):
                pe.wait_ge(a_conv, 3 * b + 3)
                for j in range(KR):
                    for g in range(2):
                        u = 2 * j + g
                        if u == 0:
                            pe.wait_ge(a_tap0, 3 * b + 3)
                        elif u < 4:
                            pe.wait_ge(a_gelu, 3 * b + u)
                        elif u == 4:
                            pe.wait_ge(a_thf, 3 * b + 1)
                        else:
                            pe.wait_ge(a_th, 3 * b + 1)
                        m = g * KR + j
                        for k in range(KR):
                            ins = pe.matmul(bank[2 + (u + 2) % 4][:, :], w_gate_sb[:, k, m * P:(m + 1) * P],
                                            conv[:, k, :], start=(k == 0), stop=(k == KR - 1))
                        ins.then_inc(a_full, 1)
                    if j == 0 and not last:
                        transpose_in(b + 1)

            def output(b):
                pe.wait_ge(a_gh, 3 * b + 3)
                pe.wait_ge(a_res, 2 * b)
                for t in range(TT):
                    for k in range(KR):
                        ins = pe.matmul(bank[6 + t // 2][:, (t % 2) * D:(t % 2 + 1) * D],
                                        scanned[:, k, t * P:(t + 1) * P], w_out_sb[:, k, :],
                                        start=(k == 0), stop=(k == KR - 1))
                    if t % 2:
                        ins.then_inc(a_o, 1)

            pe.wait_ge(ready_consts, 1)
            transpose_in(0)
            pe.wait_ge(w1s_in, 16)
            inputs(0)
            pe.wait_ge(wg_in, 16)
            pe.wait_ge(wor_in, 16)
            with pe.Fori(0, NB - 1) as b:
                gates(b, False)
                inputs(b + 1)
                output(b)
            gates(NB - 1, True)

            def bias_by_key():
                pe.wait_ge(a_th, 3 * NB)
                pe.wait_ge(a_thf, 3 * NB)
                pe.wait_ge(e_exp, TT)
                for j in range(TT):
                    for t in range(TT):
                        ins = pe.transpose(bank[2 + j][:, t * P:(t + 1) * P], ew[:, t, j * P:(j + 1) * P],
                                           ident[:, :])
                    ins.then_inc(e_tp, 1)

            def transpose_emb(b):
                pe.wait_ge(b_emb, b + 1)
                for c in range(KD):
                    for t in range(TT):
                        ins = pe.transpose(bank[c][:, t * P:(t + 1) * P], normed[:, t, c * P:(c + 1) * P],
                                           ident[:, :])
                    ins.then_inc(b_tp, 1)

            def project(b):
                pe.wait_ge(b_tp_out, 2 * b + 2)
                for i in range(3 * KD):
                    w, m = (w_k, w_v, w_q)[i // KD], i % KD
                    if i >= 2 * KD:
                        pe.wait_ge(b_ek, 2 * b + m + 1)
                    for k in range(KD):
                        ins = pe.matmul(bank[2 + i % 4][:, :], w[:, k, m * P:(m + 1) * P], normed_t[:, k, :],
                                        start=(k == 0), stop=(k == KD - 1))
                    ins.then_inc(b_full, 1)

            def keys_by_token(b):
                for i in range(4):
                    src, h = (ek, ekv)[i // 2], i % 2
                    if i == 0:
                        pe.wait_ge(b_ekv, 2 * b + 2)
                        pe.wait_ge(b_eq, 2 * b + 2)
                    if not (isinstance(b, int) and b == 0):
                        pe.wait_ge(b_relu, KF * (b - 1) + 5 + i)
                    for t in range(2):
                        for m in range(KD):
                            ins = pe.transpose(bank[2 + (2 + i) % 4][:, (2 * t + m) * P:(2 * t + m + 1) * P],
                                               src[:, m, (2 * h + t) * P:(2 * h + t + 1) * P], ident[:, :])
                    ins.then_inc(b_tk, 1)

            def mix_tokens(b):
                pe.wait_ge(b_tk_out, 4 * b + 4)
                for m in range(KD):
                    for i, src in enumerate((ek_tok, ekv_tok)):
                        for j in range(TT):
                            ins = pe.matmul(bank[2 + (2 * m + i + 2) % 4][:, :], src[:, j, m * P:(m + 1) * P],
                                            ew_t[:, j, :], start=(j == 0), stop=(j == TT - 1))
                        ins.then_inc(b_aft, 1)

            def project_mixed(b):
                pe.wait_ge(b_y, 2 * b + 2)
                for t in range(TT):
                    if t % 2 == 0:
                        pe.wait_ge(b_sum, 2 * b - 1 + t // 2) if not (isinstance(b, int) and b == 0) else None
                    for k in range(KD):
                        ins = pe.matmul(bank[6 + t // 2][:, (t % 2) * D:(t % 2 + 1) * D],
                                        y[:, k, t * P:(t + 1) * P], w_o[:, k, :], start=(k == 0),
                                        stop=(k == KD - 1))
                    if t % 2:
                        ins.then_inc(b_o, 1)

            def transpose_a(b):
                pe.wait_ge(l_out, 8 * b + 4)
                for c in range(KD):
                    for t in range(TT):
                        ins = pe.transpose(bank[c][:, t * P:(t + 1) * P], a_tok[:, t, c * P:(c + 1) * P],
                                           ident[:, :])
                    ins.then_inc(b_ta, 1)

            def mlp_up(b, nxt):
                pe.wait_ge(b_ta_out, 2 * b + 2)
                for c in range(KF):
                    if c >= 4:
                        pe.wait_ge(b_relu, KF * b + c - 3)
                    elif nxt:
                        pe.wait_ge(b_ekv if c < 2 else b_eq, 2 * (b + 1) + c % 2 + 1)
                    for k in range(KD):
                        ins = pe.matmul(bank[2 + (2 + c) % 4][:, :], w_1[:, k, c * P:(c + 1) * P], a_t[:, k, :],
                                        start=(k == 0), stop=(k == KD - 1))
                    ins.then_inc(b_f1, 1)

            def mlp_down(b):
                pe.wait_ge(b_mix, 2 * b + 2)
                for t in range(TT):
                    for k in range(KF):
                        if t == 0:
                            pe.wait_ge(b_relu, KF * b + k + 1)
                        ins = pe.matmul(bank[6 + t // 2][:, (t % 2) * D:(t % 2 + 1) * D],
                                        ff[:, k, t * P:(t + 1) * P], w_2[:, k, :], start=(k == 0),
                                        stop=(k == KF - 1))
                    if t % 2:
                        ins.then_inc(b_f2, 1)

            bias_by_key()
            transpose_emb(0)
            pe.wait_ge(e_tp_out, TT)
            pe.wait_ge(aft_in, 64)
            project(0)
            output(NB - 1)
            pe.wait_ge(a_res, 2 * NB)
            keys_by_token(0)
            mix_tokens(0)
            project_mixed(0)
            pe.wait_ge(mlp_in, 32)

            def mixing(b, nxt):
                if nxt:
                    transpose_emb(b + 1)
                    project(b + 1)
                transpose_a(b)
                mlp_up(b, nxt)
                if nxt:
                    keys_by_token(b + 1)
                    mix_tokens(b + 1)
                mlp_down(b)
                if nxt:
                    project_mixed(b + 1)

            with pe.Fori(0, NB - 1) as b:
                mixing(b, True)
            mixing(NB - 1, False)

            def transpose_x(n, par, free):
                for sem, v in free:
                    pe.wait_ge(sem, v)
                pe.wait_ge(c_xs, n + 1)
                for c in range(KD):
                    ins = pe.transpose(bank[2][:, c * P:(c + 1) * P], x_tile[:, par, c * P:(c + 1) * P], ident[:, :])
                ins.then_inc(c_xt, 1)

            def qkv(n, w, i, first=False):
                if i == 0:
                    pe.wait_ge(c_xt_out, n + 1)
                    pe.wait_ge(c_v, n)
                elif i == 1:
                    pe.wait_ge(c_rope, 6 * n)
                else:
                    pe.wait_ge(c_rope, 6 * n + 3)
                for k in range(KD):
                    ins = pe.matmul(bank[i % 2][:, :], x_t[:, k, w * P:(w + 1) * P],
                                    wqkv_sb[:, k, i * INNER:(i + 1) * INNER], start=(k == 0), stop=(k == KD - 1))
                ins.then_inc(c_p, 1)

            def transpose_k(n, par, free):
                for sem, v in free:
                    pe.wait_ge(sem, v)
                pe.wait_ge(c_kn, n + 1)
                for c in range(KI):
                    ins = pe.transpose(bank[2][:, c * P:(c + 1) * P], k_tok[:, par, c * P:(c + 1) * P], ident[:, :])
                ins.then_inc(c_t, 1)

            def transpose_q(n, par):
                pe.wait_ge(c_kt, n + 1)
                for c in range(KI):
                    ins = pe.transpose(bank[2][:, c * P:(c + 1) * P], q_tok[:, par, c * P:(c + 1) * P], ident[:, :])
                ins.then_inc(c_t, 1)

            def score(n, w, i):
                u = 4 * n + i
                if i == 0:
                    pe.wait_ge(c_qe, n + 1)
                    pe.wait_ge(c_qo, n + 1)
                if w or i >= 2:
                    pe.wait_ge(c_tt, 2 * u - 2)
                k0 = max(w - 1, 0) * P
                for e in range(2):
                    nk = (w + 1) * P - k0
                    ins = pe.matmul(bank[6 + i % 2][:, e * 2 * P:e * 2 * P + nk], q_heads[:, 2 * i + e, :],
                                    k_t[:, i, k0:(w + 1) * P], start=True, stop=True)
                ins.then_inc(c_qk, 1)

            def transpose_probs(n, w, i):
                u = 4 * n + i
                pe.wait_ge(c_ex, 2 * u + 2)
                if w or i >= 2:
                    pe.wait_ge(c_pt_out, u - 1)
                for e in range(2):
                    for k in range(2 if w else 1):
                        ins = pe.transpose(bank[4 + i % 2][:, (2 * e + k) * P:(2 * e + k + 1) * P],
                                           probs[:, i % 2, e, k * P:(k + 1) * P], ident[:, :])
                ins.then_inc(c_pt, 1)

            def weigh_values(n, w, i):
                u = 4 * n + i
                pe.wait_ge(c_pt_out, u + 1)
                if i == 0:
                    pe.wait_ge(c_v, n + 1)
                    pe.wait_ge(c_on, n)
                nk = 2 if w else 1
                for e in range(2):
                    h = 2 * i + e
                    for k in range(nk):
                        ins = pe.matmul(bank[3][:, h * DH:(h + 1) * DH], probs_t[:, i % 2, 2 * e + k, :],
                                        v_tok[:, w - nk + 1 + k, h * DH:(h + 1) * DH], start=(k == 0),
                                        stop=(k == nk - 1))
                ins.then_inc(c_pv, 1)

            def transpose_o(n, free):
                for sem, v in free:
                    pe.wait_ge(sem, v)
                pe.wait_ge(c_on, n + 1)
                for c in range(KI):
                    ins = pe.transpose(bank[2][:, c * P:(c + 1) * P], o_tok[:, c * P:(c + 1) * P], ident[:, :])
                ins.then_inc(c_ot, 1)

            def project_o(n):
                pe.wait_ge(c_ot_out, n + 1)
                for k in range(KI):
                    ins = pe.matmul(bank[2][:, 0:D], o_t[:, k, :], wo_sb[:, k, :], start=(k == 0), stop=(k == KI - 1))
                ins.then_inc(c_wo, 1)

            def attention(n0, nxt):
                free = [(c_qe, n0 + 1), (c_qo, n0 + 1), (c_res, n0)]
                for w in range(TT):
                    n = n0 + w
                    two, one, three = (w < 2 or nxt), (w < 3 or nxt), (w < 1 or nxt)
                    score(n, w, 0)
                    score(n, w, 1)
                    if w:
                        transpose_o(n - 1, free)
                    if two:
                        qkv(n + 2, (w + 2) % TT, 0)
                    transpose_probs(n, w, 0)
                    score(n, w, 2)
                    if two:
                        qkv(n + 2, (w + 2) % TT, 1)
                    weigh_values(n, w, 0)
                    transpose_probs(n, w, 1)
                    if w:
                        project_o(n - 1)
                        free = [(c_res, n)]
                    score(n, w, 3)
                    weigh_values(n, w, 1)
                    transpose_probs(n, w, 2)
                    if two and w < TT - 1:
                        qkv(n + 2, (w + 2) % TT, 2)
                    if three:
                        transpose_x(n + 3, (w + 3) % 2, free)
                        free = [(c_xt_out, n + 4)]
                    if one:
                        transpose_k(n + 1, (w + 1) % 2, free)
                    weigh_values(n, w, 2)
                    transpose_probs(n, w, 3)
                    if one:
                        transpose_q(n + 1, (w + 1) % 2)
                        free = [(c_qe, n + 2), (c_qo, n + 2)]
                    weigh_values(n, w, 3)
                    if w == TT - 1:
                        if two:
                            qkv(n + 2, (w + 2) % TT, 2)
                        transpose_o(n, free)
                        project_o(n)

            def transpose_mlp(m):
                pe.wait_ge(d_norm, 8 * m + 8)
                for c in range(KD):
                    for t in range(TT):
                        ins = pe.transpose(bank[c][:, t * P:(t + 1) * P], normed[:, t, c * P:(c + 1) * P],
                                           ident[:, :])
                    ins.then_inc(d_tp, 1)

            def mlp_up(m):
                pe.wait_ge(d_tp_out, 2 * m + 2)
                for j in range(KH):
                    r = P if j < KH - 1 else HLAST
                    for g, c0 in enumerate((HID, 0)):
                        if j >= 2:
                            pe.wait_ge((d_gelu, d_act)[g], KH * m + j - 1)
                        for k in range(KD):
                            ins = pe.matmul(bank[2 + 2 * (j % 2) + g][0:r, :], w1_sb[:, k, c0 + j * P:c0 + j * P + r],
                                            normed_t[:, k, :], start=(k == 0), stop=(k == KD - 1))
                        ins.then_inc(d_w1, 1)

            def mlp_down(m, t):
                if t % 2 == 0:
                    pe.wait_ge((d_res0, b_res)[t // 2], m if t == 0 else m + NB)
                for k in range(KH):
                    if t == 0:
                        pe.wait_ge(d_act, KH * m + k + 1)
                    r = P if k < KH - 1 else HLAST + 1
                    ins = pe.matmul(bank[6 + t // 2][:, (t % 2) * D:(t % 2 + 1) * D],
                                    hidden[0:r, k, t * P:(t + 1) * P], w2_sb[0:r, k, :], start=(k == 0),
                                    stop=(k == KH - 1))
                ins.then_inc(d_w2, 1)

            def mlp(m, nxt):
                mlp_up(m)
                mlp_down(m, 0)
                mlp_down(m, 1)
                if nxt:
                    transpose_mlp(m + 1)
                mlp_down(m, 2)
                mlp_down(m, 3)

            pe.wait_ge(c_zero, 4)
            with pe.Fori(0, LAYERS) as l:
                n0 = l * NT
                pe.wait_ge(watt_in, 32 * l + 32)
                transpose_x(n0, 0, [])
                transpose_x(n0 + 1, 1, [(c_xt_out, n0 + 1)])
                for w in range(2):
                    for i in range(3):
                        qkv(n0 + w, w, i)
                transpose_x(n0 + 2, 0, [(c_xt_out, n0 + 2)])
                transpose_k(n0, 0, [(c_xt_out, n0 + 3)])
                transpose_q(n0, 0)
                with pe.Fori(0, NB - 1) as b:
                    attention(n0 + b * TT, True)
                attention(n0 + (NB - 1) * TT, False)
                pe.wait_ge(wmlp_in, 32 * l + 32)
                transpose_mlp(l * NB)
                with pe.Fori(0, NB - 1) as b:
                    mlp(l * NB + b, True)
                mlp(l * NB + NB - 1, False)


def _chunks(w):
    k, n = w.shape
    return w.reshape(k // P, P, n).transpose(1, 0, 2)


def _columns(v):
    return v.reshape(-1, P).T


def kernel(**inputs):
    import numpy as np
    import concourse.bacc as _bacc
    from concourse.bass_utils import run_bass_kernel_spmd as _run

    a = {k: np.asarray(v) for k, v in inputs.items()}
    f32 = np.float32
    cols = np.concatenate([
        _chunks(a["L0_attn_conv_w"].reshape(RH, TAPS)).reshape(P, KR * TAPS),
        _columns(a["L0_attn_conv_b"]), _columns(a["L0_attn_b_g"]), _columns(a["L0_attn_forget_base"]),
        _columns(a["L0_xattn_bq"]), _columns(a["L0_xattn_bk"]), _columns(a["L0_xattn_bv"]),
        _columns(a["L0_xattn_b1"])], axis=1)
    rows = np.broadcast_to(np.stack([a["L0_xattn_bo"], a["L0_xattn_gamma"], a["L0_xattn_beta"],
                                     a["L0_xattn_b2"]]), (P, 4, D))

    def hid_columns(v):
        full = np.zeros((KH * P,), f32)
        full[:HID] = v
        return _columns(full)

    lcols = np.stack([np.concatenate([
        _columns(a["L0_ffn_ln_g"][l]), _columns(a["L0_ffn_ln_b"][l]),
        hid_columns(a["L0_ffn_b1"][l][:HID]), hid_columns(a["L0_ffn_b1"][l][HID:])], axis=1)
        for l in range(LAYERS)], axis=1)
    qk_scale = np.broadcast_to(np.stack([a["L0_ffn_q_scale"], a["L0_ffn_k_scale"]], axis=1), (P, LAYERS, 2, DH))
    half = np.arange(0, DH, 2, dtype=f32)
    pos = np.arange(T, dtype=f32)
    inv_freq = (f32(1.0) / f32(10000.0) ** (half / f32(DH))).astype(f32)
    freqs = pos[:, None] * inv_freq[None, :]
    freqs = np.concatenate([freqs, freqs], axis=-1)
    base = (half + f32(0.4 * DH)) / f32(1.4 * DH)
    power = (pos - f32(T // 2)) / f32(P // 2)
    scale = (base[None, :] ** power[:, None]).astype(f32)
    scale = np.concatenate([scale, scale], axis=-1)
    sign = np.concatenate([-np.ones(DH // 2, f32), np.ones(DH // 2, f32)])
    cos, sin = np.cos(freqs), np.sin(freqs) * sign
    rope = np.stack([cos * scale, sin * scale, cos / scale, sin / scale]).astype(f32)
    rope = rope.reshape(4, TT, P, DH).transpose(2, 0, 1, 3)
    w2 = np.zeros((LAYERS, KH * P, D), f32)
    w2[:, :HID] = a["L0_ffn_w2"]
    w2[:, HID] = a["L0_ffn_b2"]
    layer = lambda w: np.stack([_chunks(w[l]) for l in range(LAYERS)])
    named = {
        "x": a["x"], "ctx": a["ctx_1024"], "cols": cols, "rows": rows,
        "w_in": _chunks(a["L0_attn_W_in"].T), "w_gate": _chunks(a["L0_attn_W_g"].T),
        "w_out": _chunks(a["L0_attn_W_out"].T),
        "wq": _chunks(a["L0_xattn_wq"]), "wk": _chunks(a["L0_xattn_wk"]), "wv": _chunks(a["L0_xattn_wv"]),
        "wo_x": _chunks(a["L0_xattn_wo"]), "pos_bias": _chunks(a["L0_xattn_pos_bias"]),
        "w1_x": _chunks(a["L0_xattn_w1"]), "w2_x": _chunks(a["L0_xattn_w2"]),
        "lcols": lcols, "qk_scale": qk_scale, "rope": rope,
        "wqkv": layer(a["L0_ffn_wqkv"]), "wo_l": layer(a["L0_ffn_wo"]), "w1_l": layer(a["L0_ffn_w1"]),
        "w2_l": layer(w2)}
    nc = _bacc.Bacc("TRN2", target_bir_lowering=False, num_devices=1)
    arrays, args = {}, []
    for name, v in named.items():
        v = np.ascontiguousarray(v)
        arrays[f"in_{name}_dram"] = v
        args.append(nc.dram_tensor(f"in_{name}_dram", v.shape, mybir.dt.from_np(v.dtype), kind="ExternalInput").ap())
    args.append(nc.dram_tensor("out_0_dram", (NB, T, D), F32, kind="ExternalOutput").ap())
    build(nc, STAGES, *args)
    r = _run(nc, [arrays], core_ids=[0])
    return r.results[0]["out_0_dram"]


STAGES = 3
```

```python
from contextlib import ExitStack

import concourse.bass as bass
from concourse import mybir

F32 = mybir.dt.float32
F32R = mybir.dt.float32r
ALU = mybir.AluOpType
ACT = mybir.ActivationFunctionType
AX_X = mybir.AxisListType.X

P = 128
NB, T, D = 4, 512, 256
TT = T // P
NT = NB * TT
KD = D // P
RH = 384
KR = RH // P
TAPS = 4
FH = 1024
KF = FH // P
LAYERS, HEADS, DH = 2, 8, 64
INNER = HEADS * DH
KI = INNER // P
HID = 682
KH = 6
HLAST = HID - (KH - 1) * P
WM_PIECES = 3
WM_PIECE = 356
WM_QUARTER = WM_PIECES * WM_PIECE
W1_COLS, W2_COLS = KD * 2 * HID, KH * D
WM_COLS = NB * WM_QUARTER
BAND = 64
QK_SCALE = 8.0
LN_EPS = 1e-5
BETA_EPS = 1e-6
NEG = -1e30

C_CONVW, C_CONVB, C_BG, C_FB = 0, 12, 15, 21
C_BQ, C_BK, C_BV, C_B1 = 24, 26, 28, 30
NCOL = 38
L_G, L_B, L_B1A, L_B1G = 0, 2, 4, 10
NLCOL = 16
R_BO, R_GAMMA, R_BETA, R_B2 = range(4)
TQC, TQS, TKC, TKS = range(4)


def build(nc, stages, x, ctx_in, cols_in, rows_in, w_in, w_gate, w_out, wq, wk, wv, wo_x, pos_bias,
          w1_x, w2_x, lcols_in, qk_scale, rope, wqkv, wo_l, wm_l, out):
    with ExitStack() as ctx:
        def sb(name, shape, dt=F32, stack=ctx):
            return stack.enter_context(nc.sbuf_tensor(name, shape, dt))

        def signals(names):
            return [ctx.enter_context(nc.semaphore(n)) for n in names.split()]

        bank = [ctx.enter_context(nc.psum_tensor(f"bank{i}", [P, 512], F32)) for i in range(8)]

        stream = sb("stream", [P, NT, D])
        cols = sb("cols", [P, NCOL])
        ident = sb("ident", [P, P])
        minus_half = sb("minus_half", [P, 2 * HEADS])
        mask = sb("mask", [P, 2 * P])
        stats = sb("stats", [P, TT, 12])
        mean_var = sb("mean_var", [P, TT, 2])
        var_eps = sb("var_eps", [P, TT])
        rstd = sb("rstd", [P, TT])
        normed = sb("normed", [P, TT, D])
        normed_t = sb("normed_t", [P, KD, T])
        lcols = sb("lcols", [P, LAYERS, NLCOL])

        inner = sb("inner", [P, NT, D])
        w_stage = sb("w_stage", [P, KD * 3 * INNER])
        wo_sb = sb("wo_sb", [P, KI, D])
        qk_scale_sb = sb("qk_scale_sb", [P, LAYERS, 2, DH])
        rope_sb = sb("rope_sb", [P, 4, TT, DH])
        st12 = ExitStack()
        w_q = sb("w_q", [P, KD, D], stack=st12)
        w_k = sb("w_k", [P, KD, D], stack=st12)
        w_v = sb("w_v", [P, KD, D], stack=st12)
        w_o = sb("w_o", [P, KD, D], stack=st12)
        emb = sb("emb", [P, NT, D], stack=st12)
        ew = sb("ew", [P, TT, T], stack=st12)
        ew_t = sb("ew_t", [P, TT, T], stack=st12)
        ek = sb("ek", [P, KD, T], stack=st12)
        ekv = sb("ekv", [P, KD, T], stack=st12)
        eq = sb("eq", [P, KD, T], stack=st12)
        ew_stat = sb("ew_stat", [P, TT, 2], stack=st12)
        minus_bq = sb("minus_bq", [P, KD], stack=st12)
        kstat = sb("kstat", [P, KD, 3], stack=st12)
        w_1 = sb("w_1", [P, KD, FH], stack=st12)
        w_2 = sb("w_2", [P, KF, D], stack=st12)
        rows = sb("rows", [P, 4, D], stack=st12)
        st1 = ExitStack()
        w_in_sb = sb("w_in_sb", [P, KD, 2 * RH], stack=st1)
        w_gate_sb = sb("w_gate_sb", [P, KR, 2 * RH], stack=st1)
        w_out_sb = sb("w_out_sb", [P, KR, D], stack=st1)
        raw = sb("raw", [P, KR, TAPS - 1 + T], stack=st1)
        conv = sb("conv", [P, KR, T], stack=st1)
        gate_act = sb("gate_act", [P, 2, KR, T], stack=st1)
        th_in = sb("th_in", [P, KR, T], stack=st1)
        alpha = sb("alpha", [P, KR, T], stack=st1)
        beta = sb("beta", [P, KR, T], stack=st1)
        scanned = beta
        fb_tmp = sb("fb_tmp", [P, 3, KR], stack=st1)
        m4sp = sb("m4sp", [P, KR], stack=st1)
        half_bf = sb("half_bf", [P, 2 * KR], stack=st1)
        quarter = sb("quarter", [P, 1], stack=st1)
        st1.close()
        st2 = ExitStack()
        ek_tok = sb("ek_tok", [P, TT, D], stack=st2)
        ekv_tok = sb("ekv_tok", [P, TT, D], stack=st2)
        y = sb("y", [P, KD, T], stack=st2)
        mix = sb("mix", [P, TT, D], stack=st2)
        a_tok = sb("a_tok", [P, TT, D], stack=st2)
        a_t = sb("a_t", [P, KD, T], stack=st2)
        a_b2 = sb("a_b2", [P, TT, D], stack=st2)
        ff = sb("ff", [P, KF, T], stack=st2)
        mixed_out = sb("mixed_out", [P, TT, D], stack=st2)
        lstats = sb("lstats", [P, 2, TT, 6], stack=st2)
        lmv = sb("lmv", [P, 2, TT, 2], stack=st2)
        lveps = sb("lveps", [P, 2, TT], stack=st2)
        lrstd = sb("lrstd", [P, 2, TT], stack=st2)
        st2.close()
        st12.close()
        wqkv_hi = sb("wqkv_hi", [P, KD, 3 * INNER], F32R)
        wqkv_lo = sb("wqkv_lo", [P, KD, 3 * INNER], F32R)
        x_hi = sb("x_hi", [P, KD * (T + 1)], F32R)
        x_lo = sb("x_lo", [P, KD * (T + 1)], F32R)
        x_tile = sb("x_tile", [P, 2, D])
        rope_l = sb("rope_l", [P, 4, TT, DH])
        squares = sb("squares", [P, 2, INNER])
        norms = sb("norms", [P, 3, 2 * HEADS])
        q_rnorm = sb("q_rnorm", [P, 4, HEADS])
        row_max = sb("row_max", [P, 2, HEADS])
        row_bias = sb("row_bias", [P, 2, HEADS])
        row_sum = sb("row_sum", [P, 2, HEADS])
        row_rsum = sb("row_rsum", [P, HEADS])
        rot = sb("rot", [P, 4, INNER])
        wm_hi = sb("wm_hi", [P, WM_COLS], F32R)
        last_hi = sb("last_hi", [P, T], F32R)
        last_lo = sb("last_lo", [P, T], F32R)
        q_tok = sb("q_tok", [P, 2, INNER])
        k_tok = sb("k_tok", [P, 2, INNER])
        v_tok = sb("v_tok", [P, TT, INNER])
        q_heads = sb("q_heads", [P, HEADS, P])
        wm_lo = sb("wm_lo", [P, WM_COLS], F32R)
        shifted = sb("shifted", [P, TT, P])
        h_hi = sb("h_hi", [P, KD, T], F32R)
        h_lo = sb("h_lo", [P, KD, T], F32R)
        st_att = ExitStack()
        k_t = sb("k_t", [P, KI, T], stack=st_att)
        scores = sb("scores", [P, 2, 2, 2 * P], stack=st_att)
        probs = sb("probs", [P, 2, 2, 2 * P], stack=st_att)
        probs_t = sb("probs_t", [P, 2, 4, P], stack=st_att)
        o_tok = sb("o_tok", [P, INNER], stack=st_att)
        o_t = sb("o_t", [P, KI, P], stack=st_att)
        st_att.close()
        hidden = sb("hidden", [P, 2, T])
        hidden_hi = sb("hidden_hi", [P, KH - 1, T], F32R)
        hidden_lo = sb("hidden_lo", [P, KH - 1, T], F32R)

        (x0_in, xr_in, col_in, w1s_in, wg_in, wor_in, aft_in, ctx_sem, pos_in, mlp_in, rows_sem) = signals(
            "x0_in xr_in col_in w1s_in wg_in wor_in aft_in ctx_sem pos_in mlp_in rows_sem")
        (pool_ready, fb_step, fb_vec, ready_consts) = signals("pool_ready fb_step fb_vec ready_consts")
        (n_stats, n_aggr, n_eps, n_rstd, n_norm) = signals("n_stats n_aggr n_eps n_rstd n_norm")
        (a_tp, a_tp_out, a_full, a_thf, a_th, a_gelu, a_exp, a_sq, a_beta, a_raw, a_tap0, a_tap, a_conv,
         a_xs0, a_xs, a_scan, a_gh, a_o, a_res) = signals(
            "a_tp a_tp_out a_full a_thf a_th a_gelu a_exp a_sq a_beta a_raw a_tap0 a_tap a_conv "
            "a_xs0 a_xs a_scan a_gh a_o a_res")
        (e_band, e_max, e_neg, e_exp, e_tp, e_tp_out) = signals("e_band e_max e_neg e_exp e_tp e_tp_out")
        (b_emb, b_embo, b_tp, b_tp_out, b_full, b_kmax, b_kbias, b_ek, b_ekv, b_eq, b_tk, b_tk_out, b_aft, b_den,
         b_rec, b_y, b_o, b_mix, b_ta, b_ta_out, b_relu, b_f1, b_ab2, b_f2, b_sum, b_res) = signals(
            "b_emb b_embo b_tp b_tp_out b_full b_kmax b_kbias b_ek b_ekv b_eq b_tk b_tk_out b_aft b_den b_rec "
            "b_y b_o b_mix b_ta b_ta_out b_relu b_f1 b_ab2 b_f2 b_sum b_res")
        (l_stats, l_aggr, l_eps, l_rstd, l_mid, l_out) = signals("l_stats l_aggr l_eps l_rstd l_mid l_out")
        (n_inner, b_x2, out_sum) = signals("n_inner b_x2 out_sum")
        (c_zero, c_tab, c_lcols, c_xs, c_xt, c_xt_out, c_p, c_sq, c_v, c_ss, c_clip, c_rn, c_rq, c_rope, c_add,
         c_kn, c_t, c_kt, c_qe, c_qo, c_qk, c_tt, c_nb, c_ex, c_pt, c_pt_out, c_pv, c_ri, c_on, c_ot, c_ot_out,
         c_wo, c_res) = signals(
            "c_zero c_tab c_lcols c_xs c_xt c_xt_out c_p c_sq c_v c_ss c_clip c_rn c_rq c_rope c_add c_kn c_t "
            "c_kt c_qe c_qo c_qk c_tt c_nb c_ex c_pt c_pt_out c_pv c_ri c_on c_ot c_ot_out c_wo c_res")
        (d_shift, d_stats, d_aggr, d_eps, d_rstd, d_norm, d_tp, d_tp_out, d_w1, d_gelu, d_act, d_w2, d_res0) = signals(
            "d_shift d_stats d_aggr d_eps d_rstd d_norm d_tp d_tp_out d_w1 d_gelu d_act d_w2 d_res0")
        (rope_in, wqkv_in, wo_in, wm_in, wq_hi, wq_lo, wm_copied, wm_split, c_xt_lo, d_full, d_in_hi, d_in_lo,
         d_hi) = signals(
            "rope_in wqkv_in wo_in wm_in wq_hi wq_lo wm_copied wm_split c_xt_lo d_full d_in_hi d_in_lo d_hi")
        (out_sem,) = signals("out_sem")

        C_ZERO = 6
        tiles = lambda b: bass.ts(b, TT) if not isinstance(b, int) else slice(b * TT, (b + 1) * TT)
        block = ctx.enter_context(nc.Block())
        xv = x.rearrange("b (t p) d -> p (b t) d", p=P)
        ov = out.rearrange("b (t p) d -> p (b t) d", p=P)
        cv = ctx_in.rearrange("b (t p) d -> p (b t) d", p=P)

        def wait_alone(engine, sem, value):
            engine.wait_ge(sem, value)
            if not isinstance(value, int):
                engine.nop(nofuse=True)

        @block.sync
        def _(sp):
            sp.dma_start(stream[:, 0:TT, :], xv[:, 0:TT, :]).then_inc(x0_in, 16)
            sp.dma_start(cols[:, :], cols_in).then_inc(col_in, 16)
            sp.dma_start(w_in_sb[:, :, :], w_in).then_inc(w1s_in, 16)
            sp.dma_start(w_gate_sb[:, :, :], w_gate).then_inc(wg_in, 16)
            sp.dma_start(stream[:, TT:NT, :], xv[:, TT:NT, :]).then_inc(xr_in, 16)
            sp.dma_start(w_out_sb[:, :, :], w_out).then_inc(wor_in, 16)
            sp.dma_start(ew[:, :, :], pos_bias).then_inc(pos_in, 16)
            sp.dma_start(emb[:, :, :], cv).then_inc(ctx_sem, 16)
            for n, (w, src) in enumerate(((w_k, wk), (w_v, wv), (w_q, wq), (w_o, wo_x))):
                sp.dma_start(w[:, :, :], src).then_inc(aft_in, 16)
            sp.dma_start(rows[:, :, :], rows_in).then_inc(rows_sem, 16)
            sp.dma_start(w_1[:, :, :], w1_x).then_inc(mlp_in, 16)
            sp.dma_start(w_2[:, :, :], w2_x).then_inc(mlp_in, 16)
            sp.dma_start(rope_sb[:, :, :, :], rope).then_inc(rope_in, 16)
            sp.dma_start(qk_scale_sb[:, :, :, :], qk_scale).then_inc(rope_in, 16)
            sp.dma_start(lcols[:, :, :], lcols_in).then_inc(rope_in, 16)

            def load_att(l):
                sp.dma_start(w_stage[:, :], wqkv[l].rearrange("p k n -> p (k n)")).then_inc(wqkv_in, 16)
                if l:
                    sp.wait_ge(c_wo, l * NT)
                sp.dma_start(wo_sb[:, :, :], wo_l[l]).then_inc(wo_in, 16)

            def load_mlp(l, b):
                sp.dma_start(w_stage[:, 0:WM_QUARTER], wm_l[l, :, b * WM_QUARTER:(b + 1) * WM_QUARTER])\
                    .then_inc(wm_in, 16)

            def shift(l, b):
                m = l * NB + b
                sp.wait_ge(c_res, l * NT + b * TT + TT)
                sp.wait_ge(d_norm, 8 * m)
                sp.dma_start(shifted[1:P, :, :], inner[0:P - 1, b * TT:(b + 1) * TT, P:D]).then_inc(d_shift, 16)
                sp.dma_start(shifted[0:1, 1:TT, :], inner[P - 1:P, b * TT:(b + 1) * TT - 1, P:D]).then_inc(d_shift, 16)

            load_att(0)
            for l in range(LAYERS):
                sp.wait_ge(wq_lo, 2 * 3 * (l + 1))
                for b in range(NB):
                    if b:
                        sp.wait_ge(wm_split, WM_PIECES * (l * NB + b))
                    load_mlp(l, b)
                shift(l, 0)
                if l < LAYERS - 1:
                    sp.wait_ge(wm_split, WM_PIECES * NB * (l + 1))
                    load_att(l + 1)
                for b in range(1, NB):
                    shift(l, b)
            for b in range(NB):
                sp.wait_ge(out_sum, b + 1)
                sp.dma_start(ov[:, b * TT:(b + 1) * TT, :], stream[:, b * TT:(b + 1) * TT, :]).then_inc(out_sem, 16)
            sp.wait_ge(out_sem, 16 * NB)

        @block.gpsimd
        def _(pool):
            pool.memset(ident[:, :], 0.0).then_inc(pool_ready, 1)
            pool.memset(minus_half[:, :], -0.5).then_inc(pool_ready, 1)
            pool.memset(raw[:, :, 0:TAPS - 1], 0.0).then_inc(pool_ready, 1)
            pool.memset(mask[:, :], 0.0).then_inc(pool_ready, 1)
            pool.memset(quarter[:, :], 0.25 * (1.0 + BETA_EPS)).then_inc(pool_ready, 1)
            pool.wait_ge(pool_ready, 5)
            pool.affine_select(out=ident[:, :], in_=ident[:, :], compare_op=ALU.not_equal, fill=1.0, base=0,
                               pattern=[[-1, P]], channel_multiplier=1).then_inc(ready_consts, 1)
            pool.affine_select(out=mask[:, :], in_=mask[:, :], compare_op=ALU.is_ge, fill=NEG, base=P,
                               pattern=[[-1, 2 * P]], channel_multiplier=1).then_inc(pool_ready, 1)
            pool.wait_ge(pool_ready, 6)
            pool.affine_select(out=mask[:, :], in_=mask[:, :], compare_op=ALU.is_ge, fill=NEG, base=0,
                               pattern=[[1, 2 * P]], channel_multiplier=-1).then_inc(ready_consts, 1)

            def rstd_of(n):
                wait_alone(pool, n_aggr, 4 * n + 4)
                pool.tensor_scalar(var_eps[:, :], mean_var[:, :, 1], 1.0, LN_EPS, ALU.mult, ALU.add)\
                    .then_inc(n_eps, 1)
                pool.wait_ge(n_eps, n + 1)
                pool.tensor_tensor(rstd[:, :], var_eps[:, :], minus_half[:, 0:TT], ALU.pow).then_inc(n_rstd, 1)

            rstd_of(0)
            pool.wait_ge(pos_in, 16)
            for n, (step, ch) in enumerate(((P, 1), (-P, -1))):
                pool.wait_ge(e_band, n)
                pool.affine_select(out=ew[:, :, :], in_=ew[:, :, :], compare_op=ALU.is_ge, fill=0.0,
                                   base=BAND - 1, pattern=[[step, TT], [-ch, T]], channel_multiplier=ch)\
                    .then_inc(e_band, 1)
            with pool.Fori(0, NB - 1) as b:
                rstd_of(b + 1)

            def keep_emb(b):
                pool.wait_ge(b_emb, b + 1)
                pool.tensor_tensor(emb[:, tiles(b), :], normed[:, :, :],
                                   rows[:, R_BO:R_BO + 1, :].to_broadcast([P, TT, D]), ALU.add)\
                    .then_inc(b_embo, 1)

            def rstd_affine(i, s):
                wait_alone(pool, l_aggr, 4 * i + 4)
                pool.tensor_scalar(lveps[:, s, :], lmv[:, s, :, 1], 1.0, LN_EPS, ALU.mult, ALU.add)\
                    .then_inc(l_eps, 1)
                pool.wait_ge(l_eps, i + 1)
                pool.tensor_tensor(lrstd[:, s, :], lveps[:, s, :], minus_half[:, 0:TT], ALU.pow).then_inc(l_rstd, 1)

            def add_b2(b):
                pool.wait_ge(l_out, 8 * b + 4)
                pool.wait_ge(l_mid, 8 * b)
                pool.tensor_tensor(a_b2[:, :, :], a_tok[:, :, :],
                                   rows[:, R_B2:R_B2 + 1, :].to_broadcast([P, TT, D]), ALU.add).then_inc(b_ab2, 1)

            def add_out(b):
                pool.wait_ge(l_out, 8 * b + 8)
                pool.tensor_tensor(stream[:, tiles(b), :], stream[:, tiles(b), :], mixed_out[:, :, :], ALU.add)\
                    .then_inc(b_x2, 1)

            pool.wait_ge(rows_sem, 16)
            rstd_of(NB)
            keep_emb(0)
            rstd_of(NB + 1)
            keep_emb(1)
            rstd_affine(0, 0)
            add_b2(0)

            def finish(b, nxt, norm2):
                if norm2:
                    rstd_of(2 * b + NB + 2)
                    keep_emb(b + 2)
                rstd_affine(2 * b + 1, 1)
                if nxt:
                    rstd_affine(2 * b + 2, 0)
                add_out(b)
                if nxt:
                    add_b2(b + 1)
                rstd_of(2 * b + NB + 3 if norm2 else b + 2 * NB)

            with pool.Fori(0, NB - 2) as b:
                finish(b, True, True)
            finish(NB - 2, True, False)

            def copy_tile(n, tile, par, batch_done):
                pool.wait_ge(b_res, batch_done)
                if not (isinstance(n, int) and n < 2):
                    wait_alone(pool, c_xt, n - 1)
                pool.tensor_copy(x_tile[:, par, :], inner[:, tile, :]).then_inc(c_xs, 1)

            def rotate(n, par):
                for i, dst in enumerate((q_tok, k_tok)):
                    pool.wait_ge(c_rope, 6 * n + 3 * i + 3)
                    if not (isinstance(n, int) and n < 2):
                        pool.wait_ge(c_t, 2 * n - 2)
                    pool.tensor_tensor(dst[:, par, :], rot[:, 2 * i, :], rot[:, 2 * i + 1, :], ALU.add)\
                        .then_inc(c_add, 1)

            def rnorm(n, w):
                pool.wait_ge(c_ss, n + 1)
                if not (isinstance(n, int) and n == 0):
                    wait_alone(pool, c_kn, n)
                pool.tensor_scalar(norms[:, 1, :], norms[:, 0, :], 1e-24, 1.0, ALU.max, ALU.mult).then_inc(c_clip, 1)
                pool.wait_ge(c_clip, n + 1)
                pool.tensor_tensor(norms[:, 2, :], norms[:, 1, :], minus_half[:, :], ALU.pow).then_inc(c_rn, 1)
                wait_alone(pool, c_rn, n + 1)
                pool.tensor_scalar(q_rnorm[:, w, :], norms[:, 2, 0:HEADS], QK_SCALE, 0.0, ALU.mult, ALU.add)\
                    .then_inc(c_rq, 1)

            def split_mlp_weights(l, b, piece):
                m = l * NB + b
                src = w_stage[:, piece * WM_PIECE:(piece + 1) * WM_PIECE]
                dst = bass.ds(b * WM_QUARTER + piece * WM_PIECE, WM_PIECE)
                wait_alone(pool, wm_in, 16 * m + 16)
                pool.tensor_copy(wm_hi[:, dst], src).then_inc(wm_copied, 1)
                pool.wait_ge(wm_copied, WM_PIECES * m + piece + 1)
                pool.tensor_tensor(wm_lo[:, dst], src, wm_hi[:, dst].bitcast(F32), ALU.subtract)\
                    .then_inc(wm_split, 1)

            def attention(n0, b, l, nxt):
                for w in range(TT):
                    if w == 0 or nxt:
                        copy_tile(n0 + w + 3, (b + (w + 3) // TT) * TT + (w + 3) % TT, (w + 3) % 2,
                                  l * NB + b + (w + 3) // TT + 1)
                    if w < 2 or nxt:
                        rotate(n0 + w + 2, w % 2)
                        rnorm(n0 + w + 2, (w + 2) % TT)
                    if w:
                        split_mlp_weights(l, b, w - 1)

            def mlp_rstd(m):
                wait_alone(pool, d_aggr, 4 * m + 4)
                pool.tensor_scalar(var_eps[:, :], mean_var[:, :, 1], 1.0, LN_EPS, ALU.mult, ALU.add)\
                    .then_inc(d_eps, 1)
                pool.wait_ge(d_eps, m + 1)
                pool.tensor_tensor(rstd[:, :], var_eps[:, :], minus_half[:, 0:TT], ALU.pow).then_inc(d_rstd, 1)

            pool.wait_ge(b_ta, KD * NB)
            pool.memset(x_hi[:, T:T + 1].bitcast(F32), 0.0).then_inc(c_zero, 1)
            pool.memset(x_lo[:, T:T + 1].bitcast(F32), 0.0).then_inc(c_zero, 1)
            copy_tile(0, 0, 0, 1)
            copy_tile(1, 1, 1, 1)
            rotate(0, 0)
            rnorm(0, 0)
            finish(NB - 1, False, False)
            pool.wait_ge(b_res, NB)
            pool.memset(q_heads[:, :, :], 0.0).then_inc(c_zero, 1)
            pool.wait_ge(c_zero, 3)
            pool.memset(last_hi[32:64, :].bitcast(F32), 1.0).then_inc(c_zero, 1)
            pool.wait_ge(c_zero, 4)
            pool.memset(last_lo[32:64, :].bitcast(F32), 0.0).then_inc(c_zero, 1)
            pool.wait_ge(c_zero, 5)
            pool.memset(shifted[0:1, 0, :], 0.0).then_inc(c_zero, 1)
            pool.wait_ge(c_zero, 6)
            for l in range(LAYERS):
                n0 = l * NT
                copy_tile(n0 + 2, 2, 0, l * NB + 1)
                rotate(n0 + 1, 1)
                rnorm(n0 + 1, 1)
                with pool.Fori(0, NB - 1) as b:
                    attention(n0 + b * TT, b, l, True)
                attention(n0 + (NB - 1) * TT, NB - 1, l, False)
                mlp_rstd(l * NB)
                with pool.Fori(0, NB - 1) as b:
                    mlp_rstd(l * NB + b + 1)
                if l < LAYERS - 1:
                    for w in range(2):
                        copy_tile(n0 + NT + w, w, w, (l + 1) * NB + 1)
                    rotate(n0 + NT, 0)
                    rnorm(n0 + NT, 0)
            for b in range(NB):
                pool.wait_ge(b_res, NB * LAYERS + b + 1)
                pool.tensor_tensor(stream[:, tiles(b), :], stream[:, tiles(b), :], inner[:, tiles(b), :], ALU.add)\
                    .then_inc(out_sum, 1)

        @block.vector
        def _(dve):
            def norm(n, b, to_inner=False):
                for t in range(TT):
                    dve.bn_stats(stats[:, t, 0:6], stream[:, b * TT + t, :]).then_inc(n_stats, 1)
                for t in range(TT):
                    wait_alone(dve, n_stats, 4 * n + t + 1)
                    dve.bn_aggr(mean_var[:, t, :], stats[:, t, 0:6]).then_inc(n_aggr, 1)
                dve.wait_ge(n_rstd, n + 1)
                for t in range(TT):
                    dst = inner[:, b * TT + t, :] if to_inner else normed[:, t, :]
                    done = n_norm if not to_inner else n_inner if t < TT - 1 else b_res
                    dve.tensor_scalar(dst, stream[:, b * TT + t, :], mean_var[:, t, 0:1],
                                      rstd[:, t:t + 1], ALU.subtract, ALU.mult).then_inc(done, 1)

            def conv_taps(b):
                for j in range(KR):
                    dve.wait_ge(a_tap0, 3 * b + j + 1)
                    for k in range(1, TAPS):
                        ins = dve.scalar_tensor_tensor(
                            conv[:, j, :], raw[:, j, TAPS - 1 - k:TAPS - 1 - k + T],
                            cols[:, C_CONVW + TAPS * j + TAPS - 1 - k:C_CONVW + TAPS * j + TAPS - k],
                            conv[:, j, :], ALU.mult, ALU.add)
                        if k < TAPS - 1:
                            ins.then_inc(a_tap, 1)
                            dve.wait_ge(a_tap, 6 * b + 2 * j + k)
                        else:
                            ins.then_inc(a_conv, 1)

            def recurrence(b):
                for j in range(KR):
                    dve.wait_ge(a_th, 3 * b + j + 1)
                    dve.scalar_tensor_tensor(th_in[:, j, :], th_in[:, j, :], 1.0, conv[:, j, :], ALU.add,
                                             ALU.mult).then_inc(a_xs0, 1)
                dve.wait_ge(a_beta, b + 1)
                for j in range(KR):
                    dve.wait_ge(a_xs0, 3 * b + j + 1)
                    dve.tensor_tensor(th_in[:, j, :], th_in[:, j, :], beta[:, j, :], ALU.mult).then_inc(a_xs, 1)
                for j in range(KR):
                    dve.wait_ge(a_xs, 3 * b + j + 1)
                    dve.tensor_tensor_scan(scanned[:, j, :], alpha[:, j, :], th_in[:, j, :], 0.0, ALU.mult,
                                           ALU.add).then_inc(a_scan, 1)
                dve.wait_ge(a_gelu, 3 * b + 3)
                for j in range(KR):
                    dve.wait_ge(a_scan, 3 * b + j + 1)
                    dve.tensor_tensor(scanned[:, j, :], scanned[:, j, :], gate_act[:, b % 2, j, :], ALU.mult)\
                        .then_inc(a_gh, 1)

            def residual(b):
                for h in range(2):
                    dve.wait_ge(a_o, 2 * b + h + 1)
                    t = slice(0, 2)
                    s = stream[:, bass.ds(b * TT + 2 * h, 2), :]
                    dve.tensor_tensor(s, s, bank[6 + h][:, :].rearrange("p (t d) -> p t d", t=2), ALU.add)\
                        .then_inc(a_res, 1)

            def embed(b, n):
                dve.wait_ge(a_res, 2 * b + 2)
                if isinstance(b, int) and b == 0:
                    dve.wait_ge(a_tp, 2 * NB)
                else:
                    dve.wait_ge(b_tp, 2 * b)
                    dve.wait_ge(b_embo, b)
                norm(n, b)
                dve.wait_ge(n_norm, 4 * (NB + b) + 4)
                dve.tensor_tensor(normed[:, :, :], normed[:, :, :], emb[:, tiles(b), :], ALU.add).then_inc(b_emb, 1)

            def keys_values(b):
                for m in range(KD):
                    dve.wait_ge(b_full, 6 * b + m + 1)
                    dve.tensor_reduce(kstat[:, m, 0:1], bank[2 + m][:, :], AX_X, ALU.max).then_inc(b_kmax, 1)
                for m in range(KD):
                    bk = cols[:, C_BK + m:C_BK + m + 1]
                    dve.wait_ge(b_kmax, 4 * b + m + 1)
                    dve.tensor_scalar(kstat[:, m, 1:2], kstat[:, m, 0:1], bk, -1.0, ALU.add, ALU.mult)\
                        .then_inc(b_kmax, 1)
                for m in range(KD):
                    dve.wait_ge(b_kmax, 4 * b + 2 + m + 1)
                    dve.tensor_scalar(kstat[:, m, 2:3], kstat[:, m, 1:2], cols[:, C_BK + m:C_BK + m + 1], None,
                                      ALU.add).then_inc(b_kbias, 1)
                for m in range(KD):
                    dve.wait_ge(b_full, 6 * b + 2 + m + 1)
                    dve.wait_ge(b_ek, 2 * b + m + 1)
                    dve.scalar_tensor_tensor(ekv[:, m, :], bank[4 + m][:, :], cols[:, C_BV + m:C_BV + m + 1],
                                             ek[:, m, :], ALU.add, ALU.mult).then_inc(b_ekv, 1)

            def gated_ratio(b):
                for m in range(KD):
                    den, num = bank[2 + (2 * m + 2) % 4], bank[2 + (2 * m + 3) % 4]
                    dve.wait_ge(b_aft, 4 * b + 2 * m + 1)
                    dve.scalar_tensor_tensor(y[:, m, :], eq[:, m, :], 1.0, den[:, :], ALU.add, ALU.mult)\
                        .then_inc(b_den, 1)
                    dve.wait_ge(b_den, 2 * b + m + 1)
                    dve.reciprocal(y[:, m, :], y[:, m, :]).then_inc(b_rec, 1)
                    dve.wait_ge(b_rec, 2 * b + m + 1)
                    dve.wait_ge(b_aft, 4 * b + 2 * m + 2)
                    dve.tensor_tensor(y[:, m, :], y[:, m, :], num[:, :], ALU.mult).then_inc(b_y, 1)

            def lstat(i, s, src, done, of):
                for t in range(TT):
                    dve.wait_ge(done, of + t // 2 + 1)
                    dve.bn_stats(lstats[:, s, t, :], src[:, t, :]).then_inc(l_stats, 1)
                for t in range(TT):
                    wait_alone(dve, l_stats, 4 * i + t + 1)
                    dve.bn_aggr(lmv[:, s, t, :], lstats[:, s, t, :]).then_inc(l_aggr, 1)

            def norm_affine(i, s, src, dst):
                for t in range(TT):
                    dve.wait_ge(l_aggr, 4 * i + t + 1)
                    dve.scalar_tensor_tensor(src[:, t, :], src[:, t, :], lmv[:, s, t, 0:1], rows[:, R_GAMMA, :],
                                             ALU.subtract, ALU.mult).then_inc(l_mid, 1)
                dve.wait_ge(l_rstd, i + 1)
                for t in range(TT):
                    dve.wait_ge(l_mid, 4 * i + t + 1)
                    dve.scalar_tensor_tensor(dst[:, t, :], src[:, t, :], lrstd[:, s, t:t + 1], rows[:, R_BETA, :],
                                             ALU.mult, ALU.add).then_inc(l_out, 1)

            def mixed(b):
                dve.wait_ge(b_embo, b + 1)
                for h in range(2):
                    dve.wait_ge(b_o, 2 * b + h + 1)
                    dve.tensor_tensor(mix[:, 2 * h:2 * h + 2, :], emb[:, bass.ds(b * TT + 2 * h, 2), :],
                                      bank[6 + h][:, :].rearrange("p (t d) -> p t d", t=2), ALU.add)\
                        .then_inc(b_mix, 1)
                lstat(2 * b, 0, mix, b_mix, 2 * b)

            def to_a(b):
                dve.wait_ge(b_ab2, b)
                dve.wait_ge(b_ta, 2 * b)
                norm_affine(2 * b, 0, mix, a_tok)

            def add_mlp(b, h):
                dve.wait_ge(b_f2, 2 * b + h + 1)
                dve.tensor_tensor(a_b2[:, 2 * h:2 * h + 2, :], a_b2[:, 2 * h:2 * h + 2, :],
                                  bank[6 + h][:, :].rearrange("p (t d) -> p t d", t=2), ALU.add)\
                    .then_inc(b_sum, 1)

            def mlp_sum(b):
                dve.wait_ge(b_ab2, b + 1)
                for h in range(2):
                    add_mlp(b, h)
                lstat(2 * b + 1, 1, a_b2, b_sum, 2 * b)

            dve.wait_ge(x0_in, 16)
            dve.wait_ge(ready_consts, 2)
            norm(0, 0)
            dve.wait_ge(col_in, 16)
            dve.tensor_scalar(fb_tmp[:, 2, :], cols[:, C_FB:C_FB + KR], 0.0, None, ALU.max).then_inc(fb_vec, 1)
            dve.tensor_scalar(half_bf[:, :], cols[:, C_BG:C_BG + 2 * KR], 0.5, None, ALU.mult).then_inc(fb_vec, 1)
            dve.wait_ge(fb_step, 3)
            dve.wait_ge(fb_vec, 1)
            dve.tensor_tensor(fb_tmp[:, 2, :], fb_tmp[:, 2, :], fb_tmp[:, 0, :], ALU.add).then_inc(fb_vec, 1)
            dve.wait_ge(fb_vec, 3)
            dve.tensor_scalar(m4sp[:, :], fb_tmp[:, 2, :], -4.0, None, ALU.mult).then_inc(fb_vec, 1)
            conv_taps(0)
            dve.wait_ge(xr_in, 16)
            with dve.Fori(0, NB - 1) as b:
                dve.wait_ge(a_tp, 2 * b + 2)
                norm(b + 1, b + 1)
                recurrence(b)
                conv_taps(b + 1)
                residual(b)
            dve.wait_ge(e_band, 2)
            dve.tensor_reduce(ew_stat[:, :, 0], ew[:, :, :], AX_X, ALU.max).then_inc(e_max, 1)
            dve.wait_ge(e_max, 1)
            dve.tensor_scalar(ew_stat[:, :, 1], ew_stat[:, :, 0], -1.0, None, ALU.mult).then_inc(e_neg, 1)
            dve.wait_ge(ctx_sem, 16)
            embed(0, NB)
            recurrence(NB - 1)
            keys_values(0)
            residual(NB - 1)
            embed(1, NB + 1)
            dve.wait_ge(rows_sem, 16)
            gated_ratio(0)
            mixed(0)
            to_a(0)

            def mixing(b, nxt, norm2):
                if nxt:
                    keys_values(b + 1)
                if norm2:
                    embed(b + 2, 2 * b + NB + 2)
                if nxt:
                    gated_ratio(b + 1)
                mlp_sum(b)
                if nxt:
                    mixed(b + 1)
                dve.wait_ge(b_x2, b)
                norm_affine(2 * b + 1, 1, a_b2, mixed_out)
                if nxt:
                    to_a(b + 1)
                dve.wait_ge(b_x2, b + 1)
                norm(2 * b + NB + 3 if norm2 else b + 2 * NB, b, to_inner=True)

            with dve.Fori(0, NB - 2) as b:
                mixing(b, True, True)
            mixing(NB - 2, True, False)

            def tables(l):
                for i in range(4):
                    s = qk_scale_sb[:, l, i // 2, :].unsqueeze(1)
                    src = rope_sb[:, i, :, :]
                    dst = rope_l[:, i, :, :]
                    if i % 2:
                        for lo, other in ((0, DH // 2), (DH // 2, 0)):
                            dve.tensor_tensor(dst[:, :, lo:lo + DH // 2], src[:, :, lo:lo + DH // 2],
                                              s[:, :, other:other + DH // 2].to_broadcast([P, TT, DH // 2]),
                                              ALU.mult).then_inc(c_tab, 1)
                    else:
                        dve.tensor_tensor(dst, src, s.to_broadcast([P, TT, DH]), ALU.mult).then_inc(c_tab, 1)

            def rope_products(n, w, i):
                src = bank[i][:, :].rearrange("p (h d) -> p h d", d=DH)
                dve.wait_ge(c_sq, 2 * n + i + 1)
                if not (isinstance(n, int) and n == 0):
                    dve.wait_ge(c_add, 2 * n - 1 + i)
                cos = rope_l[:, 2 * i, w:w + 1, :].to_broadcast([P, HEADS, DH])
                dve.tensor_tensor(rot[:, 2 * i, :].rearrange("p (h d) -> p h d", d=DH), src, cos, ALU.mult)\
                    .then_inc(c_rope, 1)
                rotated = rot[:, 2 * i + 1, :].rearrange("p (h d) -> p h d", d=DH)
                for lo, other in ((0, DH // 2), (DH // 2, 0)):
                    sin = rope_l[:, 2 * i + 1, w:w + 1, lo:lo + DH // 2].to_broadcast([P, HEADS, DH // 2])
                    dve.tensor_tensor(rotated[:, :, lo:lo + DH // 2], src[:, :, other:other + DH // 2], sin,
                                      ALU.mult).then_inc(c_rope, 1)

            def sum_squares(n):
                dve.wait_ge(c_sq, 2 * n + 2)
                dve.wait_ge(c_clip, n)
                dve.tensor_reduce(norms[:, 0, :], squares[:, :, :].rearrange("p i (h d) -> p (i h) d", d=DH), AX_X,
                                  ALU.add).then_inc(c_ss, 1)

            def norm_keys(n, par):
                dve.wait_ge(c_add, 2 * n + 2)
                dve.wait_ge(c_rn, n + 1)
                k = k_tok[:, par, :].rearrange("p (h d) -> p h d", d=DH)
                dve.tensor_tensor(k, k, norms[:, 2, HEADS:2 * HEADS].unsqueeze(2).to_broadcast([P, HEADS, DH]),
                                  ALU.mult).then_inc(c_kn, 1)

            def q_odd(n):
                dve.wait_ge(c_t, 2 * n + 2)
                dve.tensor_copy(q_heads[64:128, :, :].rearrange("p (c e) t -> p e c t", e=2)[:, 1, :, :],
                                bank[2][64:128, :].rearrange("p (c t) -> p c t", t=P)).then_inc(c_qo, 1)

            def masked(n, w, i, first=False):
                u = 4 * n + i
                nk = 2 * P if w else P
                if w or i >= 2:
                    dve.wait_ge(c_ex, 2 * u - 2)
                wait_alone(dve, c_qk, u + 1)
                for e in range(2):
                    dve.tensor_tensor_reduce(scores[:, i % 2, e, 0:nk], bank[6 + i % 2][:, e * 2 * P:e * 2 * P + nk],
                                             mask[:, 2 * P - nk:2 * P], 1.0, NEG, ALU.add, ALU.max,
                                             row_max[:, w % 2, 2 * i + e:2 * i + e + 1]).then_inc(c_tt, 1)
                dve.wait_ge(c_tt, 2 * u + 2)
                dve.wait_ge(c_rq, n + 1)
                dve.scalar_tensor_tensor(row_bias[:, w % 2, 2 * i:2 * i + 2], row_max[:, w % 2, 2 * i:2 * i + 2],
                                         -1.0, q_rnorm[:, w, 2 * i:2 * i + 2], ALU.mult, ALU.mult).then_inc(c_nb, 1)

            def normalise(n, w):
                dve.wait_ge(c_ex, 8 * n + 8)
                dve.reciprocal(row_rsum[:, :], row_sum[:, w % 2, :]).then_inc(c_ri, 1)
                dve.wait_ge(c_ri, n + 1)
                dve.wait_ge(c_pv, 4 * n + 4)
                dve.tensor_tensor(o_tok[:, :].rearrange("p (h d) -> p h d", d=DH),
                                  bank[3][:, :].rearrange("p (h d) -> p h d", d=DH),
                                  row_rsum[:, :].unsqueeze(2).to_broadcast([P, HEADS, DH]), ALU.mult)\
                    .then_inc(c_on, 1)

            def o_transposed(n):
                dve.wait_ge(c_ot, n + 1)
                dve.tensor_copy(o_t[:, :, :].rearrange("p c t -> p (c t)"), bank[2][:, :]).then_inc(c_ot_out, 1)

            def att_residual(n, tile):
                dve.wait_ge(c_wo, n + 1)
                dve.tensor_tensor(inner[:, tile, :], inner[:, tile, :], bank[2][:, 0:D], ALU.add).then_inc(c_res, 1)

            def attention(n0, b, l, nxt):
                for w in range(TT):
                    n = n0 + w
                    two, one = (w < 2 or nxt), (w < 3 or nxt)
                    masked(n, w, 0)
                    masked(n, w, 1)
                    if w:
                        o_transposed(n - 1)
                    if not two:
                        if w == 2:
                            mlp_stats(l * NB, 0, 0)
                            mlp_stats(l * NB, 0, 1)
                        else:
                            mlp_aggr(l * NB)
                    if one:
                        norm_keys(n + 1, (w + 1) % 2)
                    if two:
                        rope_products(n + 2, (w + 2) % TT, 0)
                    masked(n, w, 2)
                    if two:
                        rope_products(n + 2, (w + 2) % TT, 1)
                    if w:
                        att_residual(n - 1, b * TT + w - 1)
                    if not two and w == 2:
                        mlp_stats(l * NB, 0, 2)
                        mlp_stats(l * NB, 0, 3)
                    masked(n, w, 3)
                    if not two and w == 3:
                        mlp_norm(l * NB, 0)
                    if w < 1 or nxt:
                        x_low(n + 3, (w + 3) % TT, bank[1][:, 0:D])
                    if two:
                        sum_squares(n + 2)
                    if one:
                        q_odd(n + 1)
                    normalise(n, w)
                    if not two and w == 3:
                        input_low(l * NB)
                    if w == TT - 1:
                        o_transposed(n)
                        att_residual(n, b * TT + w)

            def x_low(n, w, src):
                dve.wait_ge(c_xt_out, n + 1)
                columns = slice(w * P, (w + 1) * P)
                dve.tensor_tensor(x_lo[:, :].rearrange("p (c t) -> p c t", t=T + 1)[:, :, columns],
                                  src.rearrange("p (c t) -> p c t", t=P),
                                  x_hi[:, :].bitcast(F32).rearrange("p (c t) -> p c t", t=T + 1)[:, :, columns],
                                  ALU.subtract).then_inc(c_xt_lo, 1)

            def mlp_stats(m, b, t):
                dve.wait_ge(d_shift, 32 * m + 32)
                for i, src in enumerate((inner[:, b * TT + t, 0:P], shifted[:, t, :])):
                    dve.bn_stats(stats[:, t, 6 * i:6 * i + 6], src).then_inc(d_stats, 1)

            def mlp_aggr(m):
                for t in range(TT):
                    wait_alone(dve, d_stats, 8 * m + 2 * t + 2)
                    dve.bn_aggr(mean_var[:, t, :], stats[:, t, :]).then_inc(d_aggr, 1)

            def mlp_norm(m, b):
                dve.wait_ge(d_rstd, m + 1)
                dve.wait_ge(d_tp, 2 * m)
                for t in range(TT):
                    for i, src in enumerate((inner[:, b * TT + t, 0:P], shifted[:, t, :])):
                        dve.tensor_scalar(normed[:, t, i * P:(i + 1) * P], src, mean_var[:, t, 0:1],
                                          rstd[:, t:t + 1], ALU.subtract, ALU.mult).then_inc(d_norm, 1)

            def input_low(m):
                for c in range(KD):
                    dve.wait_ge(d_in_hi, 2 * m + c + 1)
                    dve.tensor_tensor(h_lo[:, c, :], normed_t[:, c, :], h_hi[:, c, :].bitcast(F32), ALU.subtract)\
                        .then_inc(d_in_lo, 1)

            def split_qkv(l, i):
                for k in range(KD):
                    part = slice(i * INNER, (i + 1) * INNER)
                    dve.wait_ge(wq_hi, 6 * l + 2 * i + k + 1)
                    dve.tensor_tensor(wqkv_lo[:, k, part], w_stage[:, :].rearrange("p (k n) -> p k n", k=KD)[:, k, part],
                                      wqkv_hi[:, k, part].bitcast(F32), ALU.subtract).then_inc(wq_lo, 1)

            def ahead(l, step):
                n0 = l * NT
                if step == 0:
                    tables(l)
                elif step == 1:
                    split_qkv(l, 0)
                elif step == 2:
                    split_qkv(l, 1)
                    for w in range(2):
                        x_low(n0 + w, w, bank[w][:, 0:D])
                elif step == 3:
                    split_qkv(l, 2)
                elif step == 4:
                    dve.wait_ge(c_tab, 6 * l + 6)
                    rope_products(n0, 0, 0)
                elif step == 5:
                    rope_products(n0, 0, 1)
                    sum_squares(n0)
                elif step == 6:
                    norm_keys(n0, 0)
                    rope_products(n0 + 1, 1, 0)
                elif step == 7:
                    rope_products(n0 + 1, 1, 1)
                    sum_squares(n0 + 1)
                else:
                    q_odd(n0)
                    x_low(n0 + 2, 2, bank[1][:, 0:D])

            def mlp(m, b, l, nxt):
                def low(j):
                    r = P if j < KH - 1 else HLAST
                    hi, lo = (hidden_hi[:, j, :], hidden_lo[:, j, :]) if j < KH - 1 else (last_hi, last_lo)
                    dve.wait_ge(d_hi, KH * m + j + 1)
                    dve.tensor_tensor(lo[0:r, :], hidden[0:r, j % 2, :], hi[0:r, :].bitcast(F32), ALU.subtract)\
                        .then_inc(d_act, 1)

                for j in range(KH):
                    r = P if j < KH - 1 else HLAST
                    dve.wait_ge(d_w1, 2 * (KH * m + j) + 2)
                    dve.wait_ge(d_gelu, KH * m + j + 1)
                    dve.scalar_tensor_tensor(hidden[0:r, j % 2, :], bank[3 + 2 * (j % 2)][0:r, :],
                                             lcols[0:r, l, L_B1A + j:L_B1A + j + 1], hidden[0:r, j % 2, :], ALU.add,
                                             ALU.mult).then_inc(d_full, 1)
                    if j:
                        low(j - 1)
                    if nxt:
                        if j < TT:
                            mlp_stats(m + 1, b + 1, j)
                        if j == TT:
                            mlp_aggr(m + 1)
                    elif l < LAYERS - 1 and j < 4:
                        ahead(l + 1, j)
                low(KH - 1)
                if nxt:
                    mlp_norm(m + 1, b + 1)
                    input_low(m + 1)
                elif l < LAYERS - 1:
                    ahead(l + 1, 4)
                    ahead(l + 1, 5)
                for h in range(2):
                    if h and not nxt and l < LAYERS - 1:
                        ahead(l + 1, 6)
                    dve.wait_ge(d_w2, TT * m + 2 * h + 2)
                    s = inner[:, bass.ds(b * TT + 2 * h, 2), :]
                    dve.tensor_tensor(s, s, bank[6 + h][:, :].rearrange("p (t d) -> p t d", t=2), ALU.add)\
                        .then_inc((d_res0, b_res)[h], 1)

            dve.wait_ge(rope_in, 48)
            dve.wait_ge(b_ta, KD * NB)
            for step in range(4):
                ahead(0, step)
            dve.wait_ge(b_ab2, NB)
            ahead(0, 4)
            add_mlp(NB - 1, 0)
            ahead(0, 5)
            add_mlp(NB - 1, 1)
            lstat(2 * NB - 1, 1, a_b2, b_sum, 2 * NB - 2)
            dve.wait_ge(b_x2, NB - 1)
            norm_affine(2 * NB - 1, 1, a_b2, mixed_out)
            ahead(0, 6)
            dve.wait_ge(b_x2, NB)
            norm(3 * NB - 1, NB - 1, to_inner=True)
            dve.wait_ge(c_zero, C_ZERO)
            for l in range(LAYERS):
                n0 = l * NT
                ahead(l, 7)
                ahead(l, 8)
                with dve.Fori(0, NB - 1) as b:
                    attention(n0 + b * TT, b, l, True)
                attention(n0 + (NB - 1) * TT, NB - 1, l, False)
                with dve.Fori(0, NB - 1) as b:
                    mlp(l * NB + b, b, l, True)
                mlp(l * NB + NB - 1, NB - 1, l, False)

        @block.scalar
        def _(act):
            def transposed_out(b):
                for c in range(KD):
                    act.wait_ge(a_tp, 2 * b + c + 1)
                    act.activation(normed_t[:, c, :], bank[c][:, :], ACT.Copy).then_inc(a_tp_out, 1)

            def inputs(b):
                for j in range(KR):
                    u = 12 * b + j
                    src = bank[2 + j % 4]
                    act.wait_ge(a_full, u + 1)
                    act.activation(raw[:, j, TAPS - 1:TAPS - 1 + T], src[:, :], ACT.Copy).then_inc(a_raw, 1)
                    act.activation(conv[:, j, :], src[:, :], ACT.Identity,
                                   bias=cols[:, C_CONVB + j:C_CONVB + j + 1],
                                   scale=cols[:, C_CONVW + TAPS * j + TAPS - 1:C_CONVW + TAPS * j + TAPS])\
                        .then_inc(a_tap0, 1)
                for j in range(KR):
                    act.wait_ge(a_full, 12 * b + KR + j + 1)
                    act.activation(gate_act[:, b % 2, j, :], bank[2 + (KR + j) % 4][:, :], ACT.Gelu).then_inc(a_gelu, 1)

            act.wait_ge(col_in, 16)
            act.activation(minus_bq[:, :], cols[:, C_BQ:C_BQ + KD], ACT.Copy, scale=-1.0)
            act.activation(fb_tmp[:, 0, :], cols[:, C_FB:C_FB + KR], ACT.Abs).then_inc(fb_step, 1)
            act.wait_ge(fb_step, 1)
            act.activation(fb_tmp[:, 1, :], fb_tmp[:, 0, :], ACT.Exp, scale=-1.0).then_inc(fb_step, 1)
            act.wait_ge(fb_step, 2)
            act.activation(fb_tmp[:, 0, :], fb_tmp[:, 1, :], ACT.Ln, bias=1.0).then_inc(fb_step, 1)
            transposed_out(0)
            inputs(0)

            def gates(b, last):
                act.wait_ge(fb_vec, 4)
                for j in range(KR):
                    act.wait_ge(a_full, 12 * b + 6 + 2 * j + 1)
                    act.activation(beta[:, j, :], bank[2 + (2 * j + 2) % 4][:, :], ACT.Tanh,
                                   bias=half_bf[:, j:j + 1], scale=0.5).then_inc(a_thf, 1)
                    act.wait_ge(a_full, 12 * b + 6 + 2 * j + 2)
                    act.activation(th_in[:, j, :], bank[2 + (2 * j + 3) % 4][:, :], ACT.Tanh,
                                   bias=half_bf[:, KR + j:KR + j + 1], scale=0.5).then_inc(a_th, 1)
                    act.wait_ge(a_thf, 3 * b + j + 1)
                    act.activation(alpha[:, j, :], beta[:, j, :], ACT.Exp, bias=m4sp[:, j:j + 1],
                                   scale=m4sp[:, j:j + 1]).then_inc(a_exp, 1)
                    if j == 0 and not last:
                        transposed_out(b + 1)
                for j in range(KR):
                    act.wait_ge(a_exp, 3 * b + j + 1)
                    act.activation(beta[:, j, :], alpha[:, j, :], ACT.Square).then_inc(a_sq, 1)
                act.wait_ge(a_sq, 3 * b + 3)
                act.activation(beta[:, :, :], beta[:, :, :], ACT.Sqrt, bias=quarter[:, 0:1], scale=-0.25)\
                    .then_inc(a_beta, 1)

            with act.Fori(0, NB - 1) as b:
                gates(b, False)
                act.wait_ge(a_xs0, 3 * b + 3)
                act.wait_ge(a_conv, 3 * b + 3)
                inputs(b + 1)
            gates(NB - 1, True)

            act.wait_ge(e_neg, 1)
            for t in range(TT):
                act.activation(ew[:, t, :], ew[:, t, :], ACT.Exp, bias=ew_stat[:, t, 1:2]).then_inc(e_exp, 1)
            for j in range(TT):
                act.wait_ge(e_tp, j + 1)
                act.activation(ew_t[:, j, :], bank[2 + j][:, :], ACT.Copy).then_inc(e_tp_out, 1)

            def transposed_emb(b):
                for c in range(KD):
                    act.wait_ge(b_tp, 2 * b + c + 1)
                    act.activation(normed_t[:, c, :], bank[c][:, :], ACT.Copy).then_inc(b_tp_out, 1)

            def exps(b):
                for m in range(KD):
                    act.wait_ge(b_kbias, 2 * b + m + 1)
                    act.activation(ek[:, m, :], bank[2 + m][:, :], ACT.Exp, bias=kstat[:, m, 2:3]).then_inc(b_ek, 1)
                for m in range(KD):
                    act.wait_ge(b_full, 6 * b + 4 + m + 1)
                    act.activation(eq[:, m, :], bank[2 + m][:, :], ACT.Exp, bias=minus_bq[:, m:m + 1], scale=-1.0)\
                        .then_inc(b_eq, 1)

            def by_token(b):
                for i, dst in enumerate((ek_tok, ek_tok, ekv_tok, ekv_tok)):
                    h = i % 2
                    act.wait_ge(b_tk, 4 * b + i + 1)
                    act.activation(dst[:, 2 * h:2 * h + 2, :],
                                   bank[2 + (2 + i) % 4][:, :].rearrange("p (t d) -> p t d", t=2), ACT.Copy)\
                        .then_inc(b_tk_out, 1)

            def mlp_x(b):
                for c in range(KD):
                    act.wait_ge(b_ta, 2 * b + c + 1)
                    act.activation(a_t[:, c, :], bank[c][:, :], ACT.Copy).then_inc(b_ta_out, 1)
                for c in range(KF):
                    act.wait_ge(b_f1, KF * b + c + 1)
                    act.activation(ff[:, c, :], bank[2 + (2 + c) % 4][:, :], ACT.Relu,
                                   bias=cols[:, C_B1 + c:C_B1 + c + 1]).then_inc(b_relu, 1)

            transposed_emb(0)
            exps(0)
            by_token(0)

            def mixing(b, nxt):
                if nxt:
                    transposed_emb(b + 1)
                    exps(b + 1)
                mlp_x(b)
                if nxt:
                    by_token(b + 1)

            with act.Fori(0, NB - 1) as b:
                mixing(b, True)
            mlp_x(NB - 1)

            def x_transposed(n, w, src):
                act.wait_ge(c_xt, n + 1)
                act.activation(x_hi[:, :].rearrange("p (c t) -> p c t", t=T + 1)[:, :, w * P:(w + 1) * P],
                               src.rearrange("p (c t) -> p c t", t=P), ACT.Copy)\
                    .then_inc(c_xt_out, 1)

            def square(n, i):
                act.wait_ge(c_p, 3 * n + i + 1)
                act.wait_ge(c_ss, n)
                act.activation(squares[:, i, :], bank[i][:, :], ACT.Square).then_inc(c_sq, 1)

            def values(n, w):
                act.wait_ge(c_p, 3 * n + 3)
                act.activation(v_tok[:, w, :], bank[0][:, :], ACT.Copy).then_inc(c_v, 1)

            def keys(n, w):
                act.wait_ge(c_t, 2 * n + 1)
                act.activation(k_t[:, :, w * P:(w + 1) * P], bank[2][:, :].rearrange("p (c t) -> p c t", t=P),
                               ACT.Copy).then_inc(c_kt, 1)

            def q_even(n):
                act.wait_ge(c_t, 2 * n + 2)
                act.activation(q_heads[0:64, :, :].rearrange("p (c e) t -> p e c t", e=2)[:, 0, :, :],
                               bank[2][0:64, :].rearrange("p (c t) -> p c t", t=P), ACT.Copy).then_inc(c_qe, 1)

            def exps(n, w, i):
                u = 4 * n + i
                nk = 2 * P if w else P
                act.wait_ge(c_nb, u + 1)
                if w or i >= 2:
                    act.wait_ge(c_pt, u - 1)
                for e in range(2):
                    h = 2 * i + e
                    act.activation(probs[:, i % 2, e, 0:nk], scores[:, i % 2, e, 0:nk], ACT.Exp,
                                   bias=row_bias[:, w % 2, h:h + 1], scale=q_rnorm[:, w, h:h + 1],
                                   accum_out=row_sum[:, w % 2, h:h + 1]).then_inc(c_ex, 1)

            def probs_transposed(n, w, i):
                u = 4 * n + i
                act.wait_ge(c_pt, u + 1)
                if w or i >= 2:
                    act.wait_ge(c_pv, u - 1)
                if w:
                    act.activation(probs_t[:, i % 2, :, :], bank[4 + i % 2][:, :].rearrange("p (c t) -> p c t", t=P),
                                   ACT.Copy).then_inc(c_pt_out, 1)
                else:
                    act.activation(probs_t[:, i % 2, 0:4:2, :],
                                   bank[4 + i % 2][:, :].rearrange("p (c t) -> p c t", t=P)[:, 0:4:2, :],
                                   ACT.Copy).then_inc(c_pt_out, 1)

            def attention(n0, l, nxt):
                for w in range(TT):
                    n = n0 + w
                    two, one, three = (w < 2 or nxt), (w < 3 or nxt), (w < 1 or nxt)
                    exps(n, w, 0)
                    if two:
                        square(n + 2, 0)
                    exps(n, w, 1)
                    probs_transposed(n, w, 0)
                    if two:
                        square(n + 2, 1)
                    exps(n, w, 2)
                    probs_transposed(n, w, 1)
                    exps(n, w, 3)
                    probs_transposed(n, w, 2)
                    if two and w < TT - 1:
                        values(n + 2, (w + 2) % TT)
                    if three:
                        x_transposed(n + 3, (w + 3) % TT, bank[1][:, 0:D])
                    if one:
                        keys(n + 1, (w + 1) % TT)
                    else:
                        mlp_input(l * NB, l)
                    probs_transposed(n, w, 3)
                    if one:
                        q_even(n + 1)
                    if two and w == TT - 1:
                        values(n + 2, (w + 2) % TT)

            def mlp_input(m, l):
                for c in range(KD):
                    act.wait_ge(d_tp, 2 * m + c + 1)
                    act.activation(normed_t[:, c, :], bank[c][:, :], ACT.Identity, bias=lcols[:, l, L_B + c:L_B + c + 1],
                                   scale=lcols[:, l, L_G + c:L_G + c + 1]).then_inc(d_tp_out, 1)
                for c in range(KD):
                    act.wait_ge(d_tp_out, 2 * m + c + 1)
                    act.activation(h_hi[:, c, :], normed_t[:, c, :], ACT.Copy).then_inc(d_in_hi, 1)

            def round_qkv(l, i):
                act.wait_ge(wqkv_in, 16 * l + 16)
                for k in range(KD):
                    part = slice(i * INNER, (i + 1) * INNER)
                    act.activation(wqkv_hi[:, k, part], w_stage[:, :].rearrange("p (k n) -> p k n", k=KD)[:, k, part],
                                   ACT.Copy).then_inc(wq_hi, 1)

            def ahead(l, step):
                n0 = l * NT
                if step < 3:
                    round_qkv(l, step)
                    if step == 1:
                        for w in range(2):
                            x_transposed(n0 + w, w, bank[w][:, 0:D])
                elif step < 5:
                    square(n0, step - 3)
                elif step == 5:
                    values(n0, 0)
                    square(n0 + 1, 0)
                    square(n0 + 1, 1)
                    values(n0 + 1, 1)
                else:
                    keys(n0, 0)
                    q_even(n0)
                    x_transposed(n0 + 2, 2, bank[1][:, 0:D])

            def mlp(m, l, nxt):
                for j in range(KH):
                    r = P if j < KH - 1 else HLAST
                    act.wait_ge(d_w1, 2 * (KH * m + j) + 1)
                    if j >= 2:
                        act.wait_ge(d_act, KH * m + j - 1)
                    act.activation(hidden[0:r, j % 2, :], bank[2 + 2 * (j % 2)][0:r, :], ACT.Gelu,
                                   bias=lcols[0:r, l, L_B1G + j:L_B1G + j + 1]).then_inc(d_gelu, 1)
                    hi = hidden_hi[:, j, :] if j < KH - 1 else last_hi
                    act.wait_ge(d_full, KH * m + j + 1)
                    act.activation(hi[0:r, :], hidden[0:r, j % 2, :], ACT.Copy).then_inc(d_hi, 1)
                    if not nxt and l < LAYERS - 1 and j != 3:
                        ahead(l + 1, (0, 1, 2, None, 3, 4)[j])
                if nxt:
                    mlp_input(m + 1, l)
                elif l < LAYERS - 1:
                    ahead(l + 1, 5)

            act.wait_ge(b_ta, KD * NB)
            for step in range(6):
                ahead(0, step)
            act.wait_ge(c_zero, C_ZERO)
            for l in range(LAYERS):
                n0 = l * NT
                ahead(l, 6)
                with act.Fori(0, NB - 1) as b:
                    attention(n0 + b * TT, l, True)
                attention(n0 + (NB - 1) * TT, l, False)
                with act.Fori(0, NB - 1) as b:
                    mlp(l * NB + b, l, True)
                mlp(l * NB + NB - 1, l, False)

        @block.tensor
        def _(pe):
            def product(out, terms):
                for i, (stationary, moving) in enumerate(terms):
                    ins = pe.matmul(out, stationary, moving, start=(i == 0), stop=(i == len(terms) - 1))
                return ins
            def transpose_in(b):
                pe.wait_ge(n_norm, 4 * b + 4)
                for c in range(KD):
                    for t in range(TT):
                        ins = pe.transpose(bank[c][:, t * P:(t + 1) * P], normed[:, t, c * P:(c + 1) * P],
                                           ident[:, :])
                    ins.then_inc(a_tp, 1)

            def inputs(b):
                pe.wait_ge(a_tp_out, 2 * b + 2)
                for j in range(2 * KR):
                    m = (j + KR) % (2 * KR)
                    if not (isinstance(b, int) and b == 0):
                        if j < 4:
                            if j % 2 == 0:
                                pe.wait_ge(a_thf, 3 * (b - 1) + (2 + j) // 2 + 1)
                            else:
                                pe.wait_ge(a_th, 3 * (b - 1) + (2 + j) // 2 + 1)
                    if j >= 4:
                        pe.wait_ge(a_tap0, 3 * b + j - 4 + 1)
                    for k in range(KD):
                        ins = pe.matmul(bank[2 + j % 4][:, :], w_in_sb[:, k, m * P:(m + 1) * P],
                                        normed_t[:, k, :], start=(k == 0), stop=(k == KD - 1))
                    ins.then_inc(a_full, 1)

            def gates(b, last):
                pe.wait_ge(a_conv, 3 * b + 3)
                for j in range(KR):
                    for g in range(2):
                        u = 2 * j + g
                        if u == 0:
                            pe.wait_ge(a_tap0, 3 * b + 3)
                        elif u < 4:
                            pe.wait_ge(a_gelu, 3 * b + u)
                        elif u == 4:
                            pe.wait_ge(a_thf, 3 * b + 1)
                        else:
                            pe.wait_ge(a_th, 3 * b + 1)
                        m = g * KR + j
                        for k in range(KR):
                            ins = pe.matmul(bank[2 + (u + 2) % 4][:, :], w_gate_sb[:, k, m * P:(m + 1) * P],
                                            conv[:, k, :], start=(k == 0), stop=(k == KR - 1))
                        ins.then_inc(a_full, 1)
                    if j == 0 and not last:
                        transpose_in(b + 1)

            def output(b):
                pe.wait_ge(a_gh, 3 * b + 3)
                pe.wait_ge(a_res, 2 * b)
                for t in range(TT):
                    for k in range(KR):
                        ins = pe.matmul(bank[6 + t // 2][:, (t % 2) * D:(t % 2 + 1) * D],
                                        scanned[:, k, t * P:(t + 1) * P], w_out_sb[:, k, :],
                                        start=(k == 0), stop=(k == KR - 1))
                    if t % 2:
                        ins.then_inc(a_o, 1)

            pe.wait_ge(ready_consts, 1)
            transpose_in(0)
            pe.wait_ge(w1s_in, 16)
            inputs(0)
            pe.wait_ge(wg_in, 16)
            pe.wait_ge(wor_in, 16)
            with pe.Fori(0, NB - 1) as b:
                gates(b, False)
                inputs(b + 1)
                output(b)
            gates(NB - 1, True)

            def bias_by_key():
                pe.wait_ge(a_th, 3 * NB)
                pe.wait_ge(a_thf, 3 * NB)
                pe.wait_ge(e_exp, TT)
                for j in range(TT):
                    for t in range(TT):
                        ins = pe.transpose(bank[2 + j][:, t * P:(t + 1) * P], ew[:, t, j * P:(j + 1) * P],
                                           ident[:, :])
                    ins.then_inc(e_tp, 1)

            def transpose_emb(b):
                pe.wait_ge(b_emb, b + 1)
                for c in range(KD):
                    for t in range(TT):
                        ins = pe.transpose(bank[c][:, t * P:(t + 1) * P], normed[:, t, c * P:(c + 1) * P],
                                           ident[:, :])
                    ins.then_inc(b_tp, 1)

            def project(b):
                pe.wait_ge(b_tp_out, 2 * b + 2)
                for i in range(3 * KD):
                    w, m = (w_k, w_v, w_q)[i // KD], i % KD
                    if i >= 2 * KD:
                        pe.wait_ge(b_ek, 2 * b + m + 1)
                    for k in range(KD):
                        ins = pe.matmul(bank[2 + i % 4][:, :], w[:, k, m * P:(m + 1) * P], normed_t[:, k, :],
                                        start=(k == 0), stop=(k == KD - 1))
                    ins.then_inc(b_full, 1)

            def keys_by_token(b):
                for i in range(4):
                    src, h = (ek, ekv)[i // 2], i % 2
                    if i == 0:
                        pe.wait_ge(b_ekv, 2 * b + 2)
                        pe.wait_ge(b_eq, 2 * b + 2)
                    if not (isinstance(b, int) and b == 0):
                        pe.wait_ge(b_relu, KF * (b - 1) + 5 + i)
                    for t in range(2):
                        for m in range(KD):
                            ins = pe.transpose(bank[2 + (2 + i) % 4][:, (2 * t + m) * P:(2 * t + m + 1) * P],
                                               src[:, m, (2 * h + t) * P:(2 * h + t + 1) * P], ident[:, :])
                    ins.then_inc(b_tk, 1)

            def mix_tokens(b):
                pe.wait_ge(b_tk_out, 4 * b + 4)
                for m in range(KD):
                    for i, src in enumerate((ek_tok, ekv_tok)):
                        for j in range(TT):
                            ins = pe.matmul(bank[2 + (2 * m + i + 2) % 4][:, :], src[:, j, m * P:(m + 1) * P],
                                            ew_t[:, j, :], start=(j == 0), stop=(j == TT - 1))
                        ins.then_inc(b_aft, 1)

            def project_mixed(b):
                pe.wait_ge(b_y, 2 * b + 2)
                for t in range(TT):
                    if t % 2 == 0:
                        pe.wait_ge(b_sum, 2 * b - 1 + t // 2) if not (isinstance(b, int) and b == 0) else None
                    for k in range(KD):
                        ins = pe.matmul(bank[6 + t // 2][:, (t % 2) * D:(t % 2 + 1) * D],
                                        y[:, k, t * P:(t + 1) * P], w_o[:, k, :], start=(k == 0),
                                        stop=(k == KD - 1))
                    if t % 2:
                        ins.then_inc(b_o, 1)

            def transpose_a(b):
                pe.wait_ge(l_out, 8 * b + 4)
                for c in range(KD):
                    for t in range(TT):
                        ins = pe.transpose(bank[c][:, t * P:(t + 1) * P], a_tok[:, t, c * P:(c + 1) * P],
                                           ident[:, :])
                    ins.then_inc(b_ta, 1)

            def mlp_up_x(b, nxt):
                pe.wait_ge(b_ta_out, 2 * b + 2)
                for c in range(KF):
                    if c >= 4:
                        pe.wait_ge(b_relu, KF * b + c - 3)
                    elif nxt:
                        pe.wait_ge(b_ekv if c < 2 else b_eq, 2 * (b + 1) + c % 2 + 1)
                    for k in range(KD):
                        ins = pe.matmul(bank[2 + (2 + c) % 4][:, :], w_1[:, k, c * P:(c + 1) * P], a_t[:, k, :],
                                        start=(k == 0), stop=(k == KD - 1))
                    ins.then_inc(b_f1, 1)

            def mlp_down_x(b, t):
                if t == 0:
                    pe.wait_ge(b_mix, 2 * b + 2)
                for k in range(KF):
                    if t == 0:
                        pe.wait_ge(b_relu, KF * b + k + 1)
                    ins = pe.matmul(bank[6 + t // 2][:, (t % 2) * D:(t % 2 + 1) * D],
                                    ff[:, k, t * P:(t + 1) * P], w_2[:, k, :], start=(k == 0), stop=(k == KF - 1))
                if t % 2:
                    ins.then_inc(b_f2, 1)

            bias_by_key()
            transpose_emb(0)
            pe.wait_ge(e_tp_out, TT)
            pe.wait_ge(aft_in, 64)
            project(0)
            output(NB - 1)
            pe.wait_ge(a_res, 2 * NB)
            keys_by_token(0)
            mix_tokens(0)
            project_mixed(0)
            pe.wait_ge(mlp_in, 32)

            def mixing(b, nxt):
                if nxt:
                    transpose_emb(b + 1)
                    project(b + 1)
                transpose_a(b)
                mlp_up_x(b, nxt)
                if nxt:
                    keys_by_token(b + 1)
                    mix_tokens(b + 1)
                for t in range(TT):
                    mlp_down_x(b, t)
                if nxt:
                    project_mixed(b + 1)

            with pe.Fori(0, NB - 1) as b:
                mixing(b, True)

            def transpose_x(n, par, dst, free):
                for sem, v in free:
                    pe.wait_ge(sem, v)
                pe.wait_ge(c_xs, n + 1)
                for c in range(KD):
                    ins = pe.transpose(dst[:, c * P:(c + 1) * P], x_tile[:, par, c * P:(c + 1) * P], ident[:, :])
                ins.then_inc(c_xt, 1)

            def qkv(n, w, i):
                if i == 0:
                    pe.wait_ge(c_xt_lo, n + 1)
                    pe.wait_ge(c_v, n)
                elif i == 1:
                    pe.wait_ge(c_rope, 6 * n)
                else:
                    pe.wait_ge(c_rope, 6 * n + 3)
                product(bank[i % 2][:, :], [
                    (x[:, k * T + w * P:k * T + (w + 1) * P], m[:, k, i * INNER:(i + 1) * INNER])
                    for k in range(KD)
                    for x, m in ((x_hi, wqkv_hi), (x_hi, wqkv_lo), (x_lo, wqkv_hi))]).then_inc(c_p, 1)

            def transpose_k(n, par, free):
                for sem, v in free:
                    pe.wait_ge(sem, v)
                pe.wait_ge(c_kn, n + 1)
                for c in range(KI):
                    ins = pe.transpose(bank[2][:, c * P:(c + 1) * P], k_tok[:, par, c * P:(c + 1) * P], ident[:, :])
                ins.then_inc(c_t, 1)

            def transpose_q(n, par):
                pe.wait_ge(c_kt, n + 1)
                for c in range(KI):
                    ins = pe.transpose(bank[2][:, c * P:(c + 1) * P], q_tok[:, par, c * P:(c + 1) * P], ident[:, :])
                ins.then_inc(c_t, 1)

            def score(n, w, i):
                u = 4 * n + i
                if i == 0:
                    pe.wait_ge(c_qe, n + 1)
                    pe.wait_ge(c_qo, n + 1)
                if w or i >= 2:
                    pe.wait_ge(c_tt, 2 * u - 2)
                k0 = max(w - 1, 0) * P
                for e in range(2):
                    nk = (w + 1) * P - k0
                    ins = pe.matmul(bank[6 + i % 2][:, e * 2 * P:e * 2 * P + nk], q_heads[:, 2 * i + e, :],
                                    k_t[:, i, k0:(w + 1) * P], start=True, stop=True)
                ins.then_inc(c_qk, 1)

            def transpose_probs(n, w, i):
                u = 4 * n + i
                pe.wait_ge(c_ex, 2 * u + 2)
                if w or i >= 2:
                    pe.wait_ge(c_pt_out, u - 1)
                for e in range(2):
                    for k in range(2 if w else 1):
                        ins = pe.transpose(bank[4 + i % 2][:, (2 * e + k) * P:(2 * e + k + 1) * P],
                                           probs[:, i % 2, e, k * P:(k + 1) * P], ident[:, :])
                ins.then_inc(c_pt, 1)

            def weigh_values(n, w, i):
                u = 4 * n + i
                pe.wait_ge(c_pt_out, u + 1)
                if i == 0:
                    pe.wait_ge(c_v, n + 1)
                    pe.wait_ge(c_on, n)
                nk = 2 if w else 1
                for e in range(2):
                    h = 2 * i + e
                    for k in range(nk):
                        ins = pe.matmul(bank[3][:, h * DH:(h + 1) * DH], probs_t[:, i % 2, 2 * e + k, :],
                                        v_tok[:, w - nk + 1 + k, h * DH:(h + 1) * DH], start=(k == 0),
                                        stop=(k == nk - 1))
                ins.then_inc(c_pv, 1)

            def transpose_o(n, free):
                for sem, v in free:
                    pe.wait_ge(sem, v)
                pe.wait_ge(c_on, n + 1)
                for c in range(KI):
                    ins = pe.transpose(bank[2][:, c * P:(c + 1) * P], o_tok[:, c * P:(c + 1) * P], ident[:, :])
                ins.then_inc(c_ot, 1)

            def project_o(n):
                pe.wait_ge(c_ot_out, n + 1)
                for k in range(KI):
                    ins = pe.matmul(bank[2][:, 0:D], o_t[:, k, :], wo_sb[:, k, :], start=(k == 0), stop=(k == KI - 1))
                ins.then_inc(c_wo, 1)

            def attention(n0, l, nxt):
                free = [(c_qe, n0 + 1), (c_qo, n0 + 1), (c_res, n0)]
                for w in range(TT):
                    n = n0 + w
                    two, one, three = (w < 2 or nxt), (w < 3 or nxt), (w < 1 or nxt)
                    score(n, w, 0)
                    score(n, w, 1)
                    if w:
                        transpose_o(n - 1, free)
                    if two:
                        qkv(n + 2, (w + 2) % TT, 0)
                    transpose_probs(n, w, 0)
                    score(n, w, 2)
                    if two:
                        qkv(n + 2, (w + 2) % TT, 1)
                    weigh_values(n, w, 0)
                    transpose_probs(n, w, 1)
                    if w:
                        project_o(n - 1)
                        free = [(c_res, n)]
                    score(n, w, 3)
                    weigh_values(n, w, 1)
                    transpose_probs(n, w, 2)
                    if two and w < TT - 1:
                        qkv(n + 2, (w + 2) % TT, 2)
                    if three:
                        transpose_x(n + 3, (w + 3) % 2, bank[1][:, 0:D], [(c_rope, 6 * (n + 2) + 6)])
                    if one:
                        transpose_k(n + 1, (w + 1) % 2, free)
                    else:
                        transpose_mlp(l * NB)
                    weigh_values(n, w, 2)
                    transpose_probs(n, w, 3)
                    if one:
                        transpose_q(n + 1, (w + 1) % 2)
                        free = [(c_qe, n + 2), (c_qo, n + 2)]
                    weigh_values(n, w, 3)
                    if w == TT - 1:
                        if two:
                            qkv(n + 2, (w + 2) % TT, 2)
                        transpose_o(n, free)
                        project_o(n)

            def transpose_mlp(m):
                pe.wait_ge(d_norm, 8 * m + 8)
                for c in range(KD):
                    for t in range(TT):
                        ins = pe.transpose(bank[c][:, t * P:(t + 1) * P], normed[:, t, c * P:(c + 1) * P],
                                           ident[:, :])
                    ins.then_inc(d_tp, 1)

            w1_hi, w1_lo = (w[:, 0:W1_COLS].rearrange("p (k n) -> p k n", k=KD) for w in (wm_hi, wm_lo))
            w2_hi, w2_lo = (w[:, W1_COLS:W1_COLS + W2_COLS].rearrange("p (k n) -> p k n", k=KH)
                            for w in (wm_hi, wm_lo))

            def mlp_up(m, j):
                if j == 0:
                    pe.wait_ge(d_in_lo, 2 * m + 2)
                r = P if j < KH - 1 else HLAST
                for g, c0 in enumerate((HID, 0)):
                    if j >= 2:
                        pe.wait_ge((d_gelu, d_full)[g], KH * m + j - 1)
                    product(bank[2 + 2 * (j % 2) + g][0:r, :], [
                        (w[:, k, c0 + j * P:c0 + j * P + r], h[:, k, :]) for k in range(KD)
                        for w, h in ((w1_hi, h_hi), (w1_hi, h_lo), (w1_lo, h_hi))]).then_inc(d_w1, 1)

            def mlp_down(m, t):
                if t % 2 == 0:
                    pe.wait_ge((d_res0, b_res)[t // 2], m if t == 0 else m + NB)
                for k in range(KH):
                    if t == 0:
                        pe.wait_ge(d_act, KH * m + k + 1)
                    r = P if k < KH - 1 else HLAST + 1
                    hi, lo = (hidden_hi[:, k, :], hidden_lo[:, k, :]) if k < KH - 1 else (last_hi, last_lo)
                    for h, w in ((hi, w2_hi), (hi, w2_lo), (lo, w2_hi)):
                        ins = pe.matmul(bank[6 + t // 2][:, (t % 2) * D:(t % 2 + 1) * D],
                                        h[0:r, t * P:(t + 1) * P], w[0:r, k, :], start=(k == 0 and w is w2_hi and h is hi),
                                        stop=(k == KH - 1 and h is lo))
                ins.then_inc(d_w2, 1)

            def ahead(l, step):
                n0 = l * NT
                if step == 0:
                    for w in range(2):
                        transpose_x(n0 + w, w, bank[w][:, 0:D], [])
                elif step <= 6:
                    w, i = divmod(step - 1, 3)
                    if step == 1:
                        pe.wait_ge(c_xt_lo, n0 + 2)
                    if w == 0:
                        pe.wait_ge(wq_lo, 6 * l + 2 * i + 2)
                    qkv(n0 + w, w, i)
                else:
                    transpose_k(n0, 0, [])
                    transpose_q(n0, 0)
                    transpose_x(n0 + 2, 0, bank[1][:, 0:D], [(c_rope, 6 * (n0 + 1) + 6)])

            def mlp(m, l, nxt):
                also = not nxt and l < LAYERS - 1
                for j in range(KH):
                    mlp_up(m, j)
                    if also and j in (1, 3, 4):
                        ahead(l + 1, (1, 3, 4).index(j))
                for t in range(TT):
                    mlp_down(m, t)
                    if nxt and t == 1:
                        transpose_mlp(m + 1)
                    if also:
                        ahead(l + 1, 3 + t)

            transpose_a(NB - 1)
            mlp_up_x(NB - 1, False)
            ahead(0, 0)
            mlp_down_x(NB - 1, 0)
            mlp_down_x(NB - 1, 1)
            ahead(0, 1)
            mlp_down_x(NB - 1, 2)
            ahead(0, 2)
            mlp_down_x(NB - 1, 3)
            for step in range(3, 7):
                ahead(0, step)
            for l in range(LAYERS):
                n0 = l * NT
                ahead(l, 7)
                pe.wait_ge(wo_in, 16 * l + 16)
                pe.wait_ge(b_res, NB * (l + 1))
                with pe.Fori(0, NB - 1) as b:
                    attention(n0 + b * TT, l, True)
                attention(n0 + (NB - 1) * TT, l, False)
                pe.wait_ge(wm_split, WM_PIECES * NB * (l + 1))
                pe.wait_ge(c_res, NT * (l + 1))
                with pe.Fori(0, NB - 1) as b:
                    mlp(l * NB + b, l, True)
                mlp(l * NB + NB - 1, l, False)


def _chunks(w):
    k, n = w.shape
    return w.reshape(k // P, P, n).transpose(1, 0, 2)


def _columns(v):
    return v.reshape(-1, P).T


def kernel(**inputs):
    import numpy as np
    import concourse.bacc as _bacc
    from concourse.bass_utils import run_bass_kernel_spmd as _run

    a = {k: np.asarray(v) for k, v in inputs.items()}
    f32 = np.float32
    cols = np.concatenate([
        _chunks(a["L0_attn_conv_w"].reshape(RH, TAPS)).reshape(P, KR * TAPS),
        _columns(a["L0_attn_conv_b"]), _columns(a["L0_attn_b_g"]), _columns(a["L0_attn_forget_base"]),
        _columns(a["L0_xattn_bq"]), _columns(a["L0_xattn_bk"]), _columns(a["L0_xattn_bv"]),
        _columns(a["L0_xattn_b1"])], axis=1)
    rows = np.broadcast_to(np.stack([a["L0_xattn_bo"], a["L0_xattn_gamma"], a["L0_xattn_beta"],
                                     a["L0_xattn_b2"]]), (P, 4, D))

    def hid_columns(v):
        full = np.zeros((KH * P,), f32)
        full[:HID] = v
        return _columns(full)

    lcols = np.stack([np.concatenate([
        _columns(a["L0_ffn_ln_g"][l]), _columns(a["L0_ffn_ln_b"][l]),
        hid_columns(a["L0_ffn_b1"][l][:HID]), hid_columns(a["L0_ffn_b1"][l][HID:])], axis=1)
        for l in range(LAYERS)], axis=1)
    qk_scale = np.broadcast_to(np.stack([a["L0_ffn_q_scale"], a["L0_ffn_k_scale"]], axis=1), (P, LAYERS, 2, DH))
    half = np.arange(0, DH, 2, dtype=f32)
    pos = np.arange(T, dtype=f32)
    inv_freq = (f32(1.0) / f32(10000.0) ** (half / f32(DH))).astype(f32)
    freqs = pos[:, None] * inv_freq[None, :]
    freqs = np.concatenate([freqs, freqs], axis=-1)
    base = (half + f32(0.4 * DH)) / f32(1.4 * DH)
    power = (pos - f32(T // 2)) / f32(P // 2)
    scale = (base[None, :] ** power[:, None]).astype(f32)
    scale = np.concatenate([scale, scale], axis=-1)
    sign = np.concatenate([-np.ones(DH // 2, f32), np.ones(DH // 2, f32)])
    cos, sin = np.cos(freqs), np.sin(freqs) * sign
    rope = np.stack([cos * scale, sin * scale, cos / scale, sin / scale]).astype(f32)
    rope = rope.reshape(4, TT, P, DH).transpose(2, 0, 1, 3)
    w2 = np.zeros((LAYERS, KH * P, D), f32)
    w2[:, :HID] = a["L0_ffn_w2"]
    w2[:, HID] = a["L0_ffn_b2"]
    layer = lambda w: np.stack([_chunks(w[l]) for l in range(LAYERS)])
    wm = np.concatenate([layer(a["L0_ffn_w1"]).reshape(LAYERS, P, -1), layer(w2).reshape(LAYERS, P, -1)], axis=2)
    wm = np.pad(wm, ((0, 0), (0, 0), (0, WM_COLS - wm.shape[2])))
    named = {
        "x": a["x"], "ctx": a["ctx_1024"], "cols": cols, "rows": rows,
        "w_in": _chunks(a["L0_attn_W_in"].T), "w_gate": _chunks(a["L0_attn_W_g"].T),
        "w_out": _chunks(a["L0_attn_W_out"].T),
        "wq": _chunks(a["L0_xattn_wq"]), "wk": _chunks(a["L0_xattn_wk"]), "wv": _chunks(a["L0_xattn_wv"]),
        "wo_x": _chunks(a["L0_xattn_wo"]), "pos_bias": _chunks(a["L0_xattn_pos_bias"]),
        "w1_x": _chunks(a["L0_xattn_w1"]), "w2_x": _chunks(a["L0_xattn_w2"]),
        "lcols": lcols, "qk_scale": qk_scale, "rope": rope,
        "wqkv": layer(a["L0_ffn_wqkv"]), "wo_l": layer(a["L0_ffn_wo"]), "wm_l": wm}
    nc = _bacc.Bacc("TRN2", target_bir_lowering=False, num_devices=1)
    arrays, args = {}, []
    for name, v in named.items():
        v = np.ascontiguousarray(v)
        arrays[f"in_{name}_dram"] = v
        args.append(nc.dram_tensor(f"in_{name}_dram", v.shape, mybir.dt.from_np(v.dtype), kind="ExternalInput").ap())
    args.append(nc.dram_tensor("out_0_dram", (NB, T, D), F32, kind="ExternalOutput").ap())
    build(nc, STAGES, *args)
    r = _run(nc, [arrays], core_ids=[0])
    return r.results[0]["out_0_dram"]


STAGES = 3
```

```python
from contextlib import ExitStack

import concourse.bass as bass
from concourse import mybir

F32 = mybir.dt.float32
F32R = mybir.dt.float32r
ALU = mybir.AluOpType
ACT = mybir.ActivationFunctionType
AX_X = mybir.AxisListType.X

P = 128
NB, T, D = 4, 512, 256
TT = T // P
NT = NB * TT
KD = D // P
RH = 384
KR = RH // P
TAPS = 4
FH = 1024
KF = FH // P
LAYERS, HEADS, DH = 2, 8, 64
INNER = HEADS * DH
KI = INNER // P
HID = 682
KH = 6
HLAST = HID - (KH - 1) * P
WM_PIECES = 3
WM_PIECE = 356
WM_QUARTER = WM_PIECES * WM_PIECE
WIN_COLS, WG_COLS = KD * 2 * RH, KR * 2 * RH
W1_COLS, W2_COLS = KD * 2 * HID, KH * D
WM_COLS = NB * WM_QUARTER
BAND = 64
QK_SCALE = 8.0
LN_EPS = 1e-5
BETA_EPS = 1e-6
NEG = -1e30

C_CONVW, C_CONVB, C_BG, C_FB = 0, 12, 15, 21
C_BQ, C_BK, C_BV, C_B1 = 24, 26, 28, 30
NCOL = 38
L_G, L_B, L_B1A, L_B1G = 0, 2, 4, 10
NLCOL = 16
R_BO, R_GAMMA, R_BETA, R_B2 = range(4)
TQC, TQS, TKC, TKS = range(4)


def build(nc, x, ctx_in, cols_in, rows_in, w_in, w_gate, w_out, wq, wk, wv, wo_x, pos_bias,
          w1_x, w2_x, lcols_in, qk_scale, rope, wqkv, wo_l, wm_l, out):
    with ExitStack() as ctx:
        def sb(name, shape, dt=F32, stack=ctx):
            return stack.enter_context(nc.sbuf_tensor(name, shape, dt))

        def signals(names):
            return [ctx.enter_context(nc.semaphore(n)) for n in names.split()]

        bank = [ctx.enter_context(nc.psum_tensor(f"bank{i}", [P, 512], F32)) for i in range(8)]

        stream = sb("stream", [P, NT, D])
        cols = sb("cols", [P, NCOL])
        ident = sb("ident", [P, P])
        minus_half = sb("minus_half", [P, 2 * HEADS])
        mask = sb("mask", [P, 2 * P])
        stats = sb("stats", [P, TT, 12])
        mean_var = sb("mean_var", [P, TT, 2])
        var_eps = sb("var_eps", [P, TT])
        rstd = sb("rstd", [P, TT])
        normed = sb("normed", [P, TT, D])
        t_hi = sb("t_hi", [P, KD, T], F32R)
        t_lo = sb("t_lo", [P, KD, T], F32R)
        lcols = sb("lcols", [P, LAYERS, NLCOL])

        inner = sb("inner", [P, NT, D])
        w_stage = sb("w_stage", [P, KD * 3 * INNER])
        st_scan = ExitStack()
        scanned = sb("scanned", [P, KR, T], stack=st_scan)
        st_scan.close()
        wo_sb = sb("wo_sb", [P, KI, D])
        qk_scale_sb = sb("qk_scale_sb", [P, LAYERS, 2, DH])
        rope_sb = sb("rope_sb", [P, 4, TT, DH])
        st12 = ExitStack()
        w_qkv_hi = sb("w_qkv_hi", [P, 3, KD, D], F32R, stack=st12)
        w_qkv_lo = sb("w_qkv_lo", [P, 3, KD, D], F32R, stack=st12)
        w_o = sb("w_o", [P, KD, D], stack=st12)
        st_in = ExitStack()
        w_in_hi = sb("w_in_hi", [P, KD, 2 * RH], F32R, stack=st_in)
        w_in_lo = sb("w_in_lo", [P, KD, 2 * RH], F32R, stack=st_in)
        w_gate_hi = sb("w_gate_hi", [P, KR, 2 * RH], F32R, stack=st_in)
        w_gate_lo = sb("w_gate_lo", [P, KR, 2 * RH], F32R, stack=st_in)
        st_in.close()
        emb = sb("emb", [P, NT, D], stack=st12)
        ew_t = sb("ew_t", [P, TT, T], stack=st12)
        ek = sb("ek", [P, KD, T], stack=st12)
        ekv = sb("ekv", [P, KD, T], stack=st12)
        eq = sb("eq", [P, KD, T], stack=st12)
        ew_stat = sb("ew_stat", [P, TT, 2], stack=st12)
        minus_bq = sb("minus_bq", [P, KD], stack=st12)
        kstat = sb("kstat", [P, KD, 3], stack=st12)
        st_bias = ExitStack()
        ew = sb("ew", [P, TT, T], stack=st_bias)
        st_bias.close()
        w_1_lo = sb("w_1_lo", [P, KD, FH], F32R, stack=st12)
        w_1_hi = sb("w_1_hi", [P, KD, FH], F32R, stack=st12)
        w_2 = sb("w_2", [P, KF, D], stack=st12)
        rows = sb("rows", [P, 4, D], stack=st12)
        st1 = ExitStack()
        w_out_sb = sb("w_out_sb", [P, KR, D], stack=st1)
        raw = sb("raw", [P, KR, TAPS - 1 + T], stack=st1)
        conv = sb("conv", [P, KR, T], stack=st1)
        conv_hi = sb("conv_hi", [P, KR, T], F32R, stack=st1)
        conv_lo = sb("conv_lo", [P, KR, T], F32R, stack=st1)
        gate_act = sb("gate_act", [P, 2, KR, T], stack=st1)
        th_in = sb("th_in", [P, KR, T], stack=st1)
        alpha = sb("alpha", [P, KR, T], stack=st1)
        beta = sb("beta", [P, KR, T], stack=st1)
        fb_tmp = sb("fb_tmp", [P, 3, KR], stack=st1)
        m4sp = sb("m4sp", [P, KR], stack=st1)
        half_bf = sb("half_bf", [P, 2 * KR], stack=st1)
        quarter = sb("quarter", [P, 1], stack=st1)
        st1.close()
        st2 = ExitStack()
        ek_tok = sb("ek_tok", [P, TT, D], stack=st2)
        ekv_tok = sb("ekv_tok", [P, TT, D], stack=st2)
        y = sb("y", [P, KD, T], stack=st2)
        mix = sb("mix", [P, TT, D], stack=st2)
        a_tok = sb("a_tok", [P, TT, D], stack=st2)
        a_hi = sb("a_hi", [P, KD, T], F32R, stack=st2)
        a_lo = sb("a_lo", [P, KD, T], F32R, stack=st2)
        a_b2 = sb("a_b2", [P, TT, D], stack=st2)
        mixed_out = sb("mixed_out", [P, TT, D], stack=st2)
        ff = sb("ff", [P, KF, T], stack=st2)
        lstats = sb("lstats", [P, 2, TT, 6], stack=st2)
        lmv = sb("lmv", [P, 2, TT, 2], stack=st2)
        lveps = sb("lveps", [P, 2, TT], stack=st2)
        lrstd = sb("lrstd", [P, 2, TT], stack=st2)
        st2.close()
        st12.close()
        wqkv_hi = sb("wqkv_hi", [P, KD, 3 * INNER], F32R)
        wqkv_lo = sb("wqkv_lo", [P, KD, 3 * INNER], F32R)
        x_hi = sb("x_hi", [P, KD * (T + 1)], F32R)
        x_lo = sb("x_lo", [P, KD * (T + 1)], F32R)
        x_tile = sb("x_tile", [P, 2, D])
        rope_l = sb("rope_l", [P, 4, TT, DH])
        q_heads = sb("q_heads", [P, HEADS, P])
        squares = sb("squares", [P, 2, INNER])
        rot = sb("rot", [P, 4, INNER])
        wm_hi = sb("wm_hi", [P, WM_COLS], F32R)
        wm_lo = sb("wm_lo", [P, WM_COLS], F32R)
        q_tok = sb("q_tok", [P, 2, INNER])
        k_tok = sb("k_tok", [P, 2, INNER])
        norms = sb("norms", [P, 3, 2 * HEADS])
        q_rnorm = sb("q_rnorm", [P, 4, HEADS])
        row_max = sb("row_max", [P, 2, HEADS])
        row_bias = sb("row_bias", [P, 2, HEADS])
        row_sum = sb("row_sum", [P, 2, HEADS])
        row_rsum = sb("row_rsum", [P, HEADS])
        v_tok = sb("v_tok", [P, TT, INNER])
        last_hi = sb("last_hi", [P, T], F32R)
        last_lo = sb("last_lo", [P, T], F32R)
        shifted = sb("shifted", [P, TT, P])
        h_t = sb("h_t", [P, KD, T])
        st_att = ExitStack()
        o_tok = sb("o_tok", [P, INNER], stack=st_att)
        o_t = sb("o_t", [P, KI, P], stack=st_att)
        k_t = sb("k_t", [P, KI, T], stack=st_att)
        scores = sb("scores", [P, 2, 2, 2 * P], stack=st_att)
        probs = sb("probs", [P, 2, 2, 2 * P], stack=st_att)
        probs_t = sb("probs_t", [P, 2, 4, P], stack=st_att)
        st_att.close()
        hidden = sb("hidden", [P, 2, T])
        hidden_hi = sb("hidden_hi", [P, KH - 1, T], F32R)
        hidden_lo = sb("hidden_lo", [P, KH - 1, T], F32R)

        (x0_in, xr_in, col_in, w1s_in, wg_in, wor_in, aft_in, ctx_sem, pos_in, mlp_in, rows_sem) = signals(
            "x0_in xr_in col_in w1s_in wg_in wor_in aft_in ctx_sem pos_in mlp_in rows_sem")
        (pool_ready, fb_step, fb_vec, ready_consts) = signals("pool_ready fb_step fb_vec ready_consts")
        (n_stats, n_aggr, n_eps, n_rstd, n_norm) = signals("n_stats n_aggr n_eps n_rstd n_norm")
        (a_tp, a_tp_out, a_full, a_thf, a_th, a_gelu, a_exp, a_sq, a_beta, a_tap0, a_tap, a_conv,
         a_xs0, a_xs, a_scan, a_gh, a_o, a_res) = signals(
            "a_tp a_tp_out a_full a_thf a_th a_gelu a_exp a_sq a_beta a_tap0 a_tap a_conv "
            "a_xs0 a_xs a_scan a_gh a_o a_res")
        (e_band, e_max, e_neg, e_exp, e_tp, e_tp_out) = signals("e_band e_max e_neg e_exp e_tp e_tp_out")
        (b_emb, b_embo, b_tp, b_tp_out, b_full, b_kmax, b_kbias, b_ek, b_ekv, b_eq, b_tk, b_tk_out, b_aft, b_den,
         b_rec, b_y, b_o, b_mix, b_ta, b_ta_out, b_relu, b_f1, b_ab2, b_f2, b_sum, b_x2, b_res) = signals(
            "b_emb b_embo b_tp b_tp_out b_full b_kmax b_kbias b_ek b_ekv b_eq b_tk b_tk_out b_aft b_den b_rec "
            "b_y b_o b_mix b_ta b_ta_out b_relu b_f1 b_ab2 b_f2 b_sum b_x2 b_res")
        (l_stats, l_aggr, l_eps, l_rstd, l_mid, a_out, l_out) = signals(
            "l_stats l_aggr l_eps l_rstd l_mid a_out l_out")
        (c_zero, c_tab, c_xs, c_xt, c_xt_out, c_p, c_sq, c_v, c_ss, c_clip, c_rn, c_rq, c_rope, c_add,
         c_kn, c_t, c_kt, c_qe, c_qo, c_qk, c_tt, c_nb, c_ex, c_pt, c_pt_out, c_pv, c_ri, c_on, c_ot, c_ot_out,
         c_wo, c_res) = signals(
            "c_zero c_tab c_xs c_xt c_xt_out c_p c_sq c_v c_ss c_clip c_rn c_rq c_rope c_add c_kn c_t "
            "c_kt c_qe c_qo c_qk c_tt c_nb c_ex c_pt c_pt_out c_pv c_ri c_on c_ot c_ot_out c_wo c_res")
        (d_shift, d_stats, d_aggr, d_eps, d_rstd, d_norm, d_tp, d_tp_out, d_w1, d_gelu, d_act, d_w2, d_res0) = signals(
            "d_shift d_stats d_aggr d_eps d_rstd d_norm d_tp d_tp_out d_w1 d_gelu d_act d_w2 d_res0")
        (rope_in, wqkv_in, wo_in, wm_in, wq_hi, wq_lo, wm_copied, wm_split, c_xt_lo, d_full, d_in_hi, d_in_lo,
         d_hi) = signals(
            "rope_in wqkv_in wo_in wm_in wq_hi wq_lo wm_copied wm_split c_xt_lo d_full d_in_hi d_in_lo d_hi")
        (out_sum, out_sem) = signals("out_sum out_sem")
        (win_hi, win_lo, wg_hi, wg_split, wx_in, wx_hi, wx_lo, ctx_last, a_tp_lo, a_conv_hi, a_conv_lo, b_tp_lo,
         b_ta_lo) = signals(
            "win_hi win_lo wg_hi wg_split wx_in wx_hi wx_lo ctx_last a_tp_lo a_conv_hi a_conv_lo b_tp_lo b_ta_lo")
        w_raw = inner[:, :, :].rearrange("p n d -> p (n d)")

        C_ZERO = 3
        tiles = lambda b: bass.ts(b, TT) if not isinstance(b, int) else slice(b * TT, (b + 1) * TT)
        block = ctx.enter_context(nc.Block())
        xv = x.rearrange("b (t p) d -> p (b t) d", p=P)
        ov = out.rearrange("b (t p) d -> p (b t) d", p=P)
        cv = ctx_in.rearrange("b (t p) d -> p (b t) d", p=P)

        def wait_alone(engine, sem, value):
            engine.wait_ge(sem, value)
            if not isinstance(value, int):
                engine.nop(nofuse=True)

        @block.sync
        def _(sp):
            sp.dma_start(stream[:, 0:TT, :], xv[:, 0:TT, :]).then_inc(x0_in, 16)
            sp.dma_start(cols[:, :], cols_in).then_inc(col_in, 16)
            sp.dma_start(w_raw[:, 0:WIN_COLS], w_in.rearrange("p k n -> p (k n)")).then_inc(w1s_in, 16)
            sp.dma_start(w_raw[:, WIN_COLS:WIN_COLS + WG_COLS], w_gate.rearrange("p k n -> p (k n)"))\
                .then_inc(wg_in, 16)
            sp.dma_start(stream[:, TT:NT, :], xv[:, TT:NT, :]).then_inc(xr_in, 16)
            sp.dma_start(w_out_sb[:, :, :], w_out).then_inc(wor_in, 16)
            sp.dma_start(ew[:, :, :], pos_bias).then_inc(pos_in, 16)
            sp.dma_start(rows[:, :, :], rows_in).then_inc(rows_sem, 16)
            sp.dma_start(w_o[:, :, :], wo_x).then_inc(aft_in, 16)
            sp.dma_start(w_2[:, :, :], w2_x).then_inc(mlp_in, 16)
            sp.dma_start(lcols[:, :, :], lcols_in).then_inc(rope_in, 16)
            sp.wait_ge(win_lo, 2 * KD)
            sp.wait_ge(wg_split, KR)
            for i, src in enumerate((wq, wk, wv)):
                sp.dma_start(w_raw[:, i * KD * D:(i + 1) * KD * D], src.rearrange("p k n -> p (k n)"))\
                    .then_inc(wx_in, 16)
            sp.dma_start(w_raw[:, 3 * KD * D:3 * KD * D + KD * FH], w1_x.rearrange("p k n -> p (k n)"))\
                .then_inc(wx_in, 16)
            sp.wait_ge(a_full, 12 * (NB - 1) + 2 * KR)
            sp.dma_start(emb[:, 0:NT - TT, :], cv[:, 0:NT - TT, :]).then_inc(ctx_sem, 16)
            sp.wait_ge(a_full, 12 * NB)
            sp.dma_start(emb[:, NT - TT:NT, :], cv[:, NT - TT:NT, :]).then_inc(ctx_last, 16)

            def load_att(l):
                sp.dma_start(w_stage[:, :], wqkv[l].rearrange("p k n -> p (k n)")).then_inc(wqkv_in, 16)
                if l:
                    sp.wait_ge(c_wo, l * NT)
                sp.dma_start(wo_sb[:, :, :], wo_l[l]).then_inc(wo_in, 16)

            def load_mlp(l, b):
                sp.dma_start(w_stage[:, 0:WM_QUARTER], wm_l[l, :, b * WM_QUARTER:(b + 1) * WM_QUARTER])\
                    .then_inc(wm_in, 16)

            def shift(l, b):
                m = l * NB + b
                sp.wait_ge(c_res, l * NT + b * TT + TT)
                sp.wait_ge(d_norm, 8 * m)
                sp.dma_start(shifted[1:P, :, :], inner[0:P - 1, b * TT:(b + 1) * TT, P:D]).then_inc(d_shift, 16)
                sp.dma_start(shifted[0:1, 1:TT, :], inner[P - 1:P, b * TT:(b + 1) * TT - 1, P:D]).then_inc(d_shift, 16)

            sp.wait_ge(a_o, 2 * NB)
            sp.dma_start(rope_sb[:, :, :, :], rope).then_inc(rope_in, 16)
            sp.dma_start(qk_scale_sb[:, :, :, :], qk_scale).then_inc(rope_in, 16)
            load_att(0)
            for l in range(LAYERS):
                sp.wait_ge(wq_lo, 2 * 3 * (l + 1))
                for b in range(NB):
                    if b:
                        sp.wait_ge(wm_split, WM_PIECES * (l * NB + b))
                    load_mlp(l, b)
                shift(l, 0)
                if l < LAYERS - 1:
                    sp.wait_ge(wm_split, WM_PIECES * NB * (l + 1))
                    load_att(l + 1)
                for b in range(1, NB):
                    shift(l, b)
            for b in range(NB):
                sp.wait_ge(out_sum, b + 1)
                sp.dma_start(ov[:, b * TT:(b + 1) * TT, :], stream[:, b * TT:(b + 1) * TT, :]).then_inc(out_sem, 16)
            sp.wait_ge(out_sem, 16 * NB)

        @block.gpsimd
        def _(pool):
            pool.memset(ident[:, :], 0.0).then_inc(pool_ready, 1)
            pool.memset(minus_half[:, :], -0.5).then_inc(pool_ready, 1)
            pool.memset(raw[:, :, 0:TAPS - 1], 0.0).then_inc(pool_ready, 1)
            pool.memset(mask[:, :], 0.0).then_inc(pool_ready, 1)
            pool.memset(quarter[:, :], 0.25 * (1.0 + BETA_EPS)).then_inc(pool_ready, 1)
            pool.wait_ge(pool_ready, 5)
            pool.affine_select(out=ident[:, :], in_=ident[:, :], compare_op=ALU.not_equal, fill=1.0, base=0,
                               pattern=[[-1, P]], channel_multiplier=1).then_inc(ready_consts, 1)
            pool.affine_select(out=mask[:, :], in_=mask[:, :], compare_op=ALU.is_ge, fill=NEG, base=P,
                               pattern=[[-1, 2 * P]], channel_multiplier=1).then_inc(pool_ready, 1)
            pool.wait_ge(pool_ready, 6)
            pool.affine_select(out=mask[:, :], in_=mask[:, :], compare_op=ALU.is_ge, fill=NEG, base=0,
                               pattern=[[1, 2 * P]], channel_multiplier=-1).then_inc(ready_consts, 1)

            def rstd_of(n):
                wait_alone(pool, n_aggr, 4 * n + 4)
                pool.tensor_scalar(var_eps[:, :], mean_var[:, :, 1], 1.0, LN_EPS, ALU.mult, ALU.add)\
                    .then_inc(n_eps, 1)
                pool.wait_ge(n_eps, n + 1)
                pool.tensor_tensor(rstd[:, :], var_eps[:, :], minus_half[:, 0:TT], ALU.pow).then_inc(n_rstd, 1)

            def round_conv(b):
                for j in range(KR):
                    wait_alone(pool, a_conv, 3 * b + j + 1)
                    pool.tensor_scalar(conv_hi[:, j, :], conv[:, j, :], 1.0, 0.0, ALU.mult, ALU.add).then_inc(a_conv_hi, 1)

            rstd_of(0)
            pool.wait_ge(wg_in, 16)
            for k in range(KR):
                raw_k = w_raw[:, WIN_COLS + k * 2 * RH:WIN_COLS + (k + 1) * 2 * RH]
                pool.tensor_scalar(w_gate_hi[:, k, :], raw_k, 1.0, 0.0, ALU.mult, ALU.add).then_inc(wg_hi, 1)
                pool.wait_ge(wg_hi, k + 1)
                pool.tensor_tensor(w_gate_lo[:, k, :], raw_k, w_gate_hi[:, k, :].bitcast(F32), ALU.subtract)\
                    .then_inc(wg_split, 1)
            round_conv(0)
            pool.wait_ge(pos_in, 16)
            for n, (step, ch) in enumerate(((P, 1), (-P, -1))):
                pool.wait_ge(e_band, n)
                pool.affine_select(out=ew[:, :, :], in_=ew[:, :, :], compare_op=ALU.is_ge, fill=0.0,
                                   base=BAND - 1, pattern=[[step, TT], [-ch, T]], channel_multiplier=ch)\
                    .then_inc(e_band, 1)
            rstd_of(1)
            with pool.Fori(0, NB - 2) as b:
                round_conv(b + 1)
                rstd_of(b + 2)
            round_conv(NB - 1)

            def keep_emb(b):
                pool.wait_ge(b_emb, b + 1)
                pool.tensor_tensor(emb[:, tiles(b), :], normed[:, :, :],
                                   rows[:, R_BO:R_BO + 1, :].to_broadcast([P, TT, D]), ALU.add)\
                    .then_inc(b_embo, 1)

            def rstd_affine(i, s):
                wait_alone(pool, l_aggr, 4 * i + 4)
                pool.tensor_scalar(lveps[:, s, :], lmv[:, s, :, 1], 1.0, LN_EPS, ALU.mult, ALU.add)\
                    .then_inc(l_eps, 1)
                pool.wait_ge(l_eps, i + 1)
                pool.tensor_tensor(lrstd[:, s, :], lveps[:, s, :], minus_half[:, 0:TT], ALU.pow).then_inc(l_rstd, 1)

            def add_b2(b):
                pool.wait_ge(a_out, TT * b + TT)
                if not (isinstance(b, int) and b == 0):
                    pool.wait_ge(l_out, TT * b)
                pool.tensor_tensor(a_b2[:, :, :], a_tok[:, :, :],
                                   rows[:, R_B2:R_B2 + 1, :].to_broadcast([P, TT, D]), ALU.add).then_inc(b_ab2, 1)

            def add_out(b):
                pool.wait_ge(l_out, TT * b + TT)
                pool.tensor_tensor(stream[:, tiles(b), :], stream[:, tiles(b), :], mixed_out[:, :, :], ALU.add)\
                    .then_inc(b_x2, 1)

            pool.wait_ge(wx_in, 64)
            pieces = [(w_qkv_hi[:, i, :, :], w_qkv_lo[:, i, :, :]) for i in range(3)]
            pieces += [(w_1_hi[:, k:k + 1, h * (FH // 2):(h + 1) * (FH // 2)],
                        w_1_lo[:, k:k + 1, h * (FH // 2):(h + 1) * (FH // 2)]) for k in range(KD) for h in range(2)]

            def raw_piece(i, like):
                return w_raw[:, i * T:(i + 1) * T].rearrange("p (k n) -> p k n", k=like.shape[1])

            for i, (hi, lo) in enumerate(pieces):
                pool.tensor_scalar(hi, raw_piece(i, hi), 1.0, 0.0, ALU.mult, ALU.add).then_inc(wx_hi, 1)
            for i, (hi, lo) in enumerate(pieces[:3]):
                pool.wait_ge(wx_hi, i + 1)
                pool.tensor_tensor(lo, raw_piece(i, hi), hi.bitcast(F32), ALU.subtract).then_inc(wx_lo, 1)
            pool.wait_ge(rows_sem, 16)
            rstd_of(NB)
            keep_emb(0)
            rstd_of(NB + 1)
            keep_emb(1)
            pool.wait_ge(e_tp, TT)
            pool.wait_ge(wx_hi, len(pieces))
            for i, (hi, lo) in enumerate(pieces[3:]):
                pool.tensor_tensor(lo, raw_piece(3 + i, hi), hi.bitcast(F32), ALU.subtract).then_inc(wx_lo, 1)
            rstd_affine(0, 0)
            add_b2(0)

            def finish(b, nxt, norm2):
                if norm2:
                    rstd_of(2 * b + NB + 2)
                    keep_emb(b + 2)
                rstd_affine(2 * b + 1, 1 if norm2 else 0)
                if nxt:
                    rstd_affine(2 * b + 2, 0 if norm2 else 1)
                add_out(b)
                if nxt:
                    add_b2(b + 1)
                rstd_of(2 * b + NB + 3 if norm2 else b + 2 * NB)

            with pool.Fori(0, NB - 2) as b:
                finish(b, True, True)
            finish(NB - 2, True, False)

            def copy_tile(n, tile, par, batch_done):
                pool.wait_ge(b_res, batch_done)
                if not (isinstance(n, int) and n < 2):
                    wait_alone(pool, c_xt, n - 1)
                pool.tensor_copy(x_tile[:, par, :], inner[:, tile, :]).then_inc(c_xs, 1)

            def rotate(n, par):
                for i, dst in enumerate((q_tok, k_tok)):
                    pool.wait_ge(c_rope, 6 * n + 3 * i + 3)
                    if not (isinstance(n, int) and n < 2):
                        pool.wait_ge(c_t, 2 * n - 2)
                    pool.tensor_tensor(dst[:, par, :], rot[:, 2 * i, :], rot[:, 2 * i + 1, :], ALU.add)\
                        .then_inc(c_add, 1)

            def rnorm(n, w):
                pool.wait_ge(c_ss, n + 1)
                if not (isinstance(n, int) and n == 0):
                    wait_alone(pool, c_kn, n)
                pool.tensor_scalar(norms[:, 1, :], norms[:, 0, :], 1e-24, 1.0, ALU.max, ALU.mult).then_inc(c_clip, 1)
                pool.wait_ge(c_clip, n + 1)
                pool.tensor_tensor(norms[:, 2, :], norms[:, 1, :], minus_half[:, :], ALU.pow).then_inc(c_rn, 1)
                wait_alone(pool, c_rn, n + 1)
                pool.tensor_scalar(q_rnorm[:, w, :], norms[:, 2, 0:HEADS], QK_SCALE, 0.0, ALU.mult, ALU.add)\
                    .then_inc(c_rq, 1)

            def split_mlp_weights(l, b, piece):
                m = l * NB + b
                src = w_stage[:, piece * WM_PIECE:(piece + 1) * WM_PIECE]
                dst = bass.ds(b * WM_QUARTER + piece * WM_PIECE, WM_PIECE)
                wait_alone(pool, wm_in, 16 * m + 16)
                pool.tensor_copy(wm_hi[:, dst], src).then_inc(wm_copied, 1)
                pool.wait_ge(wm_copied, WM_PIECES * m + piece + 1)
                pool.tensor_tensor(wm_lo[:, dst], src, wm_hi[:, dst].bitcast(F32), ALU.subtract)\
                    .then_inc(wm_split, 1)

            def attention(n0, b, l, nxt):
                for w in range(TT):
                    if w == 0 or nxt:
                        copy_tile(n0 + w + 3, (b + (w + 3) // TT) * TT + (w + 3) % TT, (w + 3) % 2,
                                  l * NB + b + (w + 3) // TT + 1)
                    if w < 2 or nxt:
                        rotate(n0 + w + 2, w % 2)
                        rnorm(n0 + w + 2, (w + 2) % TT)
                    if w:
                        split_mlp_weights(l, b, w - 1)

            def mlp_rstd(m):
                wait_alone(pool, d_aggr, 4 * m + 4)
                pool.tensor_scalar(var_eps[:, :], mean_var[:, :, 1], 1.0, LN_EPS, ALU.mult, ALU.add)\
                    .then_inc(d_eps, 1)
                pool.wait_ge(d_eps, m + 1)
                pool.tensor_tensor(rstd[:, :], var_eps[:, :], minus_half[:, 0:TT], ALU.pow).then_inc(d_rstd, 1)

            pool.wait_ge(b_ta, KD * NB)
            pool.memset(x_hi[:, T:T + 1].bitcast(F32), 0.0).then_inc(c_zero, 1)
            pool.memset(x_lo[:, T:T + 1].bitcast(F32), 0.0).then_inc(c_zero, 1)
            copy_tile(0, 0, 0, 1)
            copy_tile(1, 1, 1, 1)
            pool.memset(q_heads[:, :, :], 0.0).then_inc(c_zero, 1)
            rotate(0, 0)
            rnorm(0, 0)
            copy_tile(2, 2, 0, 1)
            rstd_affine(2 * NB - 1, 1)
            add_out(NB - 1)
            rotate(1, 1)
            rstd_of(3 * NB - 1)
            rnorm(1, 1)
            pool.wait_ge(c_rq, 2)
            pool.memset(last_hi[32:64, :].bitcast(F32), 1.0).then_inc(c_zero, 1)
            pool.wait_ge(c_zero, 4)
            pool.memset(last_lo[32:64, :].bitcast(F32), 0.0).then_inc(c_zero, 1)
            pool.wait_ge(c_zero, 5)
            pool.memset(shifted[0:1, 0, :], 0.0).then_inc(c_zero, 1)
            wait_alone(pool, c_zero, 6)
            for l in range(LAYERS):
                n0 = l * NT
                with pool.Fori(0, NB - 1) as b:
                    attention(n0 + b * TT, b, l, True)
                attention(n0 + (NB - 1) * TT, NB - 1, l, False)
                mlp_rstd(l * NB)
                with pool.Fori(0, NB - 1) as b:
                    mlp_rstd(l * NB + b + 1)
                if l < LAYERS - 1:
                    for w in range(3):
                        copy_tile(n0 + NT + w, w, w % 2, (l + 1) * NB + 1)
                    for w in range(2):
                        rotate(n0 + NT + w, w)
                        rnorm(n0 + NT + w, w)
            for b in range(NB):
                pool.wait_ge(b_res, NB * LAYERS + b + 1)
                pool.tensor_tensor(stream[:, tiles(b), :], stream[:, tiles(b), :], inner[:, tiles(b), :], ALU.add)\
                    .then_inc(out_sum, 1)

        @block.vector
        def _(dve):
            def norm_stats(n, b):
                for t in range(TT):
                    dve.bn_stats(stats[:, t, 0:6], stream[:, b * TT + t, :]).then_inc(n_stats, 1)
                for t in range(TT):
                    wait_alone(dve, n_stats, 4 * n + t + 1)
                    dve.bn_aggr(mean_var[:, t, :], stats[:, t, 0:6]).then_inc(n_aggr, 1)

            def norm_apply(n, b, to_inner):
                dve.wait_ge(n_rstd, n + 1)
                for t in range(TT):
                    dst = inner[:, b * TT + t, :] if to_inner else normed[:, t, :]
                    ins = dve.tensor_scalar(dst, stream[:, b * TT + t, :], mean_var[:, t, 0:1],
                                            rstd[:, t:t + 1], ALU.subtract, ALU.mult)
                    if not to_inner:
                        ins.then_inc(n_norm, 1)
                    elif t == TT - 1:
                        ins.then_inc(b_res, 1)

            def norm(n, b, to_inner=False):
                norm_stats(n, b)
                norm_apply(n, b, to_inner)

            def conv_low(b, j):
                dve.wait_ge(a_conv_hi, 3 * b + j + 1)
                dve.tensor_tensor(conv_lo[:, j, :], conv[:, j, :], conv_hi[:, j, :].bitcast(F32), ALU.subtract)\
                    .then_inc(a_conv_lo, 1)

            def conv_taps(b):
                for j in range(KR):
                    dve.wait_ge(a_tap0, 3 * b + j + 1)
                    for k in range(1, TAPS):
                        ins = dve.scalar_tensor_tensor(
                            conv[:, j, :], raw[:, j, TAPS - 1 - k:TAPS - 1 - k + T],
                            cols[:, C_CONVW + TAPS * j + TAPS - 1 - k:C_CONVW + TAPS * j + TAPS - k],
                            conv[:, j, :], ALU.mult, ALU.add)
                        if k < TAPS - 1:
                            ins.then_inc(a_tap, 1)
                            dve.wait_ge(a_tap, 6 * b + 2 * j + k)
                        else:
                            ins.then_inc(a_conv, 1)
                    if j:
                        conv_low(b, j - 1)
                conv_low(b, KR - 1)

            def low_part(b, out, done):
                for c in range(KD):
                    dve.wait_ge(out, KD * b + c + 1)
                    dve.tensor_tensor(t_lo[:, c, :], bank[c][:, :], t_hi[:, c, :].bitcast(F32), ALU.subtract)\
                        .then_inc(done, 1)

            def gated_input(b, j):
                dve.wait_ge(a_th, 3 * b + j + 1)
                dve.scalar_tensor_tensor(th_in[:, j, :], th_in[:, j, :], 1.0, conv[:, j, :], ALU.add,
                                         ALU.mult).then_inc(a_xs0, 1)

            def recurrence(b):
                dve.wait_ge(a_beta, b + 1)
                for j in range(KR):
                    dve.wait_ge(a_xs0, 3 * b + j + 1)
                    dve.tensor_tensor(th_in[:, j, :], th_in[:, j, :], beta[:, j, :], ALU.mult).then_inc(a_xs, 1)
                if not (isinstance(b, int) and b == 0):
                    dve.wait_ge(a_o, 2 * b)
                for j in range(KR):
                    dve.wait_ge(a_xs, 3 * b + j + 1)
                    dve.tensor_tensor_scan(scanned[:, j, :], alpha[:, j, :], th_in[:, j, :], 0.0, ALU.mult,
                                           ALU.add).then_inc(a_scan, 1)
                dve.wait_ge(a_gelu, 3 * b + 3)
                for j in range(KR):
                    dve.wait_ge(a_scan, 3 * b + j + 1)
                    dve.tensor_tensor(scanned[:, j, :], scanned[:, j, :], gate_act[:, b % 2, j, :], ALU.mult)\
                        .then_inc(a_gh, 1)

            def residual(b):
                for h in range(2):
                    dve.wait_ge(a_o, 2 * b + h + 1)
                    s = stream[:, bass.ds(b * TT + 2 * h, 2), :]
                    dve.tensor_tensor(s, s, bank[6 + h][:, :].rearrange("p (t d) -> p t d", t=2), ALU.add)\
                        .then_inc(a_res, 1)

            def embed(b, n):
                dve.wait_ge(a_res, 2 * b + 2)
                if isinstance(b, int) and b == 0:
                    dve.wait_ge(a_tp, 2 * NB)
                else:
                    dve.wait_ge(b_tp, 2 * b)
                    dve.wait_ge(b_embo, b)
                norm(n, b)
                dve.wait_ge(n_norm, 4 * (NB + b) + 4)
                dve.tensor_tensor(normed[:, :, :], normed[:, :, :], emb[:, tiles(b), :], ALU.add).then_inc(b_emb, 1)

            def keys_values(b):
                for m in range(KD):
                    dve.wait_ge(b_full, 6 * b + m + 1)
                    dve.tensor_reduce(kstat[:, m, 0:1], bank[2 + m][:, :], AX_X, ALU.max).then_inc(b_kmax, 1)
                for m in range(KD):
                    bk = cols[:, C_BK + m:C_BK + m + 1]
                    dve.wait_ge(b_kmax, 4 * b + m + 1)
                    dve.tensor_scalar(kstat[:, m, 1:2], kstat[:, m, 0:1], bk, -1.0, ALU.add, ALU.mult)\
                        .then_inc(b_kmax, 1)
                for m in range(KD):
                    dve.wait_ge(b_kmax, 4 * b + 2 + m + 1)
                    dve.tensor_scalar(kstat[:, m, 2:3], kstat[:, m, 1:2], cols[:, C_BK + m:C_BK + m + 1], None,
                                      ALU.add).then_inc(b_kbias, 1)
                for m in range(KD):
                    dve.wait_ge(b_full, 6 * b + 2 + m + 1)
                    dve.wait_ge(b_ek, 2 * b + m + 1)
                    dve.scalar_tensor_tensor(ekv[:, m, :], bank[4 + m][:, :], cols[:, C_BV + m:C_BV + m + 1],
                                             ek[:, m, :], ALU.add, ALU.mult).then_inc(b_ekv, 1)

            def gated_ratio(b):
                for m in range(KD):
                    den, num = bank[2 + (2 * m + 2) % 4], bank[2 + (2 * m + 3) % 4]
                    dve.wait_ge(b_aft, 4 * b + 2 * m + 1)
                    dve.scalar_tensor_tensor(y[:, m, :], eq[:, m, :], 1.0, den[:, :], ALU.add, ALU.mult)\
                        .then_inc(b_den, 1)
                    dve.wait_ge(b_den, 2 * b + m + 1)
                    dve.reciprocal(y[:, m, :], y[:, m, :]).then_inc(b_rec, 1)
                    dve.wait_ge(b_rec, 2 * b + m + 1)
                    dve.wait_ge(b_aft, 4 * b + 2 * m + 2)
                    dve.tensor_tensor(y[:, m, :], y[:, m, :], num[:, :], ALU.mult).then_inc(b_y, 1)

            def lstat(i, s, src, done, of):
                for t in range(TT):
                    dve.wait_ge(done, of + t // 2 + 1)
                    dve.bn_stats(lstats[:, s, t, :], src[:, t, :]).then_inc(l_stats, 1)
                for t in range(TT):
                    wait_alone(dve, l_stats, 4 * i + t + 1)
                    dve.bn_aggr(lmv[:, s, t, :], lstats[:, s, t, :]).then_inc(l_aggr, 1)

            def norm_affine(i, s, src, dst, order, done):
                for t in range(TT):
                    dve.wait_ge(l_aggr, 4 * i + t + 1)
                    dve.scalar_tensor_tensor(src[:, t, :], src[:, t, :], lmv[:, s, t, 0:1], rows[:, R_GAMMA, :],
                                             ALU.subtract, ALU.mult).then_inc(l_mid, 1)
                dve.wait_ge(l_rstd, i + 1)
                for t in range(TT):
                    dve.wait_ge(l_mid, 4 * order + t + 1)
                    dve.scalar_tensor_tensor(dst[:, t, :], src[:, t, :], lrstd[:, s, t:t + 1], rows[:, R_BETA, :],
                                             ALU.mult, ALU.add).then_inc(done, 1)

            def mixed(b, i, at=6):
                dve.wait_ge(b_embo, b + 1)
                for h in range(2):
                    dve.wait_ge(b_o, 2 * b + h + 1)
                    dve.tensor_tensor(mix[:, 2 * h:2 * h + 2, :], emb[:, bass.ds(b * TT + 2 * h, 2), :],
                                      bank[at + h][:, :].rearrange("p (t d) -> p t d", t=2), ALU.add)\
                        .then_inc(b_mix, 1)
                lstat(i, 0, mix, b_mix, 2 * b)

            def to_a(b, i, order):
                dve.wait_ge(b_ab2, b)
                dve.wait_ge(b_ta, 2 * b)
                norm_affine(i, 0, mix, a_tok, order, a_out)

            def add_mlp(b, h):
                dve.wait_ge(b_f2, 2 * b + h + 1)
                dve.tensor_tensor(a_b2[:, 2 * h:2 * h + 2, :], a_b2[:, 2 * h:2 * h + 2, :],
                                  bank[6 + h][:, :].rearrange("p (t d) -> p t d", t=2), ALU.add)\
                    .then_inc(b_sum, 1)

            dve.wait_ge(x0_in, 16)
            dve.wait_ge(ready_consts, 2)
            norm(0, 0)
            for i, (half, k) in enumerate(((h, k) for h in (1, 0) for k in range(KD))):
                part = slice(half * RH, (half + 1) * RH)
                dve.wait_ge(win_hi, i + 1)
                dve.tensor_tensor(w_in_lo[:, k, part], w_raw[:, 0:WIN_COLS].rearrange("p (k n) -> p k n", k=KD)[:, k, part],
                                  w_in_hi[:, k, part].bitcast(F32), ALU.subtract).then_inc(win_lo, 1)
                if i == 1:
                    low_part(0, a_tp_out, a_tp_lo)
            dve.wait_ge(col_in, 16)
            dve.tensor_scalar(fb_tmp[:, 2, :], cols[:, C_FB:C_FB + KR], 0.0, None, ALU.max).then_inc(fb_vec, 1)
            dve.tensor_scalar(half_bf[:, :], cols[:, C_BG:C_BG + 2 * KR], 0.5, None, ALU.mult).then_inc(fb_vec, 1)
            dve.wait_ge(fb_step, 3)
            dve.wait_ge(fb_vec, 1)
            dve.tensor_tensor(fb_tmp[:, 2, :], fb_tmp[:, 2, :], fb_tmp[:, 0, :], ALU.add).then_inc(fb_vec, 1)
            dve.wait_ge(fb_vec, 3)
            dve.tensor_scalar(m4sp[:, :], fb_tmp[:, 2, :], -4.0, None, ALU.mult).then_inc(fb_vec, 1)
            conv_taps(0)
            dve.wait_ge(xr_in, 16)
            dve.wait_ge(a_tp, 2)
            norm(1, 1)
            dve.wait_ge(e_band, 2)
            dve.tensor_reduce(ew_stat[:, :, 0], ew[:, :, :], AX_X, ALU.max).then_inc(e_max, 1)
            dve.wait_ge(e_max, 1)
            dve.tensor_scalar(ew_stat[:, :, 1], ew_stat[:, :, 0], -1.0, None, ALU.mult).then_inc(e_neg, 1)

            def recur(b, prev, norm2):
                for j in range(KR):
                    gated_input(b, j)
                conv_taps(b + 1)
                recurrence(b)
                if norm2:
                    dve.wait_ge(a_tp, 2 * b + 4)
                    norm(b + 2, b + 2)
                if prev:
                    residual(b - 1)
                if norm2:
                    low_part(b + 2, a_tp_out, a_tp_lo)

            low_part(1, a_tp_out, a_tp_lo)
            recur(0, False, True)

            with dve.Fori(1, NB - 2) as b:
                recur(b, True, True)
            recur(NB - 2, True, False)
            dve.wait_ge(ctx_sem, 16)
            embed(0, NB)
            for j in range(KR):
                gated_input(NB - 1, j)
            residual(NB - 2)
            low_part(0, b_tp_out, b_tp_lo)
            recurrence(NB - 1)
            keys_values(0)
            residual(NB - 1)
            dve.wait_ge(ctx_last, 16)
            embed(1, NB + 1)
            dve.wait_ge(rows_sem, 16)
            gated_ratio(0)
            low_part(1, b_tp_out, b_tp_lo)
            mixed(0, 0)
            to_a(0, 0, 0)

            def a_low(b):
                for c in range(KD):
                    dve.wait_ge(b_ta_out, KD * b + c + 1)
                    dve.tensor_tensor(a_lo[:, c, :], bank[2 + c][:, :], a_hi[:, c, :].bitcast(F32), ALU.subtract)\
                        .then_inc(b_ta_lo, 1)

            keys_values(1)
            a_low(0)
            dve.wait_ge(wx_lo, 7)
            gated_ratio(1)

            def mixing(b, norm2):
                if norm2:
                    embed(b + 2, 2 * b + NB + 2)
                    dve.wait_ge(b_ab2, b + 1)
                    add_mlp(b, 0)
                    add_mlp(b, 1)
                    lstat(2 * b + 1, 1, a_b2, b_sum, 2 * b)
                    low_part(b + 2, b_tp_out, b_tp_lo)
                    mixed(b + 1, 2 * b + 2)
                    to_a(b + 1, 2 * b + 2, 2 * b + 1)
                    keys_values(b + 2)
                    a_low(b + 1)
                else:
                    mixed(b + 1, 2 * b + 1, 0)
                    to_a(b + 1, 2 * b + 1, 2 * b + 1)
                    dve.wait_ge(b_ab2, b + 1)
                    add_mlp(b, 0)
                    a_low(b + 1)
                    add_mlp(b, 1)
                    lstat(2 * b + 2, 1, a_b2, b_sum, 2 * b)
                dve.wait_ge(b_x2, b)
                norm_affine(2 * b + 1 if norm2 else 2 * b + 2, 1, a_b2, mixed_out, 2 * b + 2, l_out)
                dve.wait_ge(b_x2, b + 1)
                norm(2 * b + NB + 3 if norm2 else b + 2 * NB, b, to_inner=True)
                if norm2:
                    gated_ratio(b + 2)

            with dve.Fori(0, NB - 2) as b:
                mixing(b, True)
            mixing(NB - 2, False)

            def tables(l):
                for i in range(4):
                    s = qk_scale_sb[:, l, i // 2, :].unsqueeze(1)
                    src = rope_sb[:, i, :, :]
                    dst = rope_l[:, i, :, :]
                    if i % 2:
                        for lo, other in ((0, DH // 2), (DH // 2, 0)):
                            dve.tensor_tensor(dst[:, :, lo:lo + DH // 2], src[:, :, lo:lo + DH // 2],
                                              s[:, :, other:other + DH // 2].to_broadcast([P, TT, DH // 2]),
                                              ALU.mult).then_inc(c_tab, 1)
                    else:
                        dve.tensor_tensor(dst, src, s.to_broadcast([P, TT, DH]), ALU.mult).then_inc(c_tab, 1)

            def rope_products(n, w, i):
                src = bank[i][:, :].rearrange("p (h d) -> p h d", d=DH)
                dve.wait_ge(c_sq, 2 * n + i + 1)
                if not (isinstance(n, int) and n == 0):
                    dve.wait_ge(c_add, 2 * n - 1 + i)
                cos = rope_l[:, 2 * i, w:w + 1, :].to_broadcast([P, HEADS, DH])
                dve.tensor_tensor(rot[:, 2 * i, :].rearrange("p (h d) -> p h d", d=DH), src, cos, ALU.mult)\
                    .then_inc(c_rope, 1)
                rotated = rot[:, 2 * i + 1, :].rearrange("p (h d) -> p h d", d=DH)
                for lo, other in ((0, DH // 2), (DH // 2, 0)):
                    sin = rope_l[:, 2 * i + 1, w:w + 1, lo:lo + DH // 2].to_broadcast([P, HEADS, DH // 2])
                    dve.tensor_tensor(rotated[:, :, lo:lo + DH // 2], src[:, :, other:other + DH // 2], sin,
                                      ALU.mult).then_inc(c_rope, 1)

            def sum_squares(n):
                dve.wait_ge(c_sq, 2 * n + 2)
                dve.wait_ge(c_clip, n)
                dve.tensor_reduce(norms[:, 0, :], squares[:, :, :].rearrange("p i (h d) -> p (i h) d", d=DH), AX_X,
                                  ALU.add).then_inc(c_ss, 1)

            def norm_keys(n, par):
                dve.wait_ge(c_add, 2 * n + 2)
                dve.wait_ge(c_rn, n + 1)
                k = k_tok[:, par, :].rearrange("p (h d) -> p h d", d=DH)
                dve.tensor_tensor(k, k, norms[:, 2, HEADS:2 * HEADS].unsqueeze(2).to_broadcast([P, HEADS, DH]),
                                  ALU.mult).then_inc(c_kn, 1)

            def q_odd(n):
                dve.wait_ge(c_t, 2 * n + 2)
                dve.tensor_copy(q_heads[64:128, :, :].rearrange("p (c e) t -> p e c t", e=2)[:, 1, :, :],
                                bank[2][64:128, :].rearrange("p (c t) -> p c t", t=P)).then_inc(c_qo, 1)

            def masked(n, w, i, first=False):
                u = 4 * n + i
                nk = 2 * P if w else P
                if not (isinstance(u, int) and u < 2):
                    dve.wait_ge(c_ex, 2 * u - 2)
                wait_alone(dve, c_qk, u + 1)
                for e in range(2):
                    dve.tensor_tensor_reduce(scores[:, i % 2, e, 0:nk], bank[6 + i % 2][:, e * 2 * P:e * 2 * P + nk],
                                             mask[:, 2 * P - nk:2 * P], 1.0, NEG, ALU.add, ALU.max,
                                             row_max[:, w % 2, 2 * i + e:2 * i + e + 1]).then_inc(c_tt, 1)
                dve.wait_ge(c_tt, 2 * u + 2)
                dve.wait_ge(c_rq, n + 1)
                dve.scalar_tensor_tensor(row_bias[:, w % 2, 2 * i:2 * i + 2], row_max[:, w % 2, 2 * i:2 * i + 2],
                                         -1.0, q_rnorm[:, w, 2 * i:2 * i + 2], ALU.mult, ALU.mult).then_inc(c_nb, 1)

            def normalise(n, w):
                dve.wait_ge(c_ex, 8 * n + 8)
                dve.reciprocal(row_rsum[:, :], row_sum[:, w % 2, :]).then_inc(c_ri, 1)
                dve.wait_ge(c_ri, n + 1)
                dve.wait_ge(c_pv, 4 * n + 4)
                dve.tensor_tensor(o_tok[:, :].rearrange("p (h d) -> p h d", d=DH),
                                  bank[3][:, :].rearrange("p (h d) -> p h d", d=DH),
                                  row_rsum[:, :].unsqueeze(2).to_broadcast([P, HEADS, DH]), ALU.mult)\
                    .then_inc(c_on, 1)

            def o_transposed(n):
                dve.wait_ge(c_ot, n + 1)
                dve.tensor_copy(o_t[:, :, :].rearrange("p c t -> p (c t)"), bank[2][:, :]).then_inc(c_ot_out, 1)

            def att_residual(n, tile):
                dve.wait_ge(c_wo, n + 1)
                dve.tensor_tensor(inner[:, tile, :], inner[:, tile, :], bank[2][:, 0:D], ALU.add).then_inc(c_res, 1)

            def attention(n0, b, l, nxt):
                for w in range(TT):
                    n = n0 + w
                    two, one = (w < 2 or nxt), (w < 3 or nxt)
                    if w:
                        o_transposed(n - 1)
                    if not two:
                        if w == 2:
                            mlp_stats(l * NB, 0, 0)
                            mlp_stats(l * NB, 0, 1)
                        else:
                            mlp_aggr(l * NB)
                    if one:
                        norm_keys(n + 1, (w + 1) % 2)
                    if two:
                        rope_products(n + 2, (w + 2) % TT, 0)
                    masked(n, w, 2)
                    if two:
                        rope_products(n + 2, (w + 2) % TT, 1)
                    if w:
                        att_residual(n - 1, b * TT + w - 1)
                    if not two and w == 2:
                        mlp_stats(l * NB, 0, 2)
                        mlp_stats(l * NB, 0, 3)
                    masked(n, w, 3)
                    if not two and w == 3:
                        mlp_norm(l * NB, 0)
                    if w < 1 or nxt:
                        x_low(n + 3, (w + 3) % TT, bank[1][:, 0:D])
                    if two:
                        sum_squares(n + 2)
                    if one:
                        q_odd(n + 1)
                    normalise(n, w)
                    if one:
                        masked(n + 1, (w + 1) % TT, 0)
                        masked(n + 1, (w + 1) % TT, 1)
                    else:
                        input_low(l * NB)
                    if w == TT - 1:
                        o_transposed(n)
                        att_residual(n, b * TT + w)

            def x_low(n, w, src):
                dve.wait_ge(c_xt_out, n + 1)
                columns = slice(w * P, (w + 1) * P)
                dve.tensor_tensor(x_lo[:, :].rearrange("p (c t) -> p c t", t=T + 1)[:, :, columns],
                                  src.rearrange("p (c t) -> p c t", t=P),
                                  x_hi[:, :].bitcast(F32).rearrange("p (c t) -> p c t", t=T + 1)[:, :, columns],
                                  ALU.subtract).then_inc(c_xt_lo, 1)

            def mlp_stats(m, b, t):
                dve.wait_ge(d_shift, 32 * m + 32)
                for i, src in enumerate((inner[:, b * TT + t, 0:P], shifted[:, t, :])):
                    dve.bn_stats(stats[:, t, 6 * i:6 * i + 6], src).then_inc(d_stats, 1)

            def mlp_aggr(m):
                for t in range(TT):
                    wait_alone(dve, d_stats, 8 * m + 2 * t + 2)
                    dve.bn_aggr(mean_var[:, t, :], stats[:, t, :]).then_inc(d_aggr, 1)

            def mlp_norm(m, b):
                dve.wait_ge(d_rstd, m + 1)
                dve.wait_ge(d_tp, 2 * m)
                for t in range(TT):
                    for i, src in enumerate((inner[:, b * TT + t, 0:P], shifted[:, t, :])):
                        dve.tensor_scalar(normed[:, t, i * P:(i + 1) * P], src, mean_var[:, t, 0:1],
                                          rstd[:, t:t + 1], ALU.subtract, ALU.mult).then_inc(d_norm, 1)

            def input_low(m):
                for c in range(KD):
                    dve.wait_ge(d_in_hi, 2 * m + c + 1)
                    dve.tensor_tensor(t_lo[:, c, :], h_t[:, c, :], t_hi[:, c, :].bitcast(F32), ALU.subtract)\
                        .then_inc(d_in_lo, 1)

            def split_qkv(l, i):
                for k in range(KD):
                    part = slice(i * INNER, (i + 1) * INNER)
                    dve.wait_ge(wq_hi, 6 * l + 2 * i + k + 1)
                    dve.tensor_tensor(wqkv_lo[:, k, part], w_stage[:, :].rearrange("p (k n) -> p k n", k=KD)[:, k, part],
                                      wqkv_hi[:, k, part].bitcast(F32), ALU.subtract).then_inc(wq_lo, 1)

            def ahead(l, step):
                n0 = l * NT
                if step == 0:
                    tables(l)
                elif step == 1:
                    split_qkv(l, 0)
                elif step == 2:
                    for w in range(2):
                        x_low(n0 + w, w, bank[w][:, 0:D])
                    split_qkv(l, 1)
                elif step == 3:
                    split_qkv(l, 2)
                elif step == 4:
                    dve.wait_ge(c_tab, 6 * l + 6)
                    rope_products(n0, 0, 0)
                elif step == 5:
                    rope_products(n0, 0, 1)
                    sum_squares(n0)
                elif step == 6:
                    norm_keys(n0, 0)
                    rope_products(n0 + 1, 1, 0)
                elif step == 7:
                    rope_products(n0 + 1, 1, 1)
                    sum_squares(n0 + 1)
                else:
                    q_odd(n0)
                    x_low(n0 + 2, 2, bank[1][:, 0:D])

            def mlp(m, b, l, nxt):
                def low(j):
                    r = P if j < KH - 1 else HLAST
                    hi, lo = (hidden_hi[:, j, :], hidden_lo[:, j, :]) if j < KH - 1 else (last_hi, last_lo)
                    dve.wait_ge(d_hi, KH * m + j + 1)
                    dve.tensor_tensor(lo[0:r, :], hidden[0:r, j % 2, :], hi[0:r, :].bitcast(F32), ALU.subtract)\
                        .then_inc(d_act, 1)

                for j in range(KH):
                    r = P if j < KH - 1 else HLAST
                    dve.wait_ge(d_w1, 2 * (KH * m + j) + 2)
                    dve.wait_ge(d_gelu, KH * m + j + 1)
                    dve.scalar_tensor_tensor(hidden[0:r, j % 2, :], bank[3 + 2 * (j % 2)][0:r, :],
                                             lcols[0:r, l, L_B1A + j:L_B1A + j + 1], hidden[0:r, j % 2, :], ALU.add,
                                             ALU.mult).then_inc(d_full, 1)
                    if j:
                        low(j - 1)
                    if nxt:
                        if j < TT:
                            mlp_stats(m + 1, b + 1, j)
                        if j == TT:
                            mlp_aggr(m + 1)
                    elif l < LAYERS - 1 and j < 4:
                        ahead(l + 1, j)
                low(KH - 1)
                if nxt:
                    mlp_norm(m + 1, b + 1)
                    input_low(m + 1)
                elif l < LAYERS - 1:
                    ahead(l + 1, 4)
                    ahead(l + 1, 5)
                for h in range(2):
                    if h and not nxt and l < LAYERS - 1:
                        ahead(l + 1, 6)
                    dve.wait_ge(d_w2, TT * m + 2 * h + 2)
                    s = inner[:, bass.ds(b * TT + 2 * h, 2), :]
                    dve.tensor_tensor(s, s, bank[6 + h][:, :].rearrange("p (t d) -> p t d", t=2), ALU.add)\
                        .then_inc((d_res0, b_res)[h], 1)

            dve.wait_ge(rope_in, 48)
            dve.wait_ge(b_ta, KD * NB)
            for step in range(4):
                ahead(0, step)
            dve.wait_ge(b_ab2, NB)
            ahead(0, 4)
            add_mlp(NB - 1, 0)
            ahead(0, 5)
            add_mlp(NB - 1, 1)
            lstat(2 * NB - 1, 1, a_b2, b_sum, 2 * NB - 2)
            ahead(0, 6)
            dve.wait_ge(b_x2, NB - 1)
            norm_affine(2 * NB - 1, 1, a_b2, mixed_out, 2 * NB - 1, l_out)
            for l in range(LAYERS):
                n0 = l * NT
                ahead(l, 7)
                if l == 0:
                    dve.wait_ge(c_zero, C_ZERO)
                ahead(l, 8)
                if l == 0:
                    dve.wait_ge(b_x2, NB)
                    norm_stats(3 * NB - 1, NB - 1)
                masked(n0, 0, 0)
                masked(n0, 0, 1)
                if l == 0:
                    norm_apply(3 * NB - 1, NB - 1, True)
                with dve.Fori(0, NB - 1) as b:
                    attention(n0 + b * TT, b, l, True)
                attention(n0 + (NB - 1) * TT, NB - 1, l, False)
                with dve.Fori(0, NB - 1) as b:
                    mlp(l * NB + b, b, l, True)
                mlp(l * NB + NB - 1, NB - 1, l, False)

        @block.scalar
        def _(act):
            def transposed_out(b):
                for c in range(KD):
                    act.wait_ge(a_tp, 2 * b + c + 1)
                    act.activation(t_hi[:, c, :], bank[c][:, :], ACT.Copy).then_inc(a_tp_out, 1)

            def taps(b):
                for j in range(KR):
                    src = bank[2 + j % 4]
                    act.wait_ge(a_full, 12 * b + j + 1)
                    act.activation(raw[:, j, TAPS - 1:TAPS - 1 + T], src[:, :], ACT.Copy)
                    act.activation(conv[:, j, :], src[:, :], ACT.Identity,
                                   bias=cols[:, C_CONVB + j:C_CONVB + j + 1],
                                   scale=cols[:, C_CONVW + TAPS * j + TAPS - 1:C_CONVW + TAPS * j + TAPS])\
                        .then_inc(a_tap0, 1)

            def gelu_gate(b):
                for j in range(KR):
                    act.wait_ge(a_full, 12 * b + KR + j + 1)
                    act.activation(gate_act[:, b % 2, j, :], bank[2 + (KR + j) % 4][:, :], ACT.Gelu).then_inc(a_gelu, 1)

            act.wait_ge(w1s_in, 16)
            for half in (1, 0):
                for k in range(KD):
                    part = slice(half * RH, (half + 1) * RH)
                    act.activation(w_in_hi[:, k, part], w_raw[:, 0:WIN_COLS].rearrange("p (k n) -> p k n", k=KD)[:, k, part],
                                   ACT.Copy).then_inc(win_hi, 1)
                if half:
                    transposed_out(0)
            act.wait_ge(col_in, 16)
            act.activation(minus_bq[:, :], cols[:, C_BQ:C_BQ + KD], ACT.Copy, scale=-1.0)
            act.activation(fb_tmp[:, 0, :], cols[:, C_FB:C_FB + KR], ACT.Abs).then_inc(fb_step, 1)
            act.wait_ge(fb_step, 1)
            act.activation(fb_tmp[:, 1, :], fb_tmp[:, 0, :], ACT.Exp, scale=-1.0).then_inc(fb_step, 1)
            act.wait_ge(fb_step, 2)
            act.activation(fb_tmp[:, 0, :], fb_tmp[:, 1, :], ACT.Ln, bias=1.0).then_inc(fb_step, 1)
            taps(0)
            gelu_gate(0)
            act.wait_ge(fb_vec, 4)

            def gates(b, nxt):
                act.wait_ge(a_scan, 3 * b)
                for j in range(KR):
                    act.wait_ge(a_full, 12 * b + 6 + 2 * j + 1)
                    act.activation(beta[:, j, :], bank[2 + (2 * j + 2) % 4][:, :], ACT.Tanh,
                                   bias=half_bf[:, j:j + 1], scale=0.5).then_inc(a_thf, 1)
                    act.wait_ge(a_full, 12 * b + 6 + 2 * j + 2)
                    act.activation(th_in[:, j, :], bank[2 + (2 * j + 3) % 4][:, :], ACT.Tanh,
                                   bias=half_bf[:, KR + j:KR + j + 1], scale=0.5).then_inc(a_th, 1)
                    act.wait_ge(a_thf, 3 * b + j + 1)
                    act.activation(alpha[:, j, :], beta[:, j, :], ACT.Exp, bias=m4sp[:, j:j + 1],
                                   scale=m4sp[:, j:j + 1]).then_inc(a_exp, 1)
                    if j == 1 and nxt:
                        transposed_out(b + 1)

            def betas(b):
                for j in range(KR):
                    act.wait_ge(a_exp, 3 * b + j + 1)
                    act.activation(beta[:, j, :], alpha[:, j, :], ACT.Square).then_inc(a_sq, 1)
                act.wait_ge(a_sq, 3 * b + 3)
                act.activation(beta[:, :, :], beta[:, :, :], ACT.Sqrt, bias=quarter[:, 0:1], scale=-0.25)\
                    .then_inc(a_beta, 1)

            with act.Fori(0, NB - 1) as b:
                gates(b, True)
                act.wait_ge(a_xs0, 3 * b + 3)
                taps(b + 1)
                betas(b)
                gelu_gate(b + 1)
            act.wait_ge(e_neg, 1)
            for t in range(TT):
                act.activation(ew[:, t, :], ew[:, t, :], ACT.Exp, bias=ew_stat[:, t, 1:2]).then_inc(e_exp, 1)
            gates(NB - 1, False)
            betas(NB - 1)

            def bias_transposed(j):
                act.wait_ge(e_tp, j + 1)
                act.activation(ew_t[:, j, :], bank[6 + j % 2][:, :], ACT.Copy).then_inc(e_tp_out, 1)

            def transposed_emb(b):
                for c in range(KD):
                    act.wait_ge(b_tp, 2 * b + c + 1)
                    act.activation(t_hi[:, c, :], bank[c][:, :], ACT.Copy).then_inc(b_tp_out, 1)

            def exps(b):
                for m in range(KD):
                    act.wait_ge(b_kbias, 2 * b + m + 1)
                    act.activation(ek[:, m, :], bank[2 + m][:, :], ACT.Exp, bias=kstat[:, m, 2:3]).then_inc(b_ek, 1)
                    if m:
                        exp_q(b, 0)

            def exp_q(b, m):
                act.wait_ge(b_full, 6 * b + 4 + m + 1)
                act.activation(eq[:, m, :], bank[m][:, :], ACT.Exp, bias=minus_bq[:, m:m + 1], scale=-1.0)\
                    .then_inc(b_eq, 1)

            def by_token(b):
                for i, dst in enumerate((ek_tok, ek_tok, ekv_tok, ekv_tok)):
                    h = i % 2
                    act.wait_ge(b_tk, 4 * b + i + 1)
                    act.activation(dst[:, 2 * h:2 * h + 2, :],
                                   bank[2 + (2 + i) % 4][:, :].rearrange("p (t d) -> p t d", t=2), ACT.Copy)\
                        .then_inc(b_tk_out, 1)

            def a_transposed(b):
                for c in range(KD):
                    act.wait_ge(b_ta, 2 * b + c + 1)
                    act.activation(a_hi[:, c, :], bank[2 + c][:, :], ACT.Copy).then_inc(b_ta_out, 1)

            def mlp_x(b):
                for c in range(KF):
                    act.wait_ge(b_f1, KF * b + c + 1)
                    act.activation(ff[:, c, :], bank[2 + (2 + c) % 4][:, :], ACT.Relu,
                                   bias=cols[:, C_B1 + c:C_B1 + c + 1]).then_inc(b_relu, 1)

            bias_transposed(0)
            bias_transposed(1)
            transposed_emb(0)
            bias_transposed(2)
            bias_transposed(3)
            exps(0)
            exp_q(0, 1)
            by_token(0)
            transposed_emb(1)

            def mixing(b, norm2):
                exps(b + 1)
                a_transposed(b)
                exp_q(b + 1, 1)
                mlp_x(b)
                by_token(b + 1)
                if norm2:
                    transposed_emb(b + 2)

            with act.Fori(0, NB - 2) as b:
                mixing(b, True)
            mixing(NB - 2, False)
            a_transposed(NB - 1)
            mlp_x(NB - 1)

            def x_transposed(n, w, src):
                act.wait_ge(c_xt, n + 1)
                act.activation(x_hi[:, :].rearrange("p (c t) -> p c t", t=T + 1)[:, :, w * P:(w + 1) * P],
                               src.rearrange("p (c t) -> p c t", t=P), ACT.Copy)\
                    .then_inc(c_xt_out, 1)

            def square(n, i):
                act.wait_ge(c_p, 3 * n + i + 1)
                act.wait_ge(c_ss, n)
                act.activation(squares[:, i, :], bank[i][:, :], ACT.Square).then_inc(c_sq, 1)

            def values(n, w):
                act.wait_ge(c_p, 3 * n + 3)
                act.activation(v_tok[:, w, :], bank[0][:, :], ACT.Copy).then_inc(c_v, 1)

            def keys(n, w):
                act.wait_ge(c_t, 2 * n + 1)
                act.activation(k_t[:, :, w * P:(w + 1) * P], bank[2][:, :].rearrange("p (c t) -> p c t", t=P),
                               ACT.Copy).then_inc(c_kt, 1)

            def q_even(n):
                act.wait_ge(c_t, 2 * n + 2)
                act.activation(q_heads[0:64, :, :].rearrange("p (c e) t -> p e c t", e=2)[:, 0, :, :],
                               bank[2][0:64, :].rearrange("p (c t) -> p c t", t=P), ACT.Copy).then_inc(c_qe, 1)

            def exps(n, w, i):
                u = 4 * n + i
                nk = 2 * P if w else P
                act.wait_ge(c_nb, u + 1)
                if w or i >= 2:
                    act.wait_ge(c_pt, u - 1)
                for e in range(2):
                    h = 2 * i + e
                    act.activation(probs[:, i % 2, e, 0:nk], scores[:, i % 2, e, 0:nk], ACT.Exp,
                                   bias=row_bias[:, w % 2, h:h + 1], scale=q_rnorm[:, w, h:h + 1],
                                   accum_out=row_sum[:, w % 2, h:h + 1]).then_inc(c_ex, 1)

            def probs_transposed(n, w, i):
                u = 4 * n + i
                act.wait_ge(c_pt, u + 1)
                if w or i >= 2:
                    act.wait_ge(c_pv, u - 1)
                if w:
                    act.activation(probs_t[:, i % 2, :, :], bank[4 + i % 2][:, :].rearrange("p (c t) -> p c t", t=P),
                                   ACT.Copy).then_inc(c_pt_out, 1)
                else:
                    act.activation(probs_t[:, i % 2, 0:4:2, :],
                                   bank[4 + i % 2][:, :].rearrange("p (c t) -> p c t", t=P)[:, 0:4:2, :],
                                   ACT.Copy).then_inc(c_pt_out, 1)

            def attention(n0, l, nxt):
                for w in range(TT):
                    n = n0 + w
                    two, one, three = (w < 2 or nxt), (w < 3 or nxt), (w < 1 or nxt)
                    exps(n, w, 0)
                    if two:
                        square(n + 2, 0)
                    exps(n, w, 1)
                    probs_transposed(n, w, 0)
                    if two:
                        square(n + 2, 1)
                    exps(n, w, 2)
                    probs_transposed(n, w, 1)
                    exps(n, w, 3)
                    probs_transposed(n, w, 2)
                    if two and w < TT - 1:
                        values(n + 2, (w + 2) % TT)
                    if three:
                        x_transposed(n + 3, (w + 3) % TT, bank[1][:, 0:D])
                    if one:
                        keys(n + 1, (w + 1) % TT)
                    probs_transposed(n, w, 3)
                    if one:
                        q_even(n + 1)
                    else:
                        mlp_input(l * NB, l)
                    if two and w == TT - 1:
                        values(n + 2, (w + 2) % TT)

            def mlp_input(m, l):
                for c in range(KD):
                    act.wait_ge(d_tp, 2 * m + c + 1)
                    act.activation(h_t[:, c, :], bank[c][:, :], ACT.Identity, bias=lcols[:, l, L_B + c:L_B + c + 1],
                                   scale=lcols[:, l, L_G + c:L_G + c + 1]).then_inc(d_tp_out, 1)
                for c in range(KD):
                    act.wait_ge(d_tp_out, 2 * m + c + 1)
                    act.activation(t_hi[:, c, :], h_t[:, c, :], ACT.Copy).then_inc(d_in_hi, 1)

            def round_qkv(l, i):
                act.wait_ge(wqkv_in, 16 * l + 16)
                for k in range(KD):
                    part = slice(i * INNER, (i + 1) * INNER)
                    act.activation(wqkv_hi[:, k, part], w_stage[:, :].rearrange("p (k n) -> p k n", k=KD)[:, k, part],
                                   ACT.Copy).then_inc(wq_hi, 1)

            def ahead(l, step):
                n0 = l * NT
                if step < 3:
                    round_qkv(l, step)
                    if step == 1:
                        for w in range(2):
                            x_transposed(n0 + w, w, bank[w][:, 0:D])
                elif step < 5:
                    square(n0, step - 3)
                elif step == 5:
                    values(n0, 0)
                    square(n0 + 1, 0)
                    square(n0 + 1, 1)
                    values(n0 + 1, 1)
                else:
                    keys(n0, 0)
                    q_even(n0)
                    x_transposed(n0 + 2, 2, bank[1][:, 0:D])

            def mlp(m, l, nxt):
                for j in range(KH):
                    r = P if j < KH - 1 else HLAST
                    act.wait_ge(d_w1, 2 * (KH * m + j) + 1)
                    if j >= 2:
                        act.wait_ge(d_act, KH * m + j - 1)
                    act.activation(hidden[0:r, j % 2, :], bank[2 + 2 * (j % 2)][0:r, :], ACT.Gelu,
                                   bias=lcols[0:r, l, L_B1G + j:L_B1G + j + 1]).then_inc(d_gelu, 1)
                    hi = hidden_hi[:, j, :] if j < KH - 1 else last_hi
                    act.wait_ge(d_full, KH * m + j + 1)
                    act.activation(hi[0:r, :], hidden[0:r, j % 2, :], ACT.Copy).then_inc(d_hi, 1)
                    if not nxt and l < LAYERS - 1 and j != 3:
                        ahead(l + 1, (0, 1, 2, None, 3, 4)[j])
                if nxt:
                    mlp_input(m + 1, l)
                elif l < LAYERS - 1:
                    ahead(l + 1, 5)

            act.wait_ge(b_ta, KD * NB)
            for step in range(6):
                ahead(0, step)
            act.wait_ge(c_zero, C_ZERO)
            for l in range(LAYERS):
                n0 = l * NT
                ahead(l, 6)
                with act.Fori(0, NB - 1) as b:
                    attention(n0 + b * TT, l, True)
                attention(n0 + (NB - 1) * TT, l, False)
                with act.Fori(0, NB - 1) as b:
                    mlp(l * NB + b, l, True)
                mlp(l * NB + NB - 1, l, False)

        @block.tensor
        def _(pe):
            def product(out, terms, first=True, last=True):
                for i, (stationary, moving) in enumerate(terms):
                    ins = pe.matmul(out, stationary, moving, start=(first and i == 0),
                                    stop=(last and i == len(terms) - 1))
                return ins

            def transpose_in(b):
                pe.wait_ge(n_norm, 4 * b + 4)
                for c in range(KD):
                    for t in range(TT):
                        ins = pe.transpose(bank[c][:, t * P:(t + 1) * P], normed[:, t, c * P:(c + 1) * P],
                                           ident[:, :])
                    ins.then_inc(a_tp, 1)

            def inputs(b):
                pe.wait_ge(a_tp_lo, 2 * b + 2)
                for j in range(2 * KR):
                    m = (j + KR) % (2 * KR)
                    if not (isinstance(b, int) and b == 0):
                        if j < 4:
                            if j % 2 == 0:
                                pe.wait_ge(a_thf, 3 * (b - 1) + (2 + j) // 2 + 1)
                            else:
                                pe.wait_ge(a_th, 3 * (b - 1) + (2 + j) // 2 + 1)
                    if j >= 4:
                        pe.wait_ge(a_tap0, 3 * b + j - 4 + 1)
                    if isinstance(b, int) and b == 0 and j % KR == 0:
                        pe.wait_ge(win_lo, KD * (j // KR + 1))
                    product(bank[2 + j % 4][:, :], [
                        (w[:, k, m * P:(m + 1) * P], x[:, k, :]) for k in range(KD)
                        for w, x in ((w_in_hi, t_hi), (w_in_hi, t_lo), (w_in_lo, t_hi))]).then_inc(a_full, 1)

            def gates(b, nxt):
                for j in range(KR):
                    for g in range(2):
                        u = 2 * j + g
                        if u == 0:
                            pe.wait_ge(a_tap0, 3 * b + 3)
                        elif u < 4:
                            pe.wait_ge(a_gelu, 3 * b + u)
                        elif u == 4:
                            pe.wait_ge(a_thf, 3 * b + 1)
                        else:
                            pe.wait_ge(a_th, 3 * b + 1)
                        m = g * KR + j
                        for k in range(KR):
                            if u == 0:
                                pe.wait_ge(a_conv_lo, 3 * b + k + 1)
                            ins = product(bank[2 + (u + 2) % 4][:, :], [
                                (w[:, k, m * P:(m + 1) * P], c[:, k, :])
                                for w, c in ((w_gate_hi, conv_hi), (w_gate_hi, conv_lo), (w_gate_lo, conv_hi))],
                                first=(k == 0), last=(k == KR - 1))
                        ins.then_inc(a_full, 1)
                    if j == 1 and nxt:
                        transpose_in(b + 1)

            def output(b):
                pe.wait_ge(a_gh, 3 * b + 3)
                pe.wait_ge(a_res, 2 * b)
                for t in range(TT):
                    for k in range(KR):
                        ins = pe.matmul(bank[6 + t // 2][:, (t % 2) * D:(t % 2 + 1) * D],
                                        scanned[:, k, t * P:(t + 1) * P], w_out_sb[:, k, :],
                                        start=(k == 0), stop=(k == KR - 1))
                    if t % 2:
                        ins.then_inc(a_o, 1)

            pe.wait_ge(ready_consts, 1)
            transpose_in(0)
            inputs(0)
            pe.wait_ge(wg_split, KR)
            pe.wait_ge(wor_in, 16)
            gates(0, True)
            inputs(1)
            with pe.Fori(1, NB - 1) as b:
                gates(b, True)
                inputs(b + 1)
                output(b - 1)
            gates(NB - 1, False)
            output(NB - 2)

            def bias_by_key(j):
                if j == 0:
                    pe.wait_ge(e_exp, TT)
                    pe.wait_ge(a_res, 2 * (NB - 1))
                elif j >= 2:
                    pe.wait_ge(e_tp_out, j - 1)
                for t in range(TT):
                    ins = pe.transpose(bank[6 + j % 2][:, t * P:(t + 1) * P], ew[:, t, j * P:(j + 1) * P], ident[:, :])
                ins.then_inc(e_tp, 1)

            def transpose_emb(b):
                pe.wait_ge(b_emb, b + 1)
                for c in range(KD):
                    for t in range(TT):
                        ins = pe.transpose(bank[c][:, t * P:(t + 1) * P], normed[:, t, c * P:(c + 1) * P],
                                           ident[:, :])
                    ins.then_inc(b_tp, 1)

            def project(b, mixed=None):
                pe.wait_ge(b_tp_lo, 2 * b + 2)
                if isinstance(b, int) and b == 0:
                    pe.wait_ge(a_th, 3 * NB)
                    pe.wait_ge(a_thf, 3 * NB)
                for i in range(3 * KD):
                    if isinstance(b, int) and b == 0 and i == 2 * KD:
                        bias_by_key(2)
                        bias_by_key(3)
                    if mixed is not None and i == 3 * KD - 1:
                        transpose_a(mixed)
                    which, m = (1, 2, 0)[i // KD], i % KD
                    product(bank[2 + i if i < 2 * KD else m][:, :], [
                        (w[:, which, k, m * P:(m + 1) * P], x[:, k, :]) for k in range(KD)
                        for w, x in ((w_qkv_hi, t_hi), (w_qkv_hi, t_lo), (w_qkv_lo, t_hi))]).then_inc(b_full, 1)

            def keys_by_token(b):
                for i in range(4):
                    src, h = (ek, ekv)[i // 2], i % 2
                    if i == 0:
                        pe.wait_ge(b_ekv, 2 * b + 2)
                        pe.wait_ge(b_eq, 2 * b + 2)
                    if not (isinstance(b, int) and b == 0):
                        pe.wait_ge(b_relu, KF * (b - 1) + 5 + i)
                    for t in range(2):
                        for m in range(KD):
                            ins = pe.transpose(bank[2 + (2 + i) % 4][:, (2 * t + m) * P:(2 * t + m + 1) * P],
                                               src[:, m, (2 * h + t) * P:(2 * h + t + 1) * P], ident[:, :])
                    ins.then_inc(b_tk, 1)

            def mix_tokens(b):
                for m in range(KD):
                    for i, src in enumerate((ek_tok, ekv_tok)):
                        if m == 0:
                            pe.wait_ge(b_tk_out, 4 * b + 2 * i + 2)
                        for j in range(TT):
                            ins = pe.matmul(bank[2 + (2 * m + i + 2) % 4][:, :], src[:, j, m * P:(m + 1) * P],
                                            ew_t[:, j, :], start=(j == 0), stop=(j == TT - 1))
                        ins.then_inc(b_aft, 1)

            def project_mixed(b, to=6):
                pe.wait_ge(b_y, 2 * b + 2)
                for t in range(TT):
                    if t % 2 == 0 and to == 6 and not (isinstance(b, int) and b == 0):
                        pe.wait_ge(b_sum, 2 * b - 1 + t // 2)
                    for k in range(KD):
                        ins = pe.matmul(bank[to + t // 2][:, (t % 2) * D:(t % 2 + 1) * D],
                                        y[:, k, t * P:(t + 1) * P], w_o[:, k, :], start=(k == 0),
                                        stop=(k == KD - 1))
                    if t % 2:
                        ins.then_inc(b_o, 1)

            def transpose_a(b, last=False):
                pe.wait_ge(a_out, TT * b + TT)
                for c in range(KD):
                    if not last:
                        pe.wait_ge(b_ek, 2 * (b + 1) + c + 1)
                    for t in range(TT):
                        ins = pe.transpose(bank[2 + c][:, t * P:(t + 1) * P], a_tok[:, t, c * P:(c + 1) * P],
                                           ident[:, :])
                    ins.then_inc(b_ta, 1)

            def mlp_up_x(b, nxt):
                pe.wait_ge(b_ta_lo, 2 * b + 2)
                for c in range(KF):
                    if c >= 4:
                        pe.wait_ge(b_relu, KF * b + c - 3)
                    elif nxt and c < 2:
                        pe.wait_ge(b_ekv, 2 * (b + 1) + c + 1)
                    product(bank[2 + (2 + c) % 4][:, :], [
                        (w[:, k, c * P:(c + 1) * P], a[:, k, :]) for k in range(KD)
                        for w, a in ((w_1_hi, a_hi), (w_1_hi, a_lo), (w_1_lo, a_hi))]).then_inc(b_f1, 1)

            def mlp_down_x(b, t):
                if t == 0:
                    pe.wait_ge(b_mix, 2 * b + 2)
                for k in range(KF):
                    if t == 0:
                        pe.wait_ge(b_relu, KF * b + k + 1)
                    ins = pe.matmul(bank[6 + t // 2][:, (t % 2) * D:(t % 2 + 1) * D],
                                    ff[:, k, t * P:(t + 1) * P], w_2[:, k, :], start=(k == 0), stop=(k == KF - 1))
                if t % 2:
                    ins.then_inc(b_f2, 1)

            bias_by_key(0)
            bias_by_key(1)
            transpose_emb(0)
            pe.wait_ge(wx_lo, 3)
            project(0)
            pe.wait_ge(aft_in, 16)
            pe.wait_ge(e_tp_out, TT)
            output(NB - 1)
            pe.wait_ge(a_res, 2 * NB)
            keys_by_token(0)
            mix_tokens(0)
            transpose_emb(1)
            project_mixed(0)
            pe.wait_ge(mlp_in, 16)
            pe.wait_ge(wx_lo, 7)

            def mixing(b, norm2):
                project(b + 1, b)
                mlp_up_x(b, True)
                keys_by_token(b + 1)
                mix_tokens(b + 1)
                if norm2:
                    for t in range(TT):
                        mlp_down_x(b, t)
                    transpose_emb(b + 2)
                    project_mixed(b + 1)
                else:
                    mlp_down_x(b, 0)
                    project_mixed(b + 1, 0)
                    for t in range(1, TT - 1):
                        mlp_down_x(b, t)
                    transpose_a(b + 1, True)
                    mlp_down_x(b, TT - 1)

            with pe.Fori(0, NB - 2) as b:
                mixing(b, True)
            mixing(NB - 2, False)

            def transpose_x(n, par, dst, free):
                for sem, v in free:
                    pe.wait_ge(sem, v)
                pe.wait_ge(c_xs, n + 1)
                for c in range(KD):
                    ins = pe.transpose(dst[:, c * P:(c + 1) * P], x_tile[:, par, c * P:(c + 1) * P], ident[:, :])
                ins.then_inc(c_xt, 1)

            def qkv(n, w, i):
                if i == 0:
                    pe.wait_ge(c_xt_lo, n + 1)
                    pe.wait_ge(c_v, n)
                elif i == 1:
                    pe.wait_ge(c_rope, 6 * n)
                else:
                    pe.wait_ge(c_rope, 6 * n + 3)
                product(bank[i % 2][:, :], [
                    (x[:, k * T + w * P:k * T + (w + 1) * P], m[:, k, i * INNER:(i + 1) * INNER])
                    for k in range(KD)
                    for x, m in ((x_hi, wqkv_hi), (x_hi, wqkv_lo), (x_lo, wqkv_hi))]).then_inc(c_p, 1)

            def transpose_k(n, par, free):
                for sem, v in free:
                    pe.wait_ge(sem, v)
                pe.wait_ge(c_kn, n + 1)
                for c in range(KI):
                    ins = pe.transpose(bank[2][:, c * P:(c + 1) * P], k_tok[:, par, c * P:(c + 1) * P], ident[:, :])
                ins.then_inc(c_t, 1)

            def transpose_q(n, par):
                pe.wait_ge(c_kt, n + 1)
                for c in range(KI):
                    ins = pe.transpose(bank[2][:, c * P:(c + 1) * P], q_tok[:, par, c * P:(c + 1) * P], ident[:, :])
                ins.then_inc(c_t, 1)

            def score(n, w, i):
                u = 4 * n + i
                if i == 0:
                    pe.wait_ge(c_qe, n + 1)
                    pe.wait_ge(c_qo, n + 1)
                if not (isinstance(u, int) and u < 2):
                    pe.wait_ge(c_tt, 2 * u - 2)
                k0 = max(w - 1, 0) * P
                for e in range(2):
                    nk = (w + 1) * P - k0
                    ins = pe.matmul(bank[6 + i % 2][:, e * 2 * P:e * 2 * P + nk], q_heads[:, 2 * i + e, :],
                                    k_t[:, i, k0:(w + 1) * P], start=True, stop=True)
                ins.then_inc(c_qk, 1)

            def transpose_probs(n, w, i):
                u = 4 * n + i
                pe.wait_ge(c_ex, 2 * u + 2)
                if w or i >= 2:
                    pe.wait_ge(c_pt_out, u - 1)
                for e in range(2):
                    for k in range(2 if w else 1):
                        ins = pe.transpose(bank[4 + i % 2][:, (2 * e + k) * P:(2 * e + k + 1) * P],
                                           probs[:, i % 2, e, k * P:(k + 1) * P], ident[:, :])
                ins.then_inc(c_pt, 1)

            def weigh_values(n, w, i):
                u = 4 * n + i
                pe.wait_ge(c_pt_out, u + 1)
                if i == 0:
                    pe.wait_ge(c_v, n + 1)
                    pe.wait_ge(c_on, n)
                nk = 2 if w else 1
                for e in range(2):
                    h = 2 * i + e
                    for k in range(nk):
                        ins = pe.matmul(bank[3][:, h * DH:(h + 1) * DH], probs_t[:, i % 2, 2 * e + k, :],
                                        v_tok[:, w - nk + 1 + k, h * DH:(h + 1) * DH], start=(k == 0),
                                        stop=(k == nk - 1))
                ins.then_inc(c_pv, 1)

            def transpose_o(n, free):
                for sem, v in free:
                    pe.wait_ge(sem, v)
                pe.wait_ge(c_on, n + 1)
                for c in range(KI):
                    ins = pe.transpose(bank[2][:, c * P:(c + 1) * P], o_tok[:, c * P:(c + 1) * P], ident[:, :])
                ins.then_inc(c_ot, 1)

            def project_o(n):
                pe.wait_ge(c_ot_out, n + 1)
                for k in range(KI):
                    ins = pe.matmul(bank[2][:, 0:D], o_t[:, k, :], wo_sb[:, k, :], start=(k == 0), stop=(k == KI - 1))
                ins.then_inc(c_wo, 1)

            def attention(n0, l, nxt):
                free = []
                for w in range(TT):
                    n = n0 + w
                    two, one, three = (w < 2 or nxt), (w < 3 or nxt), (w < 1 or nxt)
                    if two:
                        qkv(n + 2, (w + 2) % TT, 0)
                    transpose_probs(n, w, 0)
                    score(n, w, 2)
                    if two:
                        qkv(n + 2, (w + 2) % TT, 1)
                    weigh_values(n, w, 0)
                    transpose_probs(n, w, 1)
                    if w:
                        project_o(n - 1)
                        free = [(c_res, n)]
                    score(n, w, 3)
                    weigh_values(n, w, 1)
                    transpose_probs(n, w, 2)
                    if two and w < TT - 1:
                        qkv(n + 2, (w + 2) % TT, 2)
                    if three:
                        transpose_x(n + 3, (w + 3) % 2, bank[1][:, 0:D], [(c_rope, 6 * (n + 2) + 6)])
                    if one:
                        transpose_k(n + 1, (w + 1) % 2, free)
                    weigh_values(n, w, 2)
                    transpose_probs(n, w, 3)
                    if one:
                        transpose_q(n + 1, (w + 1) % 2)
                        free = [(c_qe, n + 2), (c_qo, n + 2)]
                    else:
                        transpose_mlp(l * NB)
                    weigh_values(n, w, 3)
                    if one:
                        score(n + 1, (w + 1) % TT, 0)
                        score(n + 1, (w + 1) % TT, 1)
                    transpose_o(n, free)
                    if w == TT - 1:
                        if two:
                            qkv(n + 2, (w + 2) % TT, 2)
                        project_o(n)
                        free = [(c_res, n + 1)]

            def transpose_mlp(m):
                pe.wait_ge(d_norm, 8 * m + 8)
                for c in range(KD):
                    for t in range(TT):
                        ins = pe.transpose(bank[c][:, t * P:(t + 1) * P], normed[:, t, c * P:(c + 1) * P],
                                           ident[:, :])
                    ins.then_inc(d_tp, 1)

            w1_hi, w1_lo = (w[:, 0:W1_COLS].rearrange("p (k n) -> p k n", k=KD) for w in (wm_hi, wm_lo))
            w2_hi, w2_lo = (w[:, W1_COLS:W1_COLS + W2_COLS].rearrange("p (k n) -> p k n", k=KH)
                            for w in (wm_hi, wm_lo))

            def mlp_up(m, j):
                if j == 0:
                    pe.wait_ge(d_in_lo, 2 * m + 2)
                r = P if j < KH - 1 else HLAST
                for g, c0 in enumerate((HID, 0)):
                    if j >= 2:
                        pe.wait_ge((d_gelu, d_full)[g], KH * m + j - 1)
                    product(bank[2 + 2 * (j % 2) + g][0:r, :], [
                        (w[:, k, c0 + j * P:c0 + j * P + r], h[:, k, :]) for k in range(KD)
                        for w, h in ((w1_hi, t_hi), (w1_hi, t_lo), (w1_lo, t_hi))]).then_inc(d_w1, 1)

            def mlp_down(m, t):
                if t % 2 == 0:
                    pe.wait_ge((d_res0, b_res)[t // 2], m if t == 0 else m + NB)
                for k in range(KH):
                    if t == 0:
                        pe.wait_ge(d_act, KH * m + k + 1)
                    r = P if k < KH - 1 else HLAST + 1
                    hi, lo = (hidden_hi[:, k, :], hidden_lo[:, k, :]) if k < KH - 1 else (last_hi, last_lo)
                    for h, w in ((hi, w2_hi), (hi, w2_lo), (lo, w2_hi)):
                        ins = pe.matmul(bank[6 + t // 2][:, (t % 2) * D:(t % 2 + 1) * D],
                                        h[0:r, t * P:(t + 1) * P], w[0:r, k, :], start=(k == 0 and w is w2_hi and h is hi),
                                        stop=(k == KH - 1 and h is lo))
                ins.then_inc(d_w2, 1)

            def ahead(l, step):
                n0 = l * NT
                if step == 0:
                    for w in range(2):
                        transpose_x(n0 + w, w, bank[w][:, 0:D], [])
                elif step <= 6:
                    w, i = divmod(step - 1, 3)
                    if step == 1:
                        pe.wait_ge(c_xt_lo, n0 + 2)
                    if w == 0:
                        pe.wait_ge(wq_lo, 6 * l + 2 * i + 2)
                    qkv(n0 + w, w, i)
                else:
                    transpose_k(n0, 0, [])
                    transpose_q(n0, 0)
                    transpose_x(n0 + 2, 0, bank[1][:, 0:D], [(c_rope, 6 * (n0 + 1) + 6)])

            def mlp(m, l, nxt):
                also = not nxt and l < LAYERS - 1
                for j in range(KH):
                    mlp_up(m, j)
                    if also and j in (1, 4, 5):
                        ahead(l + 1, (1, 4, 5).index(j))
                for t in range(TT):
                    mlp_down(m, t)
                    if nxt and t == 1:
                        transpose_mlp(m + 1)
                    if also:
                        ahead(l + 1, 3 + t)

            mlp_up_x(NB - 1, False)
            mlp_down_x(NB - 1, 0)
            ahead(0, 0)
            mlp_down_x(NB - 1, 1)
            ahead(0, 1)
            mlp_down_x(NB - 1, 2)
            ahead(0, 2)
            mlp_down_x(NB - 1, 3)
            for step in range(3, 7):
                ahead(0, step)
            for l in range(LAYERS):
                n0 = l * NT
                ahead(l, 7)
                pe.wait_ge(wo_in, 16 * l + 16)
                if l == 0:
                    pe.wait_ge(b_sum, 2 * NB)
                else:
                    pe.wait_ge(b_res, NB * (l + 1))
                score(n0, 0, 0)
                score(n0, 0, 1)
                with pe.Fori(0, NB - 1) as b:
                    attention(n0 + b * TT, l, True)
                attention(n0 + (NB - 1) * TT, l, False)
                pe.wait_ge(wm_split, WM_PIECES * NB * (l + 1))
                pe.wait_ge(c_res, NT * (l + 1))
                with pe.Fori(0, NB - 1) as b:
                    mlp(l * NB + b, l, True)
                mlp(l * NB + NB - 1, l, False)


def _chunks(w):
    k, n = w.shape
    return w.reshape(k // P, P, n).transpose(1, 0, 2)


def _columns(v):
    return v.reshape(-1, P).T


def kernel(**inputs):
    import numpy as np
    import concourse.bacc as _bacc
    from concourse.bass_utils import run_bass_kernel_spmd as _run

    a = {k: np.asarray(v) for k, v in inputs.items()}
    f32 = np.float32
    cols = np.concatenate([
        _chunks(a["L0_attn_conv_w"].reshape(RH, TAPS)).reshape(P, KR * TAPS),
        _columns(a["L0_attn_conv_b"]), _columns(a["L0_attn_b_g"]), _columns(a["L0_attn_forget_base"]),
        _columns(a["L0_xattn_bq"]), _columns(a["L0_xattn_bk"]), _columns(a["L0_xattn_bv"]),
        _columns(a["L0_xattn_b1"])], axis=1)
    rows = np.broadcast_to(np.stack([a["L0_xattn_bo"], a["L0_xattn_gamma"], a["L0_xattn_beta"],
                                     a["L0_xattn_b2"]]), (P, 4, D))

    def hid_columns(v):
        full = np.zeros((KH * P,), f32)
        full[:HID] = v
        return _columns(full)

    lcols = np.stack([np.concatenate([
        _columns(a["L0_ffn_ln_g"][l]), _columns(a["L0_ffn_ln_b"][l]),
        hid_columns(a["L0_ffn_b1"][l][:HID]), hid_columns(a["L0_ffn_b1"][l][HID:])], axis=1)
        for l in range(LAYERS)], axis=1)
    qk_scale = np.broadcast_to(np.stack([a["L0_ffn_q_scale"], a["L0_ffn_k_scale"]], axis=1), (P, LAYERS, 2, DH))
    half = np.arange(0, DH, 2, dtype=f32)
    pos = np.arange(T, dtype=f32)
    inv_freq = (f32(1.0) / f32(10000.0) ** (half / f32(DH))).astype(f32)
    freqs = pos[:, None] * inv_freq[None, :]
    freqs = np.concatenate([freqs, freqs], axis=-1)
    base = (half + f32(0.4 * DH)) / f32(1.4 * DH)
    power = (pos - f32(T // 2)) / f32(P // 2)
    scale = (base[None, :] ** power[:, None]).astype(f32)
    scale = np.concatenate([scale, scale], axis=-1)
    sign = np.concatenate([-np.ones(DH // 2, f32), np.ones(DH // 2, f32)])
    cos, sin = np.cos(freqs), np.sin(freqs) * sign
    rope = np.stack([cos * scale, sin * scale, cos / scale, sin / scale]).astype(f32)
    rope = rope.reshape(4, TT, P, DH).transpose(2, 0, 1, 3)
    w2 = np.zeros((LAYERS, KH * P, D), f32)
    w2[:, :HID] = a["L0_ffn_w2"]
    w2[:, HID] = a["L0_ffn_b2"]
    layer = lambda w: np.stack([_chunks(w[l]) for l in range(LAYERS)])
    wm = np.concatenate([layer(a["L0_ffn_w1"]).reshape(LAYERS, P, -1), layer(w2).reshape(LAYERS, P, -1)], axis=2)
    wm = np.pad(wm, ((0, 0), (0, 0), (0, WM_COLS - wm.shape[2])))
    named = {
        "x": a["x"], "ctx": a["ctx_1024"], "cols": cols, "rows": rows,
        "w_in": _chunks(a["L0_attn_W_in"].T), "w_gate": _chunks(a["L0_attn_W_g"].T),
        "w_out": _chunks(a["L0_attn_W_out"].T),
        "wq": _chunks(a["L0_xattn_wq"]), "wk": _chunks(a["L0_xattn_wk"]), "wv": _chunks(a["L0_xattn_wv"]),
        "wo_x": _chunks(a["L0_xattn_wo"]), "pos_bias": _chunks(a["L0_xattn_pos_bias"]),
        "w1_x": _chunks(a["L0_xattn_w1"]), "w2_x": _chunks(a["L0_xattn_w2"]),
        "lcols": lcols, "qk_scale": qk_scale, "rope": rope,
        "wqkv": layer(a["L0_ffn_wqkv"]), "wo_l": layer(a["L0_ffn_wo"]), "wm_l": wm}
    nc = _bacc.Bacc("TRN2", target_bir_lowering=False, num_devices=1)
    arrays, args = {}, []
    for name, v in named.items():
        v = np.ascontiguousarray(v)
        arrays[f"in_{name}_dram"] = v
        args.append(nc.dram_tensor(f"in_{name}_dram", v.shape, mybir.dt.from_np(v.dtype), kind="ExternalInput").ap())
    args.append(nc.dram_tensor("out_0_dram", (NB, T, D), F32, kind="ExternalOutput").ap())
    build(nc, *args)
    r = _run(nc, [arrays], core_ids=[0])
    return r.results[0]["out_0_dram"]
```
